# Optimizing a Trainium2 kernel written in Bass

```python
import numpy as np
import jax
import jax.numpy as jnp

def _softmax(x, axis=-1):
    return jax.nn.softmax(x, axis=axis)

def _gelu(x):
    return jax.nn.gelu(x, approximate=True)

def _silu(x):
    return jax.nn.silu(x)

def _sigmoid(x):
    return jax.nn.sigmoid(x)

def _layernorm(x, axis=-1, eps=1e-05):
    m = jnp.mean(x, axis=axis, keepdims=True)
    v = jnp.var(x, axis=axis, keepdims=True)
    return (x - m) / jnp.sqrt(v + eps)

def _scatter_add(tgt, idx, src, axis=0):
    return tgt.at[idx].add(src)

def _segment_sum(src, seg, n):
    return jax.ops.segment_sum(src, seg, n)
kernel_name = 'mk_xattn_ffn_d4_seqx_r8_c27f85'

def setup_inputs(seed: int=0):
    np.random.seed(seed)
    _w = jnp.asarray

    def _rec_inputs():
        import jax
        import jax.numpy as jnp
        _rk = jax.random.key(seed)
        x = -0.000125 + 0.9999 * jax.random.normal(jax.random.fold_in(_rk, 1), (4, 512, 128), jnp.float32)
        _lenS = 512 - jax.random.randint(jax.random.fold_in(_rk, 7), (4,), 0, max(1, 512 // 4) + 1, jnp.int32)
        _lenS2 = 77 - jax.random.randint(jax.random.fold_in(_rk, 8), (4,), 0, max(1, 77 // 4) + 1, jnp.int32)
        _ctx_768P = jax.random.normal(jax.random.fold_in(_rk, 11), (4, 16, 96), jnp.float32)
        _ctx_768c = jax.random.dirichlet(jax.random.fold_in(_rk, 511), 0.3 * jnp.ones((16,), jnp.float32), (4, 77))
        _ctx_768t = jnp.einsum('bsk,bkd->bsd', _ctx_768c, _ctx_768P)
        _ctx_768t = _ctx_768t * jax.lax.rsqrt(jnp.mean(jnp.square(_ctx_768t)) + 1e-12) * 0.953939
        ctx_768 = 0.00272024 + 0.999456 * (_ctx_768t + 0.3 * jax.random.normal(jax.random.fold_in(_rk, 611), (4, 77, 96), jnp.float32))
        _validS = jnp.arange(512)[None, :] < _lenS[:, None]
        _validS2 = jnp.arange(77)[None, :] < _lenS2[:, None]
        _causal = jnp.tril(jnp.ones((512, 512), dtype=bool))
        mask_BxS2_bf1 = jnp.ones((4, 77), dtype=bool)
        return (x, ctx_768, mask_BxS2_bf1)
    x, ctx_768, mask_BxS2_bf1 = _rec_inputs()

    def _L0_xattn_setup():
        import jax, jax.numpy as jnp
        import numpy as np
        HEADS = 16
        DIM_HEAD = 64
        SCALE = DIM_HEAD ** (-0.5)
        QUERY_DIM = 128
        CONTEXT_DIM = 96
        INNER_DIM = HEADS * DIM_HEAD
        key = jax.random.key(seed)
        ks = jax.random.split(key, 7)
        B, Nq, Nk = (8, 512, 77)
        x = jax.random.normal(ks[0], (B, Nq, QUERY_DIM), dtype=jnp.float32)
        context = jax.random.normal(ks[1], (B, Nk, CONTEXT_DIM), dtype=jnp.float32)
        Wq = jax.random.normal(ks[2], (QUERY_DIM, INNER_DIM), dtype=jnp.float32) * QUERY_DIM ** (-0.5)
        Wk = jax.random.normal(ks[3], (CONTEXT_DIM, INNER_DIM), dtype=jnp.float32) * CONTEXT_DIM ** (-0.5)
        Wv = jax.random.normal(ks[4], (CONTEXT_DIM, INNER_DIM), dtype=jnp.float32) * CONTEXT_DIM ** (-0.5)
        Wo = jax.random.normal(ks[5], (INNER_DIM, QUERY_DIM), dtype=jnp.float32) * INNER_DIM ** (-0.5)
        bo = jnp.zeros((QUERY_DIM,), dtype=jnp.float32)
        return {'x': x, 'context': context, 'Wq': Wq, 'Wk': Wk, 'Wv': Wv, 'Wo': Wo, 'bo': bo}
    _L0_xattn_all = _L0_xattn_setup()
    _L0_xattn_in = {k: v for k, v in _L0_xattn_all.items() if k in ('Wq', 'Wk', 'Wv', 'Wo', 'bo')}
    del _L0_xattn_all

    def _L0_ffn_setup():
        import jax, jax.numpy as jnp
        import numpy as np
        NUM_EXPERTS = 8
        TOP_K = 2
        ROUTE_SCALE = 1.0
        DIM = 128
        HID = 128
        B, S = (2, 512)
        key = jax.random.key(seed)
        ks = jax.random.split(key, 9)
        sc = 0.05
        return {'x': jax.random.normal(ks[0], (B, S, DIM), dtype=jnp.float32), 'gate_w': jax.random.normal(ks[1], (NUM_EXPERTS, DIM), dtype=jnp.float32) * sc, 'w1': jax.random.normal(ks[2], (NUM_EXPERTS, HID, DIM), dtype=jnp.float32) * sc, 'w2': jax.random.normal(ks[3], (NUM_EXPERTS, DIM, HID), dtype=jnp.float32) * sc, 'w3': jax.random.normal(ks[4], (NUM_EXPERTS, HID, DIM), dtype=jnp.float32) * sc, 'sw1': jax.random.normal(ks[5], (HID, DIM), dtype=jnp.float32) * sc, 'sw2': jax.random.normal(ks[6], (DIM, HID), dtype=jnp.float32) * sc, 'sw3': jax.random.normal(ks[7], (HID, DIM), dtype=jnp.float32) * sc, 'expert_bias': jnp.zeros((NUM_EXPERTS,), dtype=jnp.float32)}
    _L0_ffn_all = _L0_ffn_setup()
    _L0_ffn_in = {k: v for k, v in _L0_ffn_all.items() if k in ('gate_w', 'w1', 'w2', 'w3', 'sw1', 'sw2', 'sw3', 'expert_bias')}
    del _L0_ffn_all

    def _L1_xattn_setup():
        import jax, jax.numpy as jnp
        import numpy as np
        NUM_HEADS = 8
        DIM_HEAD = 128
        SCALE = DIM_HEAD ** (-0.25)
        key = jax.random.key(seed)
        ks = jax.random.split(key, 7)
        B, Tq, Dq = (8, 512, 128)
        Tk, Dc = (128, 96)
        inner = NUM_HEADS * DIM_HEAD
        s = lambda d: 1.0 / np.sqrt(d)
        return {'x': jax.random.normal(ks[0], (B, Tq, Dq), jnp.float32), 'context': jax.random.normal(ks[1], (B, Tk, Dc), jnp.float32), 'Wq': jax.random.normal(ks[2], (Dq, inner), jnp.float32) * s(Dq), 'Wk': jax.random.normal(ks[3], (Dc, inner), jnp.float32) * s(Dc), 'Wv': jax.random.normal(ks[4], (Dc, inner), jnp.float32) * s(Dc), 'Wo': jax.random.normal(ks[5], (inner, Dq), jnp.float32) * s(inner), 'bo': jnp.zeros((Dq,), jnp.float32)}
    _L1_xattn_all = _L1_xattn_setup()
    _L1_xattn_in = {k: v for k, v in _L1_xattn_all.items() if k in ('Wq', 'Wk', 'Wv', 'Wo', 'bo')}
    del _L1_xattn_all

    def _L1_ffn_setup():
        import jax, jax.numpy as jnp
        import numpy as np
        TOP_K = 2
        CAPACITY = 512
        EPS = 1e-06
        W_SCALE = 0.02

        def _rms(x, w):
            return x * jax.lax.rsqrt(jnp.mean(x * x, axis=-1, keepdims=True) + EPS) * w
        key = jax.random.key(seed)
        ks = jax.random.split(key, 8)
        B, S, H, F, E = (8, 512, 128, 256, 8)
        F4 = F // 4
        return {'hidden_states': jax.random.normal(ks[0], (B, S, H), jnp.float32), 'Wr': jax.random.normal(ks[1], (H, E), jnp.float32) * W_SCALE, 'norm_w': jnp.ones((E, H), jnp.float32), 'Wg': jax.random.normal(ks[2], (E, H, F), jnp.float32) * W_SCALE, 'Wu': jax.random.normal(ks[3], (E, H, F), jnp.float32) * W_SCALE, 'Wd': jax.random.normal(ks[4], (E, F, H), jnp.float32) * W_SCALE, 'f_norm': jnp.ones((H,), jnp.float32), 'fWg': jax.random.normal(ks[5], (H, F4), jnp.float32) * W_SCALE, 'fWu': jax.random.normal(ks[6], (H, F4), jnp.float32) * W_SCALE, 'fWd': jax.random.normal(ks[7], (F4, H), jnp.float32) * W_SCALE}
    _L1_ffn_all = _L1_ffn_setup()
    _L1_ffn_in = {k: v for k, v in _L1_ffn_all.items() if k in ('Wr', 'norm_w', 'Wg', 'Wu', 'Wd', 'f_norm', 'fWg', 'fWu', 'fWd')}
    del _L1_ffn_all

    def _L2_xattn_setup():
        import jax, jax.numpy as jnp
        import numpy as np
        import math
        B, N, M = (4, 128, 128)
        DIM, CTX_DIM = (128, 96)
        HEADS, DIM_HEAD = (16, 64)
        INNER = HEADS * DIM_HEAD

        def layer_norm(t, g, eps=1e-05):
            mean = jnp.mean(t, axis=-1, keepdims=True)
            var = jnp.mean((t - mean) ** 2, axis=-1, keepdims=True)
            return (t - mean) * jax.lax.rsqrt(var + eps) * g
        key = jax.random.key(seed)
        ks = jax.random.split(key, 8)
        return {'x': jax.random.normal(ks[0], (B, N, DIM), jnp.float32), 'context': jax.random.normal(ks[1], (B, M, CTX_DIM), jnp.float32), 'mask': jnp.ones((B, M), dtype=bool), 'g_norm': jnp.ones((DIM,), jnp.float32), 'null_kv': jax.random.normal(ks[2], (2, DIM_HEAD), jnp.float32), 'Wq': jax.random.normal(ks[3], (DIM, INNER), jnp.float32) * DIM ** (-0.5), 'Wkv': jax.random.normal(ks[4], (CTX_DIM, 2 * INNER), jnp.float32) * CTX_DIM ** (-0.5), 'Wout': jax.random.normal(ks[5], (INNER, DIM), jnp.float32) * INNER ** (-0.5), 'g_out': jnp.ones((DIM,), jnp.float32)}
    _L2_xattn_all = _L2_xattn_setup()
    _L2_xattn_in = {k: v for k, v in _L2_xattn_all.items() if k in ('g_norm', 'null_kv', 'Wq', 'Wkv', 'Wout', 'g_out')}
    del _L2_xattn_all

    def _L2_ffn_setup():
        import jax, jax.numpy as jnp
        import numpy as np
        H = 128
        I = 64
        E = 8
        K = 2
        SI = I * 2
        B, S = (2, 128)

        def _mlp(x, gw, uw, dw):
            return jax.nn.silu(x @ gw.T) * (x @ uw.T) @ dw.T
        key = jax.random.key(seed)
        ks = jax.random.split(key, 9)
        s = 0.02
        return {'x': jax.random.normal(ks[0], (B, S, H), jnp.float32), 'gate_w': jax.random.normal(ks[1], (E, H), jnp.float32) * s, 'lb_bias': jnp.zeros((E,), jnp.float32), 'expert_gate_w': jax.random.normal(ks[2], (E, I, H), jnp.float32) * s, 'expert_up_w': jax.random.normal(ks[3], (E, I, H), jnp.float32) * s, 'expert_down_w': jax.random.normal(ks[4], (E, H, I), jnp.float32) * s, 'shared_gate_w': jax.random.normal(ks[5], (SI, H), jnp.float32) * s, 'shared_up_w': jax.random.normal(ks[6], (SI, H), jnp.float32) * s, 'shared_down_w': jax.random.normal(ks[7], (H, SI), jnp.float32) * s}
    _L2_ffn_all = _L2_ffn_setup()
    _L2_ffn_in = {k: v for k, v in _L2_ffn_all.items() if k in ('gate_w', 'lb_bias', 'expert_gate_w', 'expert_up_w', 'expert_down_w', 'shared_gate_w', 'shared_up_w', 'shared_down_w')}
    del _L2_ffn_all

    def _L3_xattn_setup():
        import jax, jax.numpy as jnp
        import numpy as np
        N_HEADS = 16
        EMBED_DIM = 128
        CROSS_DIM = 96
        HEAD_DIM = EMBED_DIM // N_HEADS
        key = jax.random.key(seed)
        ks = jax.random.split(key, 12)
        B, SQ, SKV = (2, 256, 256)
        s_in = 1.0 / np.sqrt(EMBED_DIM)
        s_cross = 1.0 / np.sqrt(CROSS_DIM)
        return {'x': jax.random.normal(ks[0], (B, SQ, EMBED_DIM), jnp.float32), 'y': jax.random.normal(ks[1], (B, SKV, CROSS_DIM), jnp.float32), 'wq': jax.random.normal(ks[2], (EMBED_DIM, EMBED_DIM), jnp.float32) * s_in, 'bq': jax.random.normal(ks[3], (EMBED_DIM,), jnp.float32) * s_in, 'wk': jax.random.normal(ks[4], (EMBED_DIM, CROSS_DIM), jnp.float32) * s_cross, 'bk': jax.random.normal(ks[5], (EMBED_DIM,), jnp.float32) * s_cross, 'wv': jax.random.normal(ks[6], (EMBED_DIM, CROSS_DIM), jnp.float32) * s_cross, 'bv': jax.random.normal(ks[7], (EMBED_DIM,), jnp.float32) * s_cross, 'wo': jax.random.normal(ks[8], (EMBED_DIM, EMBED_DIM), jnp.float32) * s_in, 'bo': jax.random.normal(ks[9], (EMBED_DIM,), jnp.float32) * s_in}
    _L3_xattn_all = _L3_xattn_setup()
    _L3_xattn_in = {k: v for k, v in _L3_xattn_all.items() if k in ('wq', 'bq', 'wk', 'bk', 'wv', 'bv', 'wo', 'bo')}
    del _L3_xattn_all

    def _L3_ffn_setup():
        import math
        import jax, jax.numpy as jnp
        import numpy as np
        D_MODEL = 128
        D_FF = 512
        E = 8
        K = 2
        CAP_FACTOR = 1.25
        CLAMP = 10000.0
        LN_EPS = 1e-05
        B, S = (2, 256)
        key = jax.random.key(seed)
        ks = jax.random.split(key, 6)
        b12 = math.sqrt(6.0 / (D_MODEL + 2 * D_FF))
        b3 = math.sqrt(6.0 / (D_FF + D_MODEL))
        br = 0.02 * math.sqrt(3.0)
        return {'x': jax.random.normal(ks[0], (B, S, D_MODEL), dtype=jnp.float32), 'ln_gamma': jnp.ones((D_MODEL,), jnp.float32), 'ln_beta': jnp.zeros((D_MODEL,), jnp.float32), 'router_w': jax.random.uniform(ks[1], (E, D_MODEL), jnp.float32, -br, br), 'w12': jax.random.uniform(ks[2], (E, 2 * D_FF, D_MODEL), jnp.float32, -b12, b12), 'w3': jax.random.uniform(ks[3], (E, D_MODEL, D_FF), jnp.float32, -b3, b3)}
    _L3_ffn_all = _L3_ffn_setup()
    _L3_ffn_in = {k: v for k, v in _L3_ffn_all.items() if k in ('ln_gamma', 'ln_beta', 'router_w', 'w12', 'w3')}
    del _L3_ffn_all
    return {'x': x, 'ctx_768': ctx_768, 'mask_BxS2_bf1': mask_BxS2_bf1, 'L0_xattn_Wq': _L0_xattn_in['Wq'], 'L0_xattn_Wk': _L0_xattn_in['Wk'], 'L0_xattn_Wv': _L0_xattn_in['Wv'], 'L0_xattn_Wo': _L0_xattn_in['Wo'], 'L0_xattn_bo': _L0_xattn_in['bo'], 'L0_ffn_gate_w': _L0_ffn_in['gate_w'], 'L0_ffn_w1': _L0_ffn_in['w1'], 'L0_ffn_w2': _L0_ffn_in['w2'], 'L0_ffn_w3': _L0_ffn_in['w3'], 'L0_ffn_sw1': _L0_ffn_in['sw1'], 'L0_ffn_sw2': _L0_ffn_in['sw2'], 'L0_ffn_sw3': _L0_ffn_in['sw3'], 'L0_ffn_expert_bias': _L0_ffn_in['expert_bias'], 'L1_xattn_Wq': _L1_xattn_in['Wq'], 'L1_xattn_Wk': _L1_xattn_in['Wk'], 'L1_xattn_Wv': _L1_xattn_in['Wv'], 'L1_xattn_Wo': _L1_xattn_in['Wo'], 'L1_xattn_bo': _L1_xattn_in['bo'], 'L1_ffn_Wr': _L1_ffn_in['Wr'], 'L1_ffn_norm_w': _L1_ffn_in['norm_w'], 'L1_ffn_Wg': _L1_ffn_in['Wg'], 'L1_ffn_Wu': _L1_ffn_in['Wu'], 'L1_ffn_Wd': _L1_ffn_in['Wd'], 'L1_ffn_f_norm': _L1_ffn_in['f_norm'], 'L1_ffn_fWg': _L1_ffn_in['fWg'], 'L1_ffn_fWu': _L1_ffn_in['fWu'], 'L1_ffn_fWd': _L1_ffn_in['fWd'], 'L2_xattn_g_norm': _L2_xattn_in['g_norm'], 'L2_xattn_null_kv': _L2_xattn_in['null_kv'], 'L2_xattn_Wq': _L2_xattn_in['Wq'], 'L2_xattn_Wkv': _L2_xattn_in['Wkv'], 'L2_xattn_Wout': _L2_xattn_in['Wout'], 'L2_xattn_g_out': _L2_xattn_in['g_out'], 'L2_ffn_gate_w': _L2_ffn_in['gate_w'], 'L2_ffn_lb_bias': _L2_ffn_in['lb_bias'], 'L2_ffn_expert_gate_w': _L2_ffn_in['expert_gate_w'], 'L2_ffn_expert_up_w': _L2_ffn_in['expert_up_w'], 'L2_ffn_expert_down_w': _L2_ffn_in['expert_down_w'], 'L2_ffn_shared_gate_w': _L2_ffn_in['shared_gate_w'], 'L2_ffn_shared_up_w': _L2_ffn_in['shared_up_w'], 'L2_ffn_shared_down_w': _L2_ffn_in['shared_down_w'], 'L3_xattn_wq': _L3_xattn_in['wq'], 'L3_xattn_bq': _L3_xattn_in['bq'], 'L3_xattn_wk': _L3_xattn_in['wk'], 'L3_xattn_bk': _L3_xattn_in['bk'], 'L3_xattn_wv': _L3_xattn_in['wv'], 'L3_xattn_bv': _L3_xattn_in['bv'], 'L3_xattn_wo': _L3_xattn_in['wo'], 'L3_xattn_bo': _L3_xattn_in['bo'], 'L3_ffn_ln_gamma': _L3_ffn_in['ln_gamma'], 'L3_ffn_ln_beta': _L3_ffn_in['ln_beta'], 'L3_ffn_router_w': _L3_ffn_in['router_w'], 'L3_ffn_w12': _L3_ffn_in['w12'], 'L3_ffn_w3': _L3_ffn_in['w3']}

def reference(x, ctx_768, mask_BxS2_bf1, L0_xattn_Wq, L0_xattn_Wk, L0_xattn_Wv, L0_xattn_Wo, L0_xattn_bo, L0_ffn_gate_w, L0_ffn_w1, L0_ffn_w2, L0_ffn_w3, L0_ffn_sw1, L0_ffn_sw2, L0_ffn_sw3, L0_ffn_expert_bias, L1_xattn_Wq, L1_xattn_Wk, L1_xattn_Wv, L1_xattn_Wo, L1_xattn_bo, L1_ffn_Wr, L1_ffn_norm_w, L1_ffn_Wg, L1_ffn_Wu, L1_ffn_Wd, L1_ffn_f_norm, L1_ffn_fWg, L1_ffn_fWu, L1_ffn_fWd, L2_xattn_g_norm, L2_xattn_null_kv, L2_xattn_Wq, L2_xattn_Wkv, L2_xattn_Wout, L2_xattn_g_out, L2_ffn_gate_w, L2_ffn_lb_bias, L2_ffn_expert_gate_w, L2_ffn_expert_up_w, L2_ffn_expert_down_w, L2_ffn_shared_gate_w, L2_ffn_shared_up_w, L2_ffn_shared_down_w, L3_xattn_wq, L3_xattn_bq, L3_xattn_wk, L3_xattn_bk, L3_xattn_wv, L3_xattn_bv, L3_xattn_wo, L3_xattn_bo, L3_ffn_ln_gamma, L3_ffn_ln_beta, L3_ffn_router_w, L3_ffn_w12, L3_ffn_w3):
    import jax
    import jax.numpy as jnp

    def _L0_xattn_ref(x, context, Wq, Wk, Wv, Wo, bo):
        import jax, jax.numpy as jnp
        import numpy as np
        HEADS = 16
        DIM_HEAD = 64
        SCALE = DIM_HEAD ** (-0.5)
        QUERY_DIM = 128
        CONTEXT_DIM = 96
        INNER_DIM = HEADS * DIM_HEAD
        B, Nq, _ = x.shape
        Nk = context.shape[1]
        q = x @ Wq
        k = context @ Wk
        v = context @ Wv
        q = q.reshape(B, Nq, HEADS, DIM_HEAD).transpose(0, 2, 1, 3)
        k = k.reshape(B, Nk, HEADS, DIM_HEAD).transpose(0, 2, 1, 3)
        v = v.reshape(B, Nk, HEADS, DIM_HEAD).transpose(0, 2, 1, 3)
        sim = jnp.einsum('bhid,bhjd->bhij', q, k) * SCALE
        attn = jax.nn.softmax(sim, axis=-1)
        out = jnp.einsum('bhij,bhjd->bhid', attn, v)
        out = out.transpose(0, 2, 1, 3).reshape(B, Nq, INNER_DIM)
        return out @ Wo + bo

    def _L0_ffn_ref(x, gate_w, w1, w2, w3, sw1, sw2, sw3, expert_bias):
        import jax, jax.numpy as jnp
        import numpy as np
        NUM_EXPERTS = 8
        TOP_K = 2
        ROUTE_SCALE = 1.0
        DIM = 128
        HID = 128
        B, S = (2, 512)
        bs, slen, dim = x.shape
        xf = x.reshape(-1, dim)
        scores = jax.nn.sigmoid((xf @ gate_w.T).astype(jnp.float32))
        _, sel = jax.lax.top_k(scores + expert_bias[None, :], TOP_K)
        top_scores = jnp.take_along_axis(scores, sel, axis=1) * ROUTE_SCALE
        flat_sel = sel.reshape(-1)
        order = jnp.argsort(flat_sel, stable=True)
        scores_sorted = top_scores.reshape(-1)[order]
        tok_idx = order // TOP_K
        expert_ids = flat_sel[order]
        routed = xf[tok_idx]
        routed = (routed.astype(jnp.float32) * scores_sorted[:, None]).astype(x.dtype)
        out_r = jnp.zeros_like(routed)
        for e in range(NUM_EXPERTS):
            m = (expert_ids == e)[:, None]
            h = jax.nn.silu(routed @ w1[e].T) * (routed @ w3[e].T)
            out_r = out_r + jnp.where(m, h @ w2[e].T, jnp.zeros((), routed.dtype))
        shared = jax.nn.silu(xf @ sw1.T) * (xf @ sw3.T) @ sw2.T
        out_r = (out_r.astype(jnp.float32) * scores_sorted[:, None]).astype(x.dtype)
        out = shared.at[tok_idx].add(out_r)
        return out.reshape(bs, slen, dim)

    def _L1_xattn_ref(x, context, Wq, Wk, Wv, Wo, bo):
        import jax, jax.numpy as jnp
        import numpy as np
        NUM_HEADS = 8
        DIM_HEAD = 128
        SCALE = DIM_HEAD ** (-0.25)
        B, Tq, _ = x.shape
        Tk = context.shape[1]
        h, C = (NUM_HEADS, DIM_HEAD)
        q = (x @ Wq).reshape(B, Tq, h, C) * SCALE
        k = (context @ Wk).reshape(B, Tk, h, C) * SCALE
        v = (context @ Wv).reshape(B, Tk, h, C)
        attn = jax.nn.softmax(jnp.einsum('bqhc,bkhc->bhqk', q, k), axis=-1)
        out = jnp.einsum('bhqk,bkhc->bqhc', attn, v).reshape(B, Tq, h * C)
        return out @ Wo + bo

    def _L1_ffn_ref(hidden_states, Wr, norm_w, Wg, Wu, Wd, f_norm, fWg, fWu, fWd):
        import jax, jax.numpy as jnp
        import numpy as np
        TOP_K = 2
        CAPACITY = 512
        EPS = 1e-06
        W_SCALE = 0.02

        def _rms(x, w):
            return x * jax.lax.rsqrt(jnp.mean(x * x, axis=-1, keepdims=True) + EPS) * w
        B, S, H = hidden_states.shape
        E = Wr.shape[1]
        N = B * S
        x = hidden_states.reshape(N, H)
        probs = jax.nn.softmax(x @ Wr, axis=-1)
        w_topk, e_topk = jax.lax.top_k(probs, TOP_K)
        e_flat = e_topk.reshape(-1)
        oh = jax.nn.one_hot(e_flat, E, dtype=jnp.int32)
        pos = jnp.take_along_axis(jnp.cumsum(oh, axis=0) - 1, e_flat[:, None], axis=1)[:, 0]
        keep = pos < CAPACITY
        x_rep = jnp.repeat(x, TOP_K, axis=0)
        buf = jnp.zeros((E, CAPACITY, H), x.dtype).at[e_flat, pos].set(x_rep, mode='drop')
        h = _rms(buf, norm_w[:, None, :])
        gate = jax.nn.gelu(jnp.einsum('ech,ehf->ecf', h, Wg), approximate=False)
        up = jnp.einsum('ech,ehf->ecf', h, Wu)
        buf_out = jnp.einsum('ecf,efh->ech', gate * up, Wd) + buf
        exp_out = buf_out[e_flat, jnp.minimum(pos, CAPACITY - 1)]
        contrib = w_topk.reshape(-1)[:, None] * exp_out * keep[:, None].astype(x.dtype)
        combined = x + contrib.reshape(N, TOP_K, H).sum(axis=1)
        overflow = (~keep).reshape(N, TOP_K).any(axis=1)
        fh = _rms(x, f_norm)
        fout = jax.nn.gelu(fh @ fWg, approximate=False) * (fh @ fWu) @ fWd + x
        out = jnp.where(overflow[:, None], fout, combined)
        return out.reshape(B, S, H)

    def _L2_xattn_ref(x, context, mask, g_norm, null_kv, Wq, Wkv, Wout, g_out):
        import jax, jax.numpy as jnp
        import numpy as np
        import math
        B, N, M = (4, 128, 128)
        DIM, CTX_DIM = (128, 96)
        HEADS, DIM_HEAD = (16, 64)
        INNER = HEADS * DIM_HEAD

        def layer_norm(t, g, eps=1e-05):
            mean = jnp.mean(t, axis=-1, keepdims=True)
            var = jnp.mean((t - mean) ** 2, axis=-1, keepdims=True)
            return (t - mean) * jax.lax.rsqrt(var + eps) * g
        b = x.shape[0]
        scale = DIM_HEAD ** (-0.5)
        sqrt_scale = math.sqrt(scale)
        x = layer_norm(x, g_norm)
        q = x @ Wq
        kv = context @ Wkv
        k, v = jnp.split(kv, 2, axis=-1)

        def to_heads(t):
            return t.reshape(b, t.shape[1], HEADS, DIM_HEAD).transpose(0, 2, 1, 3)
        q, k, v = (to_heads(q), to_heads(k), to_heads(v))
        nk = jnp.broadcast_to(null_kv[0], (b, HEADS, 1, DIM_HEAD))
        nv = jnp.broadcast_to(null_kv[1], (b, HEADS, 1, DIM_HEAD))
        k = jnp.concatenate([nk, k], axis=2)
        v = jnp.concatenate([nv, v], axis=2)
        q = q * sqrt_scale
        k = k * sqrt_scale
        sim = jnp.einsum('bhid,bhjd->bhij', q, k)
        max_neg = -jnp.finfo(sim.dtype).max
        full_mask = jnp.pad(mask, ((0, 0), (1, 0)), constant_values=True)
        sim = jnp.where(full_mask[:, None, None, :], sim, max_neg)
        attn = jax.nn.softmax(sim.astype(jnp.float32), axis=-1).astype(sim.dtype)
        out = jnp.einsum('bhij,bhjd->bhid', attn, v)
        out = out.transpose(0, 2, 1, 3).reshape(b, -1, INNER)
        out = out @ Wout
        return layer_norm(out, g_out)

    def _L2_ffn_ref(x, gate_w, lb_bias, expert_gate_w, expert_up_w, expert_down_w, shared_gate_w, shared_up_w, shared_down_w):
        import jax, jax.numpy as jnp
        import numpy as np
        H = 128
        I = 64
        E = 8
        K = 2
        SI = I * 2
        B, S = (2, 128)

        def _mlp(x, gw, uw, dw):
            return jax.nn.silu(x @ gw.T) * (x @ uw.T) @ dw.T
        b, s, h = x.shape
        xf = x.reshape(-1, h)
        logits = xf @ gate_w.T + lb_bias
        scores = jax.nn.sigmoid(logits.astype(jnp.float32))
        topw, topi = jax.lax.top_k(scores, K)
        topw = (topw / (topw.sum(-1, keepdims=True) + 1e-08)).astype(x.dtype)
        out = jnp.zeros_like(xf)
        for e in range(E):
            m = topi == e
            sel = m.any(axis=-1)
            cnt = m.sum()
            wmean = (topw * m).sum() / jnp.maximum(cnt, 1).astype(topw.dtype)
            y = _mlp(xf, expert_gate_w[e], expert_up_w[e], expert_down_w[e])
            out = out + jnp.where(sel[:, None], y * wmean, jnp.zeros((), x.dtype))
        out = out.reshape(b, s, h)
        out = out + _mlp(x, shared_gate_w, shared_up_w, shared_down_w)
        return out

    def _L3_xattn_ref(x, y, wq, bq, wk, bk, wv, bv, wo, bo):
        import jax, jax.numpy as jnp
        import numpy as np
        N_HEADS = 16
        EMBED_DIM = 128
        CROSS_DIM = 96
        HEAD_DIM = EMBED_DIM // N_HEADS
        B, SQ, E = x.shape
        q = x @ wq.T + bq
        k = y @ wk.T + bk
        v = y @ wv.T + bv
        q = q.reshape(B, SQ, N_HEADS, HEAD_DIM).transpose(0, 2, 1, 3)
        k = k.reshape(B, -1, N_HEADS, HEAD_DIM).transpose(0, 2, 1, 3)
        v = v.reshape(B, -1, N_HEADS, HEAD_DIM).transpose(0, 2, 1, 3)
        scale = 1.0 / jnp.sqrt(jnp.asarray(HEAD_DIM, x.dtype))
        score = jnp.einsum('bhqd,bhkd->bhqk', q, k) * scale
        attn = jax.nn.softmax(score, axis=-1)
        out = jnp.einsum('bhqk,bhkd->bhqd', attn, v)
        out = out.transpose(0, 2, 1, 3).reshape(B, SQ, E)
        return out @ wo.T + bo

    def _L3_ffn_ref(x, ln_gamma, ln_beta, router_w, w12, w3):
        import math
        import jax, jax.numpy as jnp
        import numpy as np
        D_MODEL = 128
        D_FF = 512
        E = 8
        K = 2
        CAP_FACTOR = 1.25
        CLAMP = 10000.0
        LN_EPS = 1e-05
        B, S = (2, 256)
        Bq, Sq, D = x.shape
        T = Bq * Sq
        mu = jnp.mean(x, axis=-1, keepdims=True)
        var = jnp.mean(jnp.square(x - mu), axis=-1, keepdims=True)
        xn = (x - mu) * jax.lax.rsqrt(var + LN_EPS) * ln_gamma + ln_beta
        xf = xn.reshape(T, D)
        logits = jnp.clip(xf @ router_w.T, -CLAMP, CLAMP)
        top_v, top_i = jax.lax.top_k(logits, K)
        m = jnp.max(top_v, axis=-1, keepdims=True)
        ev = jnp.exp(top_v - m)
        top_p = ev / (jnp.sum(ev, axis=-1, keepdims=True) + 1e-12)
        Stot = T * K
        experts = top_i.reshape(-1)
        weights = top_p.reshape(-1)
        tokens = jnp.repeat(jnp.arange(T), K)
        oh = (experts[:, None] == jnp.arange(E)[None, :]).astype(jnp.int32)
        pos = jnp.take_along_axis(jnp.cumsum(oh, axis=0) - 1, experts[:, None], axis=1)[:, 0]
        C = max(1, math.ceil(T * K * CAP_FACTOR / E))
        kept = pos < C
        slot = jnp.where(kept, experts * C + pos, E * C)
        buf = jnp.zeros((E * C + 1, D), x.dtype).at[slot].set(xf[tokens])
        xb = buf[:E * C].reshape(E, C, D)
        gu = jnp.einsum('ecd,efd->ecf', xb, w12)
        g, u = jnp.split(gu, 2, axis=-1)
        h = jax.nn.silu(g) * u
        yb = jnp.einsum('ecf,edf->ecd', h, w3).reshape(E * C, D)
        ys = yb[jnp.minimum(slot, E * C - 1)] * (weights * kept.astype(weights.dtype))[:, None]
        out = jnp.zeros((T, D), x.dtype).at[tokens].add(ys)
        return out.reshape(Bq, Sq, D)
    x = x + _L0_xattn_ref(_layernorm(x, axis=-1), ctx_768, L0_xattn_Wq, L0_xattn_Wk, L0_xattn_Wv, L0_xattn_Wo, L0_xattn_bo)
    x = x + _L0_ffn_ref(_layernorm(x, axis=-1), L0_ffn_gate_w, L0_ffn_w1, L0_ffn_w2, L0_ffn_w3, L0_ffn_sw1, L0_ffn_sw2, L0_ffn_sw3, L0_ffn_expert_bias)
    x = x + _L1_xattn_ref(_layernorm(x, axis=-1), ctx_768, L1_xattn_Wq, L1_xattn_Wk, L1_xattn_Wv, L1_xattn_Wo, L1_xattn_bo)
    x = x + _L1_ffn_ref(_layernorm(x, axis=-1), L1_ffn_Wr, L1_ffn_norm_w, L1_ffn_Wg, L1_ffn_Wu, L1_ffn_Wd, L1_ffn_f_norm, L1_ffn_fWg, L1_ffn_fWu, L1_ffn_fWd)
    x = x + _L2_xattn_ref(_layernorm(x, axis=-1), ctx_768, mask_BxS2_bf1, L2_xattn_g_norm, L2_xattn_null_kv, L2_xattn_Wq, L2_xattn_Wkv, L2_xattn_Wout, L2_xattn_g_out)
    x = x + _L2_ffn_ref(_layernorm(x, axis=-1), L2_ffn_gate_w, L2_ffn_lb_bias, L2_ffn_expert_gate_w, L2_ffn_expert_up_w, L2_ffn_expert_down_w, L2_ffn_shared_gate_w, L2_ffn_shared_up_w, L2_ffn_shared_down_w)
    x = x + _L3_xattn_ref(_layernorm(x, axis=-1), ctx_768, L3_xattn_wq, L3_xattn_bq, L3_xattn_wk, L3_xattn_bk, L3_xattn_wv, L3_xattn_bv, L3_xattn_wo, L3_xattn_bo)
    x = x + _L3_ffn_ref(_layernorm(x, axis=-1), L3_ffn_ln_gamma, L3_ffn_ln_beta, L3_ffn_router_w, L3_ffn_w12, L3_ffn_w3)
    return x

_drawn_inputs = setup_inputs


def setup_inputs(seed=0):
    import zlib

    import numpy as np

    out = dict(_drawn_inputs(seed))
    spreads = {'L0_xattn_bo': (0.0, 0.1),
     'L0_ffn_expert_bias': (0.0, 0.469),
     'L1_xattn_bo': (0.0, 0.1),
     'L1_ffn_norm_w': (1.0, 0.6),
     'L1_ffn_f_norm': (1.0, 0.6),
     'L2_xattn_g_norm': (1.0, 0.2),
     'L2_xattn_g_out': (1.0, 0.2),
     'L2_ffn_lb_bias': (0.0, 0.8),
     'L3_ffn_ln_gamma': (1.0, 0.6),
     'L3_ffn_ln_beta': (0.0, 0.618)}
    factors = {'L1_ffn_Wg': 8.0,
     'L1_ffn_Wu': 8.0,
     'L1_ffn_Wd': 8.0,
     'L1_ffn_fWg': 8.0,
     'L1_ffn_fWu': 8.0,
     'L1_ffn_fWd': 8.0,
     'L2_xattn_null_kv': 3.17,
     'L2_ffn_gate_w': 8.0,
     'L2_ffn_expert_gate_w': 8.0,
     'L2_ffn_expert_up_w': 8.0,
     'L2_ffn_expert_down_w': 8.0,
     'L2_ffn_shared_gate_w': 8.0,
     'L2_ffn_shared_up_w': 8.0,
     'L2_ffn_shared_down_w': 8.0,
     'L3_xattn_bq': 7.953,
     'L3_xattn_bk': 64.0,
     'L3_xattn_bv': 3.472,
     'L3_xattn_bo': 3.474}
    for name, (base, spread) in spreads.items():
        noise = np.random.default_rng([zlib.crc32(name.encode()), seed]).standard_normal(out[name].shape)
        drawn = base * np.exp(spread * noise) if base else spread * noise
        out[name] = jnp.asarray(drawn.astype(out[name].dtype))
    for name, factor in factors.items():
        out[name] = (out[name] * factor).astype(out[name].dtype)
    return out
```

```python
from contextlib import ExitStack

import numpy as np

import concourse.bass as bass
from concourse import mybir

F32 = mybir.dt.float32
BF16 = mybir.dt.bfloat16
U8 = mybir.dt.uint8
ALU = mybir.AluOpType
ACT = mybir.ActivationFunctionType
AX = mybir.AxisListType

P = 128
B, S, D, CD, NK = 4, 512, 128, 96, 77
T = B * S // P
TPB = S // P
E = 8
NTOK = B * S

LN_EPS = 1e-5
RMS_EPS = 1e-6
NEG = -3.3e38
CAP1 = 512
CAP3 = 640
CLAMP = 10000.0

HEADS = [16, 8, 16, 16]
KEYS = [NK, NK, NK + 1, NK]
PER = [2, 1, 2, 16]
CHUNKS = [8, 8, 8, 1]
HALVES = [2, 1, 2, 2]
LAG = [1, 2, 1, 1]
SCALE = [64 ** -0.5, 128 ** -0.5, 64 ** -0.5, 8 ** -0.5]
KMAX = NK + 1
UNIT0 = [T * sum(HALVES[:l]) for l in range(4)]
PADV = 128

EB = E + 1
F0 = dict(gate=0, bias=8, up=136, down=136 + EB * 256)
F0["end"] = F0["down"] + EB * 128
F1 = dict(gate=0, norm=8, g=17, u=17 + 17 * 128, down=17 + 34 * 128)
F1["end"] = F1["down"] + 17 * 128
F2 = dict(gate=0, bias=8, g=136, u=136 + 5 * 128, down=136 + 10 * 128)
F2["end"] = F2["down"] + 5 * 128
F3 = dict(gate=0, gamma=8, beta=9, g=10, u=10 + 32 * 128, down=10 + 64 * 128)
F3["end"] = F3["down"] + 32 * 128
FA_COLS = max(F0["end"], F2["end"])
FB_COLS = max(F1["end"], F3["end"])
C_ID, C_ONE, C_TRI, C_IOTA, C_BM, C_GO = 0, 128, 256, 384, 512, 528
C_COL = 528 + 128
C_END = C_COL + 6


PLANS = {
    1: [(2 * e + c, P, [(e, 0, P, c == 0, c == 1)]) for e in range(E) for c in range(2)] + [(2 * E, P, [(E, 0, P, True, True)])],
    2: [(c, P, [(2 * c, 0, 64, True, True), (2 * c + 1, 64, P, True, True)]) for c in range(4)] + [(4, P, [(E, 0, P, True, True)])],
    3: [(4 * e + c, P, [(e, 0, P, c == 0, c == 3)]) for e in range(E) for c in range(4)],
}
SUMS = {1: EB, 2: EB, 3: E}
UP0 = {1: 0, 2: B * len(PLANS[1]), 3: B * (len(PLANS[1]) + len(PLANS[2]))}
DOWN0 = {1: 0, 2: B * SUMS[1], 3: B * (SUMS[1] + SUMS[2])}
POWS = [1, 1, 1, 2, 2, 1, 1, 2]
POW0 = [sum(POWS[:s]) for s in range(8)]


def fused_decoder_kernel(nc, x, ctxT, mask, consts, rows, aw, fw, out):
    with ExitStack() as ctx:
        def sb(name, shape, dt=F32):
            return ctx.enter_context(nc.sbuf_tensor(name, shape, dt))

        def sem(name):
            return ctx.enter_context(nc.semaphore(name))

        X = sb("X", [P, T, D])
        XTA = sb("XTA", [P, NTOK])
        AW = sb("AW", [P, 4096])
        G = sb("G", [P, B * 16 * KMAX])
        VW = sb("VW", [P, B, 10, D])
        KV = sb("KV", [P, 8, B * NK + 1])
        VB = sb("VB", [P, 8, 2 * PADV + 2 * KMAX])
        FA = sb("FA", [P, FA_COLS])
        FB = sb("FB", [P, FB_COLS])
        CT = sb("CT", [CD, B * NK])
        CN = sb("CN", [P, C_END])
        BO = sb("BO", [1, 3 * 128])
        MK = sb("MK", [1, B * KMAX], U8)
        MB = sb("MB", [1, B, 8, KMAX], BF16)
        MKF = sb("MKF", [1, B * KMAX])
        gcol = sb("gcol", [P, 1])
        ONEB = sb("ONEB", [1, P], BF16)
        NH = sb("NH", [P, T])
        ST = sb("ST", [P, T, 6])
        SM = sb("SM", [P, 16, T])
        XN = sb("XN", [P, 2, D])
        XTB = sb("XTB", [P, 2, P])
        QTB = sb("QTB", [P, 2, P])
        PR = sb("PR", [P, 4, 8 * KMAX])
        PT = sb("PT", [P, 5, P])
        MX = sb("MX", [P, 2, 8])
        RS = sb("RS", [P, 2, 8])
        RI = sb("RI", [P, 2, 8])
        OT = sb("OT", [P, 2, D])
        O6 = sb("O6", [P, 2, 6])
        O2 = sb("O2", [P, 2, 2])
        OR = sb("OR", [P, 2, 1])
        OE = sb("OE", [P, 2, 1])
        GS = sb("GS", [P, 2, 512])
        HS = sb("HS", [P, 2, 512])
        RT = sb("RT", [P, 12, T, E])
        RC = sb("RC", [P, 2, 24, E])
        W9 = sb("W9", [P, T, EB])
        S9 = sb("S9", [P, T, EB])
        W2 = sb("W2", [P, 4, E])
        PS = ctx.enter_context(nc.psum_tensor("PS", [P, 8, 512], F32))

        ident = CN[:, C_ID:C_ID + P]
        ones = CN[:, C_ONE:C_ONE + P]
        before = CN[:, C_TRI:C_TRI + P]
        iota = CN[:, C_IOTA:C_IOTA + T * E].rearrange("p (t e) -> p t e", e=E)
        headmask = CN[:, C_BM:C_BM + 16]
        g_out = CN[:, C_GO:C_GO + P]
        g_norm, null_k, null_v, bq, bk, bv = (CN[:, C_COL + i:C_COL + i + 1] for i in range(6))

        x_in, const_in, stored = sem("x_in"), sem("const_in"), sem("stored")
        aw_in = [sem(f"aw_in{l}") for l in range(4)]
        fw_in = [sem(f"fw_in{l}") for l in range(4)]
        zeroed, mask_made, nh_made = sem("zeroed"), sem("mask_made"), sem("nh_made")
        stats_done, var_ready, pow_ready, rstd_ready = sem("stats_done"), sem("var_ready"), sem("pow_ready"), sem("rstd_ready")
        p_mm, p_ev, vb_ready = sem("p_mm"), sem("p_ev"), sem("vb_ready")
        vb_step = sem("vb_step")
        vb_zero, null_in, gk_done = sem("vb_zero"), sem("null_in"), sem("gk_done")
        xn_ready, xt_ready, xtb_ready = sem("xn_ready"), sem("xt_ready"), sem("xtb_ready")
        q_ready, qtb_ready = sem("q_ready"), sem("qtb_ready")
        score_ready, max_ready, sub_ready, exp_ready = sem("score_ready"), sem("max_ready"), sem("sub_ready"), sem("exp_ready")
        sum_ready, inv_ready, prob_ready = sem("sum_ready"), sem("inv_ready"), sem("prob_ready")
        pt_ready, pte_ready, out_ready, upd_done = sem("pt_ready"), sem("pte_ready"), sem("out_ready"), sem("upd_done")
        o_chain, o_eps, o_rstd = sem("o_chain"), sem("o_eps"), sem("o_rstd")
        f_xn, f_xt, f_xtb, f_xta, f_gate = sem("f_xn"), sem("f_xt"), sem("f_xtb"), sem("f_xta"), sem("f_gate")
        r_chain, r_logit, r_exp, r_count, r_sums, r_done, wn_done = (
            sem("r_chain"), sem("r_logit"), sem("r_exp"), sem("r_count"), sem("r_sums"), sem("r_done"), sem("wn_done"))
        e_up, e_act, e_mul, e_down, e_acc = sem("e_up"), sem("e_act"), sem("e_mul"), sem("e_down"), sem("e_acc")
        t_in, t_up, t_act, t_mul, t_tr, t_ev, t_out, t_upd = (sem(n) for n in (
            "t_in", "t_up", "t_act", "t_mul", "t_tr", "t_ev", "t_out", "t_upd"))
        xres_chain = sem("xres_chain")

        block = ctx.enter_context(nc.Block())

        VB3 = VB[:, :, :].rearrange("p j n -> p (j n)")

        def gview(l):
            return G[:, 0:B * HEADS[l] * KEYS[l]].rearrange("p (b h k) -> p b h k", b=B, k=KEYS[l])

        def prview(l, i):
            return PR[:, i, 0:8 * KEYS[l]].rearrange("p (h k) -> p h k", k=KEYS[l])

        def wait(eng, s, v):
            if isinstance(v, int) and v <= 0:
                return
            eng.wait_ge(s, v)

        def wait_from(eng, s, base, v):
            if not isinstance(v, int) or v > 0:
                eng.wait_ge(s, base + v)

        def in_pairs(eng, body):
            body(0, 0)
            body(1, 1)
            with eng.Fori(1, T // 2 - 1) as i:
                body(2 * i, 0)
                body(2 * i + 1, 1)
            body(T - 2, 0)
            body(T - 1, 1)

        def at(start, n):
            return slice(start, start + n) if isinstance(start, int) else bass.ds(start, n)

        def last(t):
            return isinstance(t, int) and t == T - 1

        def batch_of(t):
            return t // TPB

        def windows(l, r, m):
            wide = PER[l] * KEYS[l]
            return [(j, PADV + r - j * wide) for j in range(CHUNKS[l]) if r < (j + 1) * wide and j * wide < r + m]

        def rows_of(l, c):
            return min(P, 8 * KEYS[l] - P * c)

        def prep_counts(l):
            k = CHUNKS[l]
            g = HEADS[l] if l < 3 else 0
            return k, g, k, B * HALVES[l] * 2
        PREP0 = [sum(sum(prep_counts(m)) for m in range(l)) for l in range(5)]

        @block.sync
        def _(sp):
            sp.dma_start(CT[:, :], ctxT).then_inc(const_in, 16)
            sp.dma_start(CN[:, :], consts).then_inc(const_in, 16)
            sp.dma_start(BO[:, :], rows).then_inc(const_in, 16)
            sp.dma_start(MK[:, :], mask).then_inc(const_in, 16)
            sp.dma_start(AW[:, :], aw[0]).then_inc(aw_in[0], 16)
            sp.dma_start(X[:, :, :], x.rearrange("(t p) d -> p t d", p=P)).then_inc(x_in, 16)
            sp.dma_start(FA[:, 0:F0["end"]], fw[0]).then_inc(fw_in[0], 16)
            sp.dma_start(FB[:, 0:F1["end"]], fw[1]).then_inc(fw_in[1], 16)
            for l in range(1, 4):
                sp.wait_ge(p_mm, PREP0[l])
                n = 4096 if l < 3 else 512
                sp.dma_start(AW[:, 0:n], aw[l]).then_inc(aw_in[l], 16)
                if l >= 2:
                    if l == 2:
                        sp.wait_ge(t_upd, T)
                    else:
                        sp.wait_ge(e_acc, DOWN0[2])
                    dst = FA if l == 2 else FB
                    sp.dma_start(dst[:, 0:(F2 if l == 2 else F3)["end"]], fw[l]).then_inc(fw_in[l], 16)
            with sp.Fori(0, B) as b:
                sp.wait_ge(e_acc, DOWN0[3] + (b + 1) * SUMS[3])
                sp.dma_start(out.rearrange("(b t p) d -> p b t d", p=P, t=TPB)[:, b, :, :],
                             X[:, :, :].rearrange("p (b t) d -> p b t d", t=TPB)[:, b, :, :]).then_inc(stored, 16)
            sp.wait_ge(stored, 16 * B)

        @block.tensor
        def _(pe):
            mm = nc.tensor.matmul

            def prep(l):
                k, g, v, vw = prep_counts(l)
                n0 = PREP0[l]
                pe.wait_ge(aw_in[l], 16)
                if l == 0:
                    pe.wait_ge(const_in, 64)
                slot = [n0]

                def bank():
                    wait(pe, p_ev, slot[0] - 1)
                    slot[0] += 1
                    return 6 + (slot[0] - 1) % 2
                wide = 1024 if l < 3 else P
                for j in range(k):
                    bk_ = bank()
                    mm(PS[:, bk_, 0:B * NK], AW[0:CD, j * P:(j + 1) * P], CT[:, :], start=True, stop=True).then_inc(p_mm, 1)
                if l < 3:
                    dh = P // PER[l]
                    for h in range(g):
                        j, r = h // PER[l], dh * (h % PER[l])
                        if h == 0:
                            pe.wait_ge(p_ev, n0 + k)
                            if l == 2:
                                pe.wait_ge(null_in, 1)
                        bk_ = bank()
                        n = B * NK + (l == 2)
                        mm(PS[:, bk_, 0:n], AW[r:r + dh, 2048 + j * P:2048 + (j + 1) * P], KV[r:r + dh, j, 0:n],
                           start=True, stop=True).then_inc(p_mm, 1)
                for j in range(v):
                    bk_ = bank()
                    mm(PS[:, bk_, 0:B * NK], AW[0:CD, wide + j * P:wide + (j + 1) * P], CT[:, :], start=True, stop=True).then_inc(p_mm, 1)
                w0 = 3072 if l < 3 else 384
                for b in range(B):
                    pe.wait_ge(vb_ready, B * l + b + 1)
                    for hf in range(HALVES[l]):
                        for part in ([0, 1, 2, 3], [4]):
                            bk_ = bank()
                            for c in part:
                                m = rows_of(l, c)
                                r = 8 * KEYS[l] * hf + P * c
                                ws = windows(l, r, m) if l < 3 else [(0, r)]
                                for n, (j, col) in enumerate(ws):
                                    lhs = VB[:, j, col:col + m] if l < 3 else VB3[:, col:col + m]
                                    op = mm(PS[0:m, bk_, (c % 4) * P:(c % 4 + 1) * P], lhs,
                                            AW[:, w0 + j * P:w0 + (j + 1) * P], start=(n == 0), stop=(n == len(ws) - 1))
                            op.then_inc(p_mm, 1)

            def attention(l):
                H, K8 = HALVES[l], 8 * KEYS[l]
                t0, u0 = T * l, UNIT0[l]
                lag = LAG[l]
                pe.wait_ge(p_ev, PREP0[l + 1])
                if l == 2:
                    pe.wait_ge(mask_made, 1)
                if l == 3:
                    pe.wait_ge(gk_done, B)

                def transpose_x(t, par):
                    pe.wait_ge(xn_ready, t0 + t + 1)
                    wait(pe, xtb_ready, t0 + t)
                    if l == 3:
                        wait(pe, qtb_ready, t)
                    mm(PS[:, 5, P:2 * P], XN[:, par, :], ident, is_transpose=True, start=True, stop=True).then_inc(xt_ready, 1)

                def query(t, par):
                    pe.wait_ge(xtb_ready, t0 + t + 1)
                    mm(PS[:, 5, 2 * P:3 * P], AW[:, 256:384], XTB[:, par, :], start=True, stop=True).then_inc(q_ready, 1)

                def scores(t, par, hf):
                    u = t * H + hf
                    lhs = XTB if l < 3 else QTB
                    if hf == 0:
                        if l < 3:
                            pe.wait_ge(xtb_ready, t0 + t + 1)
                        else:
                            pe.wait_ge(qtb_ready, t + 1)
                    wait(pe, sub_ready, u0 + u - 1)
                    bk_ = 2 * ((par * H + hf) % 2)
                    flat = PS[:, bk_:bk_ + 2, :].rearrange("p a n -> p (a n)")
                    g = gview(l).rearrange("p b h k -> p b (h k)")[:, batch_of(t), (hf * K8):(hf * K8) + K8]
                    for a, z in ((0, 512), (512, K8)):
                        op = mm(flat[:, a:z], lhs[:, par, :], g[:, a:z], start=True, stop=(l != 2))
                        if l == 2:
                            mb = MB[:, :, :, :].rearrange("p b h k -> p b (h k)")[:, batch_of(t), a:z]
                            op = mm(flat[:, a:z], ONEB[:, :], mb, start=False, stop=True)
                    op.then_inc(score_ready, 1)

                def transpose_p(t, par, hf, x_next):
                    u = t * H + hf
                    pe.wait_ge(prob_ready, u0 + u + 1)
                    wait(pe, pte_ready, u0 + u)
                    src = PR[:, (par * H + hf) % (2 * H), :]
                    for c in range(4):
                        mm(PS[:, 4, c * P:(c + 1) * P], src[:, c * P:(c + 1) * P], ident, is_transpose=True,
                           start=True, stop=True)
                    x_next()
                    m = rows_of(l, 4)
                    mm(PS[0:m, 5, 0:P], src[:, 4 * P:4 * P + m], ident, is_transpose=True,
                       start=True, stop=True).then_inc(pt_ready, 1)

                def project(t, par, hf):
                    u = t * H + hf
                    acc = PS[:, 6 + par, 0:D]
                    if hf == 0:
                        wait_from(pe, stats_done, T * (2 * l + 1), t - 1)
                        if l != 2:
                            mm(acc, CN[0:1, C_ONE:C_ONE + P], BO[0:1, min(l, 2) * P:(min(l, 2) + 1) * P], start=True, stop=False)
                    pe.wait_ge(pte_ready, u0 + u + 1)
                    for c in range(5):
                        m = rows_of(l, c)
                        end = hf == H - 1 and c == 4
                        op = mm(acc, PT[0:m, c, :], VW[0:m, batch_of(t), hf * 5 + c, :],
                                start=(l == 2 and hf == 0 and c == 0), stop=end)
                    if hf == H - 1:
                        op.then_inc(out_ready, 1)

                transpose_x(0, 0)
                if l == 3:
                    query(0, 0)

                def body(t, par):
                    more = not last(t)
                    if isinstance(t, int) and t < lag:
                        if more:
                            transpose_x(t + 1, 1 - par)
                            if l == 3:
                                query(t + 1, 1 - par)
                        for hf in range(H):
                            scores(t, par, hf)
                        return
                    for hf in range(H):
                        def x_next():
                            if not more:
                                pe.wait_ge(xtb_ready, t0 + T)
                                if l == 3:
                                    pe.wait_ge(qtb_ready, T)
                            if more and hf == 0:
                                transpose_x(t + 1, 1 - par)
                            if more and hf == 1:
                                pe.wait_ge(xtb_ready, t0 + t + 2)
                            if more and l == 3 and hf == 1:
                                query(t + 1, 1 - par)
                        transpose_p(t - lag, (par + lag) % 2, hf, x_next)
                        scores(t, par, hf)
                        project(t - lag, (par + lag) % 2, hf)

                in_pairs(pe, body)
                for t in range(T - lag, T):
                    for hf in range(H):
                        transpose_p(t, t % 2, hf, lambda: pe.wait_ge(xtb_ready, t0 + T))
                        project(t, t % 2, hf)

            def front(l):
                t0 = T * l
                pe.wait_ge(fw_in[l], 16)
                fbuf, off = (FA if l % 2 == 0 else FB), 0

                def gate(t, par):
                    pe.wait_ge(f_xtb, t0 + t + 1)
                    mm(PS[:, 3, at(t * E, E)], XTB[:, par, :], fbuf[:, off:off + E], start=True, stop=True).then_inc(f_gate, 1)

                def body(t, par):
                    pe.wait_ge(f_xn, t0 + t + 1)
                    wait(pe, f_xtb, t0 + t - 1)
                    mm(PS[:, 4 + par, 0:P], XN[:, par, :], ident, is_transpose=True, start=True, stop=True).then_inc(f_xt, 1)
                    if not (isinstance(t, int) and t == 0):
                        gate(t - 1, 1 - par)
                in_pairs(pe, body)
                gate(T - 1, 1)

            def router(l):
                if l in (1, 3):
                    m = RT[:, 5, :, :].rearrange("p t e -> p (t e)")
                    pe.wait_ge(r_count, l)
                    mm(PS[:, 0, 0:T * E], before, m, start=True, stop=True)
                    mm(PS[:, 1, 0:T * E], ones, m, start=True, stop=True).then_inc(r_sums, 1)
                if l == 2:
                    pe.wait_ge(r_count, 2)
                    m = RT[:, 5:7, :, :].rearrange("p a t e -> p (a t e)")
                    mm(PS[:, 0, 0:2 * T * E], ones, m, start=True, stop=True).then_inc(r_sums, 1)

            def experts0():
                pe.wait_ge(p_ev, PREP0[2])
                pe.wait_ge(r_done, 1)

                def up(t, par, g):
                    n = t * 3 + g
                    if g == 0:
                        pe.wait_ge(t_in, t + 1)
                    wait(pe, t_mul, n - 1)
                    q = (par * 3 + g) % 2
                    mm(PS[:, 2 * q, 0:384], XTB[:, par, :], FA[:, F0["up"] + g * 768:F0["up"] + g * 768 + 384], start=True, stop=True)
                    mm(PS[:, 2 * q + 1, 0:384], XTB[:, par, :], FA[:, F0["up"] + g * 768 + 384:F0["up"] + g * 768 + 768],
                       start=True, stop=True).then_inc(t_up, 1)

                def turn(t, par, g):
                    n = t * 3 + g
                    q = (par * 3 + g) % 2
                    pe.wait_ge(t_mul, n + 1)
                    wait(pe, t_ev, n)
                    for k in range(3):
                        op = mm(PS[:, 4, k * P:(k + 1) * P], HS[:, q, k * P:(k + 1) * P], ident, is_transpose=True, start=True, stop=True)
                    op.then_inc(t_tr, 1)

                def down(t, par, g):
                    n = t * 3 + g
                    if g == 0:
                            wait_from(pe, stats_done, 2 * T, t - 1)
                    pe.wait_ge(t_ev, n + 1)
                    for k in range(3):
                        e = g * 3 + k
                        op = mm(PS[:, 6 + par, 0:D], PT[:, k, :], FA[:, F0["down"] + e * P:F0["down"] + (e + 1) * P],
                                start=(e == 0), stop=(e == EB - 1))
                    if g == 2:
                        op.then_inc(t_out, 1)

                def body(t, par):
                    first = isinstance(t, int) and t == 0
                    for g in range(3):
                        prev = (t, par, g - 1) if g else (t - 1, 1 - par, 2)
                        lag = not (first and g == 0)
                        up(t, par, g)
                        if lag:
                            turn(*prev)
                            down(*prev)
                in_pairs(pe, body)
                turn(T - 1, 1, 2)
                down(T - 1, 1, 2)

            def experts(l):
                plan = PLANS[l]
                n0, q0 = UP0[l], DOWN0[l]
                N, Q = len(plan), SUMS[l]
                fbuf = FA if l == 2 else FB
                fo = {1: F1, 2: F2, 3: F3}[l]
                pe.wait_ge(f_xta, T * (l + 1))
                pe.wait_ge(r_done, l + 1)
                if l == 1:
                    pe.wait_ge(wn_done, 1)

                def up(b, n):
                    c, m, _ = plan[n]
                    k = n0 + b * N + n
                    if n >= 2:
                        pe.wait_ge(e_mul, k - 1)
                    rhs = XTA[:, bass.ds(b * S, S)]
                    bkp = n % 2
                    mm(PS[0:m, bkp, :], fbuf[:, fo["g"] + c * P:fo["g"] + c * P + m], rhs, start=True, stop=True)
                    mm(PS[0:m, 2 + bkp, :], fbuf[:, fo["u"] + c * P:fo["u"] + c * P + m], rhs, start=True, stop=True).then_inc(e_up, 1)

                def down(b, n):
                    c, m, downs = plan[n]
                    k = n0 + b * N + n
                    pe.wait_ge(e_mul, k + 1)
                    for e, lo, hi, start, stop in downs:
                        q = q0 + b * Q + e
                        if start and e >= 2:
                            pe.wait_ge(e_acc, q - 1)
                        for j in range(TPB):
                            op = mm(PS[:, 4 + e % 2, j * P:(j + 1) * P], HS[lo:hi, n % 2, j * P:(j + 1) * P],
                                    fbuf[lo:hi, fo["down"] + c * P:fo["down"] + (c + 1) * P],
                                    start=(start and j == 0), stop=stop, skip_group_check=True)
                        if stop:
                            op.then_inc(e_down, 1)

                with pe.Fori(0, B) as b:
                    for n in range(N):
                        up(b, n)
                        if n:
                            down(b, n - 1)
                    down(b, N - 1)
                    pe.wait_ge(e_mul, n0 + (b + 1) * N)
                    pe.wait_ge(e_acc, q0 + (b + 1) * Q)

            prep(0)
            for l in range(4):
                attention(l)
                front(l)
                if l < 3:
                    prep(l + 1)
                router(l)
                if l == 0:
                    experts0()
                else:
                    experts(l)

        @block.scalar
        def _(act):
            A = nc.scalar.activation

            def prep(l):
                k, g, v, vw = prep_counts(l)
                slot = [PREP0[l]]

                def bank():
                    slot[0] += 1
                    act.wait_ge(p_mm, slot[0])
                    return 6 + (slot[0] - 1) % 2
                bkv = [bk, bv] if l == 3 else [0.0, 0.0]

                def take(dst, src, bias):
                    if l == 3:
                        return A(dst, src, ACT.Identity, bias=bias)
                    return A(dst, src, ACT.Copy)
                if l > 0:
                    act.wait_ge(vb_ready, B * l)
                for j in range(k):
                    b_ = bank()
                    take(KV[:, j, 0:B * NK], PS[:, b_, 0:B * NK], bkv[0]).then_inc(p_ev, 1)
                if l == 3:
                    act.wait_ge(gk_done, B)
                for h in range(g):
                    b_ = bank()
                    o = 1 if l == 2 else 0
                    dst = gview(l)[:, :, h, o:o + NK]
                    src = PS[:, b_, 0:B * NK].rearrange("p (b k) -> p b k", k=NK)
                    if l == 2:
                        A(dst, src, ACT.Copy, scale=gcol[:, 0:1])
                        A(gview(l)[:, :, h, 0:1], PS[:, b_, B * NK:B * NK + 1].unsqueeze(1).to_broadcast([P, B, 1]),
                          ACT.Copy, scale=gcol[:, 0:1]).then_inc(p_ev, 1)
                    else:
                        A(dst, src, ACT.Copy, scale=float(SCALE[l])).then_inc(p_ev, 1)
                for j in range(v):
                    b_ = bank()
                    take(KV[:, j, 0:B * NK], PS[:, b_, 0:B * NK], bkv[1]).then_inc(p_ev, 1)
                for b in range(B):
                    for hf in range(HALVES[l]):
                        b_ = bank()
                        A(VW[:, b, hf * 5:hf * 5 + 4, :], PS[:, b_, :].rearrange("p (c d) -> p c d", d=D), ACT.Copy).then_inc(p_ev, 1)
                        b_ = bank()
                        m = rows_of(l, 4)
                        A(VW[0:m, b, hf * 5 + 4, :], PS[0:m, b_, 0:D], ACT.Copy).then_inc(p_ev, 1)

            def attention(l):
                H = HALVES[l]
                t0, u0 = T * l, UNIT0[l]

                def x_out(t, par):
                    act.wait_ge(xt_ready, t0 + t + 1)
                    if l < 3:
                        wait(act, score_ready, u0 + (t - 1) * H)
                    else:
                        wait(act, q_ready, t - 1)
                    A(XTB[:, par, :], PS[:, 5, P:2 * P], ACT.Copy).then_inc(xtb_ready, 1)

                def q_out(t, par):
                    act.wait_ge(q_ready, t + 1)
                    wait(act, score_ready, u0 + (t - 1) * H)
                    A(QTB[:, par, :], PS[:, 5, 2 * P:3 * P], ACT.Identity, bias=bq).then_inc(qtb_ready, 1)

                def p_out(t, par, hf):
                    act.wait_ge(pt_ready, u0 + t * H + hf + 1)
                    A(PT[:, 0:4, :], PS[:, 4, :].rearrange("p (c n) -> p c n", n=P), ACT.Copy)
                    m = rows_of(l, 4)
                    A(PT[0:m, 4, :], PS[0:m, 5, 0:P], ACT.Copy).then_inc(pte_ready, 1)

                def expo(t, par, hf):
                    u = t * H + hf
                    act.wait_ge(sub_ready, u0 + u + 1)
                    p = prview(l, (par * H + hf) % (2 * H))
                    A(p, p, ACT.Exp).then_inc(exp_ready, 1)

                x_out(0, 0)
                if l == 3:
                    q_out(0, 0)

                lag = LAG[l]

                def body(t, par):
                    first = isinstance(t, int) and t == 0
                    for hf in range(H):
                        if not (isinstance(t, int) and t < lag):
                            p_out(t - lag, (par + lag) % 2, hf)
                        if hf == 0 and not last(t):
                            x_out(t + 1, 1 - par)
                        if l == 3 and (hf == 1 or first) and not last(t) and not (first and hf == 1):
                            q_out(t + 1, 1 - par)
                        expo(t, par, hf)
                in_pairs(act, body)
                for t in range(T - lag, T):
                    for hf in range(H):
                        p_out(t, t % 2, hf)

            def front(l):
                t0 = T * l

                def body(t, par):
                    act.wait_ge(f_xt, t0 + t + 1)
                    wait(act, f_gate, t0 + t - 1)
                    wait(act, f_xta, t0 + t - 1)
                    if l == 3:
                        A(XTB[:, par, :], PS[:, 4 + par, 0:P], ACT.Identity, bias=FB[:, F3["beta"]:F3["beta"] + 1],
                          scale=FB[:, F3["gamma"]:F3["gamma"] + 1]).then_inc(f_xtb, 1)
                    else:
                        A(XTB[:, par, :], PS[:, 4 + par, 0:P], ACT.Copy).then_inc(f_xtb, 1)
                if l == 3:
                    act.wait_ge(fw_in[3], 16)
                in_pairs(act, body)

            def router(l):
                if l == 0:
                    act.wait_ge(f_gate, T)
                    A(RT[:, 0, :, :], PS[:, 3, 0:T * E].rearrange("p (t e) -> p t e", e=E), ACT.Exp, scale=-1.0).then_inc(r_exp, 1)
                else:
                    act.wait_ge(r_logit, l)
                    if l == 3:
                        A(SM[:, 12, :], SM[:, 12, :], ACT.Exp).then_inc(r_exp, 1)
                    else:
                        A(RT[:, 0, :, :], RT[:, 0, :, :], ACT.Exp, scale=(1.0 if l == 1 else -1.0)).then_inc(r_exp, 1)

            def experts0():
                def gate(t, par, g):
                    n = t * 3 + g
                    q = (par * 3 + g) % 2
                    act.wait_ge(t_up, n + 1)
                    wait(act, t_mul, n - 1)
                    for k in range(3):
                        op = A(GS[:, q, k * P:(k + 1) * P], PS[:, 2 * q, k * P:(k + 1) * P], ACT.Silu,
                               scale=S9[:, t, g * 3 + k:g * 3 + k + 1])
                    op.then_inc(t_act, 1)

                def ev(t, par, g):
                    n = t * 3 + g
                    act.wait_ge(t_tr, n + 1)
                    A(PT[:, 0:3, :], PS[:, 4, 0:384].rearrange("p (c n) -> p c n", n=P), ACT.Copy).then_inc(t_ev, 1)

                act.wait_ge(r_done, 1)

                def body(t, par):
                    first = isinstance(t, int) and t == 0
                    for g in range(3):
                        gate(t, par, g)
                        if not (first and g == 0):
                            ev(*((t, par, g - 1) if g else (t - 1, 1 - par, 2)))
                in_pairs(act, body)
                ev(T - 1, 1, 2)

            def experts(l):
                plan, n0 = PLANS[l], UP0[l]
                N = len(plan)
                func = ACT.Gelu if l == 1 else ACT.Silu
                with act.Fori(0, B) as b:
                    for n in range(N):
                        m = plan[n][1]
                        act.wait_ge(e_up, n0 + b * N + n + 1)
                        if n >= 2:
                            act.wait_ge(e_mul, n0 + b * N + n - 1)
                        A(GS[0:m, n % 2, :], PS[0:m, n % 2, :], func).then_inc(e_act, 1)
                    act.wait_ge(e_mul, n0 + (b + 1) * N)

            act.wait_ge(const_in, 64)
            A(gcol[:, 0:1], g_norm, ACT.Copy, scale=float(SCALE[2])).then_inc(zeroed, 1)
            act.wait_ge(zeroed, 1)
            prep(0)
            for l in range(4):
                attention(l)
                front(l)
                if l < 3:
                    prep(l + 1)
                router(l)
                if l == 0:
                    experts0()
                else:
                    experts(l)

        @block.gpsimd
        def _(pool):
            g = nc.gpsimd
            links = [0]

            def link(op):
                links[0] += 1
                op.then_inc(vb_step, 1)
                pool.wait_ge(vb_step, links[0])

            def powers(l, stage):
                for n in range(POWS[stage]):
                    c = POW0[stage] + n
                    pool.wait_ge(var_ready, c + 1)
                    g.tensor_tensor(SM[:, 8 + n, :], SM[:, 6 + n, :], NH[:, :], ALU.pow).then_inc(pow_ready, 1)

            def prep(l):
                k, gh, v, vw = prep_counts(l)
                if l > 0:
                    pool.wait_ge(p_ev, PREP0[l])
                if l < 3:
                    g.memset(VB[:, :, :], 0.0).then_inc(vb_zero, 1)
                    pool.wait_ge(vb_zero, l + 1)
                if l == 2:
                    pool.wait_ge(p_ev, PREP0[l] )
                    g.tensor_copy(KV[:, :, B * NK:B * NK + 1], null_k.unsqueeze(1).to_broadcast([P, 8, 1])).then_inc(null_in, 1)
                    for hh in range(2):
                        r = 64 * hh
                        c = PADV + hh * KEYS[2]
                        link(g.tensor_copy(VB[r:r + 64, :, c:c + 1], CN[r:r + 64, C_COL + 2:C_COL + 3].unsqueeze(1).to_broadcast([64, 8, 1])))
                pool.wait_ge(p_ev, PREP0[l] + k + gh + v)
                for b in range(B):
                    if b:
                        pool.wait_ge(p_mm, PREP0[l] + k + gh + v + b * HALVES[l] * 2)
                    if l < 3:
                        for hh in range(PER[l]):
                            dh = P // PER[l]
                            r = dh * hh
                            c = PADV + hh * KEYS[l] + (l == 2)
                            op = g.tensor_copy(VB[r:r + dh, :, c:c + NK], KV[r:r + dh, :, b * NK:(b + 1) * NK])
                            if hh < PER[l] - 1:
                                link(op)
                        op.then_inc(vb_ready, 1)
                        pool.wait_ge(vb_ready, B * l + b + 1)
                    else:
                        g.tensor_tensor(VB3[:, 0:16 * NK].rearrange("p (h k) -> p h k", k=NK),
                                        KV[:, 0, b * NK:(b + 1) * NK].unsqueeze(1).to_broadcast([P, 16, NK]),
                                        headmask.unsqueeze(2).to_broadcast([P, 16, NK]), ALU.mult).then_inc(vb_ready, 1)

            def attention(l):
                H = HALVES[l]
                t0, u0 = T * l, UNIT0[l]

                def body(t, par):
                    for hf in range(H):
                        u = t * H + hf
                        pool.wait_ge(inv_ready, u0 + u + 1)
                        q = (par * H + hf) % 2
                        p = prview(l, (par * H + hf) % (2 * H))
                        g.tensor_tensor(p, p, RI[:, q, :].unsqueeze(2).to_broadcast([P, 8, KEYS[l]]), ALU.mult).then_inc(prob_ready, 1)
                    if l == 2:
                        lagged = t - 1
                        if not (isinstance(t, int) and t == 0):
                            o_pow(lagged, 1 - par)

                def o_pow(t, par):
                    pool.wait_ge(o_eps, t + 1)
                    g.tensor_tensor(OR[:, par, :], OE[:, par, :], NH[:, 0:1], ALU.pow).then_inc(o_rstd, 1)
                in_pairs(pool, body)
                if l == 2:
                    o_pow(T - 1, 1)

            def front(l):
                t0 = T * l

                def body(t, par):
                    pool.wait_ge(f_xtb, t0 + t + 1)
                    g.tensor_copy(XTA[:, at(t * P, P)],
                                  XTB[:, par, :]).then_inc(f_xta, 1)
                in_pairs(pool, body)

            def experts0():
                def body(t, par):
                    wait(pool, t_up, 3 * (t - 1))
                    if isinstance(t, int) and t == 0:
                        pool.wait_ge(f_gate, T)
                    src = XTA[:, at(t * P, P)]
                    g.tensor_copy(XTB[:, par, :], src).then_inc(t_in, 1)
                pool.wait_ge(f_xta, T)
                in_pairs(pool, body)

            g.memset(NH[:, :], -0.5).then_inc(nh_made, 1)
            pool.wait_ge(nh_made, 1)
            pool.wait_ge(const_in, 64)
            prep(0)
            for l in range(4):
                powers(l, 2 * l)
                attention(l)
                powers(l, 2 * l + 1)
                front(l)
                if l < 3:
                    prep(l + 1)
                if l == 0:
                    experts0()

        @block.vector
        def _(dve):
            v = nc.vector
            links = [0]

            def link(op):
                links[0] += 1
                op.then_inc(r_chain, 1)
                dve.wait_ge(r_chain, links[0])

            def tt(o, a, b_, op):
                return v.tensor_tensor(o, a, b_, op)

            def ts(o, a, s1, s2, op0, op1=None):
                return v.tensor_scalar(o, a, s1, s2, op0, op1) if op1 is not None else v.tensor_scalar(o, a, s1, s2, op0)

            def deviations(stage):
                l = stage // 2
                dve.wait_ge(stats_done, T * (stage + 1))
                m0, m1, q0, q1 = (ST[:, :, i] for i in (1, 4, 2, 5))
                link(tt(SM[:, 1, :], m0, m1, ALU.add))
                link(tt(SM[:, 2, :], q0, q1, ALU.add))
                link(tt(SM[:, 3, :], m0, m1, ALU.subtract))
                link(tt(SM[:, 3, :], SM[:, 3, :], SM[:, 3, :], ALU.mult))
                link(ts(SM[:, 0, :], SM[:, 1, :], 0.5, None, ALU.mult))
                link(ts(SM[:, 2, :], SM[:, 2, :], 1.0 / D, None, ALU.mult))
                link(v.scalar_tensor_tensor(out=SM[:, 5, :], in0=SM[:, 3, :], scalar=0.25, in1=SM[:, 2, :], op0=ALU.mult, op1=ALU.add))
                v.tensor_scalar(SM[:, 6, :], SM[:, 5, :], LN_EPS, None, ALU.add).then_inc(var_ready, 1)
                dve.wait_ge(pow_ready, POW0[stage] + 1)
                if POWS[stage] == 1:
                    link(v.tensor_copy(SM[:, 10, :], SM[:, 8, :]))
                    return
                link(tt(SM[:, 3, :], SM[:, 5, :], SM[:, 8, :], ALU.mult))
                link(tt(SM[:, 3, :], SM[:, 3, :], SM[:, 8, :], ALU.mult))
                v.tensor_scalar(SM[:, 7, :], SM[:, 3, :], RMS_EPS if stage == 3 else LN_EPS, None, ALU.add).then_inc(var_ready, 1)
                dve.wait_ge(pow_ready, POW0[stage] + 2)
                link(tt(SM[:, 10, :], SM[:, 8, :], SM[:, 9, :], ALU.mult))
                if stage == 3:
                    link(tt(SM[:, 11, :], SM[:, 7, :], SM[:, 9, :], ALU.mult))

            def stats(t):
                v.bn_stats(ST[:, t, :], X[:, t, :]).then_inc(stats_done, 1)

            def attention(l):
                H = HALVES[l]
                t0, u0 = T * l, UNIT0[l]
                K8 = 8 * KEYS[l]

                def x_norm(t, par):
                    wait(dve, xt_ready, t0 + t - 1)
                    v.tensor_scalar(XN[:, par, :], X[:, t, :], SM[:, 0, at(t, 1)], SM[:, 10, at(t, 1)],
                                    ALU.subtract, ALU.mult).then_inc(xn_ready, 1)

                def shift(t, par, hf):
                    u = t * H + hf
                    q = (par * H + hf) % 2
                    sc = PS[:, 2 * q:2 * q + 2, :].rearrange("p a n -> p (a n)")[:, 0:K8].rearrange("p (h k) -> p h k", k=KEYS[l])
                    dve.wait_ge(score_ready, u0 + u + 1)
                    v.tensor_reduce(MX[:, q, :], sc, AX.X, ALU.max).then_inc(max_ready, 1)
                    dve.wait_ge(max_ready, u0 + u + 1)
                    wait(dve, pt_ready, u0 + u - 2 * H + 1)
                    v.tensor_tensor(prview(l, (par * H + hf) % (2 * H)), sc, MX[:, q, :].unsqueeze(2).to_broadcast([P, 8, KEYS[l]]),
                                    ALU.subtract).then_inc(sub_ready, 1)

                def total(t, par, hf):
                    u = t * H + hf
                    q = (par * H + hf) % 2
                    dve.wait_ge(exp_ready, u0 + u + 1)
                    v.tensor_reduce(RS[:, q, :], prview(l, (par * H + hf) % (2 * H)), AX.X, ALU.add).then_inc(sum_ready, 1)
                    dve.wait_ge(sum_ready, u0 + u + 1)
                    wait(dve, prob_ready, u0 + u - 1)
                    v.reciprocal(RI[:, q, :], RS[:, q, :]).then_inc(inv_ready, 1)

                def update(t, par):
                    dve.wait_ge(out_ready, t0 + t + 1)
                    o = PS[:, 6 + par, 0:D]
                    if l != 2:
                        v.tensor_tensor(X[:, t, :], X[:, t, :], o, ALU.add).then_inc(upd_done, 1)
                    else:
                        v.bn_stats(O6[:, par, :], o)
                        dve.drain()
                        v.bn_aggr(O2[:, par, :], O6[:, par, :]).then_inc(o_chain, 1)
                        dve.wait_ge(o_chain, 3 * t + 1)
                        v.tensor_scalar(OE[:, par, :], O2[:, par, 1:2], LN_EPS, None, ALU.add).then_inc(o_eps, 1)
                        dve.wait_ge(o_rstd, t + 1)
                        v.tensor_scalar(OT[:, par, :], o, O2[:, par, 0:1], OR[:, par, 0:1], ALU.subtract, ALU.mult).then_inc(o_chain, 1)
                        dve.wait_ge(o_chain, 3 * t + 2)
                        v.tensor_tensor(OT[:, par, :], OT[:, par, :], g_out, ALU.mult).then_inc(o_chain, 1)
                        dve.wait_ge(o_chain, 3 * t + 3)
                        v.tensor_tensor(X[:, t, :], X[:, t, :], OT[:, par, :], ALU.add).then_inc(upd_done, 1)
                    dve.wait_ge(upd_done, t0 + t + 1)
                    stats(t)

                x_norm(0, 0)

                def body(t, par):
                    first = isinstance(t, int) and t == 0
                    for hf in range(H):
                        if hf == 0 and not last(t):
                            x_norm(t + 1, 1 - par)
                        shift(t, par, hf)
                        if hf:
                            total(t, par, hf - 1)
                        elif not first:
                            total(t - 1, 1 - par, H - 1)
                            second = isinstance(t, int) and t == 1
                            if not second:
                                update(t - 2, par)
                in_pairs(dve, body)
                total(T - 1, 1, H - 1)
                update(T - 2, 0)
                update(T - 1, 1)

            def front(l):
                t0 = T * l

                def body(t, par):
                    wait(dve, f_xt, t0 + t - 1)
                    v.tensor_scalar(XN[:, par, :], X[:, t, :], SM[:, 0, at(t, 1)], SM[:, 10, at(t, 1)],
                                    ALU.subtract, ALU.mult).then_inc(f_xn, 1)
                in_pairs(dve, body)

            def wide(a):
                return a.unsqueeze(2).to_broadcast([P, T, E])

            def top2(src):
                for k, (val, oh) in enumerate(((13, 1), (14, 2))):
                    link(v.tensor_reduce(SM[:, val, :], src, AX.X, ALU.max))
                    link(tt(RT[:, 3, :, :], src, wide(SM[:, val, :]), ALU.is_equal))
                    link(v.scalar_tensor_tensor(out=RT[:, 3, :, :], in0=RT[:, 3, :, :], scalar=-16.0, in1=iota, op0=ALU.mult, op1=ALU.add))
                    link(v.tensor_reduce(SM[:, 15, :], RT[:, 3, :, :], AX.X, ALU.min))
                    link(tt(RT[:, oh, :, :], RT[:, 3, :, :], wide(SM[:, 15, :]), ALU.is_equal))
                    if k == 0:
                        link(v.scalar_tensor_tensor(out=RT[:, 4, :, :], in0=RT[:, 1, :, :], scalar=-3e38, in1=src, op0=ALU.mult, op1=ALU.add))
                        src = RT[:, 4, :, :]

            def places():
                v.tensor_tensor(RT[:, 5, :, :], RT[:, 1, :, :], RT[:, 2, :, :], ALU.add).then_inc(r_count, 1)
                link(v.memset(RC[:, :, 0:8, :], 0.0))
                dve.wait_ge(r_sums, counts[0] + 1)
                counts[0] += 1
                flat = PS[:, 1, 0:T * E].rearrange("p (t e) -> p t e", e=E)
                link(v.tensor_copy(RC[:, 0, 8:24, :], flat))
                a = 0
                for step in (1, 2, 4, 8):
                    link(tt(RC[:, 1 - a, 8:24, :], RC[:, a, 8:24, :], RC[:, a, 8 - step:24 - step, :], ALU.add))
                    a = 1 - a
                link(tt(RT[:, 7, :, :], PS[:, 0, 0:T * E].rearrange("p (t e) -> p t e", e=E), RC[:, a, 7:23, :], ALU.add))

            counts = [0]

            def router(l):
                z = PS[:, 3, 0:T * E].rearrange("p (t e) -> p t e", e=E)
                dve.wait_ge(f_gate, T * (l + 1))
                dve.wait_ge(fw_in[l], 16)
                if l == 0:
                    dve.wait_ge(r_exp, 1)
                    link(ts(RT[:, 0, :, :], RT[:, 0, :, :], 1.0, None, ALU.add))
                    link(v.memset(S9[:, :, E:EB], 1.0))
                    link(v.memset(W9[:, :, E:EB], 1.0))
                    link(v.reciprocal(S9[:, :, 0:E], RT[:, 0, :, :]))
                    link(tt(RT[:, 6, :, :], S9[:, :, 0:E], FA[:, F0["bias"]:F0["bias"] + T * E].rearrange("p (t e) -> p t e", e=E), ALU.add))
                    top2(RT[:, 6, :, :])
                    link(tt(RT[:, 1, :, :], RT[:, 1, :, :], RT[:, 2, :, :], ALU.add))
                    link(tt(RT[:, 1, :, :], RT[:, 1, :, :], S9[:, :, 0:E], ALU.mult))
                    v.tensor_tensor(W9[:, :, 0:E], RT[:, 1, :, :], S9[:, :, 0:E], ALU.mult).then_inc(r_done, 1)
                if l == 1:
                    link(tt(RT[:, 0, :, :], z, wide(SM[:, 11, :]), ALU.mult))
                    link(v.tensor_reduce(SM[:, 1, :], RT[:, 0, :, :], AX.X, ALU.max))
                    v.tensor_tensor(RT[:, 0, :, :], RT[:, 0, :, :], wide(SM[:, 1, :]), ALU.subtract).then_inc(r_logit, 1)
                    dve.wait_ge(r_exp, 2)
                    link(v.tensor_reduce(SM[:, 1, :], RT[:, 0, :, :], AX.X, ALU.add))
                    link(v.reciprocal(SM[:, 2, :], SM[:, 1, :]))
                    link(tt(RT[:, 6, :, :], RT[:, 0, :, :], wide(SM[:, 2, :]), ALU.mult))
                    top2(RT[:, 6, :, :])
                    places()
                    link(ts(RT[:, 8, :, :], RT[:, 7, :, :], float(CAP1), None, ALU.is_ge))
                    link(tt(RT[:, 8, :, :], RT[:, 8, :, :], RT[:, 5, :, :], ALU.mult))
                    link(v.tensor_reduce(SM[:, 3, :], RT[:, 8, :, :], AX.X, ALU.max))
                    link(ts(SM[:, 4, :], SM[:, 3, :], -1.0, 1.0, ALU.mult, ALU.add))
                    link(tt(RT[:, 6, :, :], RT[:, 6, :, :], RT[:, 5, :, :], ALU.mult))
                    link(tt(W9[:, :, 0:E], RT[:, 6, :, :], wide(SM[:, 4, :]), ALU.mult))
                    link(v.tensor_copy(W9[:, :, E], SM[:, 3, :]))
                    link(v.tensor_reduce(SM[:, 5, :], W9[:, :, 0:E], AX.X, ALU.add))
                    link(ts(SM[:, 5, :], SM[:, 5, :], 1.0, None, ALU.add))
                    link(tt(SM[:, 5, :], SM[:, 5, :], SM[:, 8, :], ALU.mult))
                    for e in range(EB):
                        n = 2 * P if e < E else P // 2
                        for o in (F1["g"], F1["u"]):
                            w = FB[:, o + e * 2 * P:o + e * 2 * P + n]
                            op = v.tensor_scalar(w, w, FB[:, F1["norm"] + e:F1["norm"] + e + 1], None, ALU.mult)
                    op.then_inc(wn_done, 1)
                    dve.wait_ge(wn_done, 1)
                    v.tensor_copy(SM[:, 1, :], SM[:, 5, :]).then_inc(r_done, 1)
                    dve.wait_ge(r_done, 2)

                    def residual(t, par):
                        v.tensor_scalar(XN[:, par, :], X[:, t, :], SM[:, 0, at(t, 1)], SM[:, 1, at(t, 1)],
                                        ALU.subtract, ALU.mult).then_inc(xres_chain, 1)
                        dve.wait_ge(xres_chain, 2 * t + 1)
                        v.tensor_tensor(X[:, t, :], X[:, t, :], XN[:, par, :], ALU.add).then_inc(xres_chain, 1)
                    in_pairs(dve, residual)
                    dve.wait_ge(xres_chain, 2 * T)
                if l == 2:
                    v.tensor_tensor(RT[:, 0, :, :], z, FA[:, F2["bias"]:F2["bias"] + T * E].rearrange("p (t e) -> p t e", e=E), ALU.add).then_inc(r_logit, 1)
                    dve.wait_ge(r_exp, 3)
                    link(ts(RT[:, 0, :, :], RT[:, 0, :, :], 1.0, None, ALU.add))
                    link(v.reciprocal(RT[:, 7, :, :], RT[:, 0, :, :]))
                    top2(RT[:, 7, :, :])
                    link(tt(SM[:, 1, :], SM[:, 13, :], SM[:, 14, :], ALU.add))
                    link(ts(SM[:, 1, :], SM[:, 1, :], 1e-8, None, ALU.add))
                    link(v.reciprocal(SM[:, 2, :], SM[:, 1, :]))
                    link(tt(RT[:, 6, :, :], RT[:, 1, :, :], RT[:, 2, :, :], ALU.add))
                    link(tt(RT[:, 5, :, :], RT[:, 7, :, :], wide(SM[:, 2, :]), ALU.mult))
                    v.tensor_tensor(RT[:, 5, :, :], RT[:, 5, :, :], RT[:, 6, :, :], ALU.mult).then_inc(r_count, 1)
                    dve.wait_ge(r_sums, counts[0] + 1)
                    counts[0] += 1
                    sums = PS[:, 0, 0:2 * T * E].rearrange("p (a t e) -> p a e t", a=2, e=E)
                    for a in range(2):
                        link(v.tensor_reduce(W2[:, a, :], sums[:, a, :, :], AX.X, ALU.add))
                    link(ts(W2[:, 1, :], W2[:, 1, :], 1.0, None, ALU.max))
                    link(v.reciprocal(W2[:, 2, :], W2[:, 1, :]))
                    link(tt(W2[:, 3, :], W2[:, 0, :], W2[:, 2, :], ALU.mult))
                    link(v.memset(W9[:, :, E:EB], 1.0))
                    v.tensor_tensor(W9[:, :, 0:E], RT[:, 6, :, :], W2[:, 3, :].unsqueeze(1).to_broadcast([P, T, E]), ALU.mult).then_inc(r_done, 1)
                if l == 3:
                    link(ts(RT[:, 0, :, :], z, CLAMP, -CLAMP, ALU.min, ALU.max))
                    top2(RT[:, 0, :, :])
                    v.tensor_tensor(SM[:, 12, :], SM[:, 14, :], SM[:, 13, :], ALU.subtract).then_inc(r_logit, 1)
                    dve.wait_ge(r_exp, 4)
                    link(ts(SM[:, 1, :], SM[:, 12, :], 1.0, 1e-12, ALU.add, ALU.add))
                    link(v.reciprocal(SM[:, 2, :], SM[:, 1, :]))
                    link(tt(SM[:, 3, :], SM[:, 12, :], SM[:, 2, :], ALU.mult))
                    places()
                    link(ts(RT[:, 8, :, :], RT[:, 7, :, :], float(CAP3), None, ALU.is_lt))
                    link(tt(RT[:, 1, :, :], RT[:, 1, :, :], wide(SM[:, 2, :]), ALU.mult))
                    link(tt(RT[:, 2, :, :], RT[:, 2, :, :], wide(SM[:, 3, :]), ALU.mult))
                    link(tt(RT[:, 1, :, :], RT[:, 1, :, :], RT[:, 2, :, :], ALU.add))
                    v.tensor_tensor(W9[:, :, 0:E], RT[:, 1, :, :], RT[:, 8, :, :], ALU.mult).then_inc(r_done, 1)

            def experts0():
                dve.wait_ge(r_done, 1)

                def gated(t, par, g):
                    n = t * 3 + g
                    q = (par * 3 + g) % 2
                    dve.wait_ge(t_act, n + 1)
                    wait(dve, t_tr, n - 1)
                    for k in range(3):
                        e = g * 3 + k
                        op = v.scalar_tensor_tensor(out=HS[:, q, k * P:(k + 1) * P], in0=PS[:, 2 * q + 1, k * P:(k + 1) * P],
                                                    scalar=W9[:, t, e:e + 1], in1=GS[:, q, k * P:(k + 1) * P], op0=ALU.mult, op1=ALU.mult)
                    op.then_inc(t_mul, 1)

                def update(t, par):
                    dve.wait_ge(t_out, t + 1)
                    v.tensor_tensor(X[:, t, :], X[:, t, :], PS[:, 6 + par, 0:D], ALU.add).then_inc(t_upd, 1)
                    dve.wait_ge(t_upd, t + 1)
                    stats(t)

                def body(t, par):
                    for g in range(3):
                        gated(t, par, g)
                        if g == 1 and not (isinstance(t, int) and t == 0):
                            update(t - 1, 1 - par)
                in_pairs(dve, body)
                update(T - 1, 1)

            def experts(l):
                plan = PLANS[l]
                n0, q0 = UP0[l], DOWN0[l]
                N, Q = len(plan), SUMS[l]
                dve.wait_ge(r_done, l + 1)

                def gated(b, n):
                    m = plan[n][1]
                    dve.wait_ge(e_act, n0 + b * N + n + 1)
                    v.tensor_tensor(HS[0:m, n % 2, :], PS[0:m, 2 + n % 2, :], GS[0:m, n % 2, :], ALU.mult).then_inc(e_mul, 1)

                def weigh(b, e, n_e):
                    dve.wait_ge(e_down, q0 + b * Q + e + 1)
                    for j in range(TPB):
                        t = b * TPB + j
                        op = v.scalar_tensor_tensor(out=X[:, t, :], in0=PS[:, 4 + e % 2, j * P:(j + 1) * P],
                                                    scalar=W9[:, t, e:e + 1], in1=X[:, t, :], op0=ALU.mult, op1=ALU.add)
                    op.then_inc(e_acc, 1)
                    dve.wait_ge(e_acc, q0 + b * Q + e + 1)

                with dve.Fori(0, B) as b:
                    for n in range(N):
                        gated(b, n)
                        if n:
                            for e, lo, hi, start, stop in plan[n - 1][2]:
                                if stop:
                                    weigh(b, e, n)
                    for e, lo, hi, start, stop in plan[N - 1][2]:
                        if stop:
                            weigh(b, e, N)
                    if l < 3:
                        for j in range(TPB):
                            stats(b * TPB + j)

            dve.wait_ge(const_in, 64)
            v.memset(ONEB[:, :], 1.0)
            link(ts(MKF[:, :], MK[:, :], -NEG, NEG, ALU.mult, ALU.add))
            for h in range(8):
                op = v.tensor_copy(MB[:, :, h, :], MKF[:, :].rearrange("p (b k) -> p b k", k=KMAX))
            op.then_inc(mask_made, 1)
            dve.wait_ge(x_in, 16)
            with dve.Fori(0, T) as t:
                stats(t)
            for l in range(4):
                deviations(2 * l)
                attention(l)
                deviations(2 * l + 1)
                front(l)
                if l == 2:
                    for b in range(B):
                        if b == 0:
                            dve.wait_ge(p_ev, PREP0[3] + 1)
                        v.scalar_tensor_tensor(out=gview(3)[:, b, :, :], in0=KV[:, 0, b * NK:(b + 1) * NK].unsqueeze(1).to_broadcast([P, 16, NK]),
                                               scalar=float(SCALE[3]), in1=headmask.unsqueeze(2).to_broadcast([P, 16, NK]),
                                               op0=ALU.mult, op1=ALU.mult).then_inc(gk_done, 1)
                router(l)
                if l == 0:
                    experts0()
                else:
                    experts(l)


def kernel(**inputs):
    import concourse.bacc as bacc
    from concourse.bass_utils import run_bass_kernel_spmd

    a = {k: np.asarray(v) for k, v in inputs.items()}

    def cols(w):
        o = np.zeros((P, w.shape[1]), w.dtype)
        o[:w.shape[0]] = w
        return o

    def chunks(w):
        return w.reshape(-1, P, w.shape[1]).transpose(1, 0, 2).reshape(P, -1)

    def everywhere(r):
        return np.broadcast_to(r.reshape(1, -1), (P, r.size))

    def attention_weights(wq, wk, wv, wo):
        return np.concatenate([cols(wk), cols(wv), chunks(wq.T), chunks(wo)], 1)

    l2k, l2v = np.split(a["L2_xattn_Wkv"], 2, axis=1)
    aw = [
        attention_weights(a["L0_xattn_Wq"], a["L0_xattn_Wk"], a["L0_xattn_Wv"], a["L0_xattn_Wo"]),
        attention_weights(a["L1_xattn_Wq"], a["L1_xattn_Wk"], a["L1_xattn_Wv"], a["L1_xattn_Wo"]),
        attention_weights(a["L2_xattn_Wq"], l2k, l2v, a["L2_xattn_Wout"]),
        np.concatenate([cols(a["L3_xattn_wk"].T), cols(a["L3_xattn_wv"].T), a["L3_xattn_wq"].T, a["L3_xattn_wo"].T], 1),
    ]

    w1 = np.concatenate([a["L0_ffn_w1"], a["L0_ffn_sw1"][None]]).transpose(2, 0, 1)
    w3 = np.concatenate([a["L0_ffn_w3"], a["L0_ffn_sw3"][None]]).transpose(2, 0, 1)
    w2 = np.concatenate([a["L0_ffn_w2"], a["L0_ffn_sw2"][None]]).transpose(2, 0, 1)
    up = np.stack([w1.reshape(P, 3, 384), w3.reshape(P, 3, 384)], 2).reshape(P, -1)
    fw0 = [a["L0_ffn_gate_w"].T, everywhere(np.tile(a["L0_ffn_expert_bias"], T)), up, w2.reshape(P, -1)]

    def padded(w):
        return np.concatenate([w, np.zeros((P, P - w.shape[1]), w.dtype)], 1)

    fw1 = [a["L1_ffn_Wr"], a["L1_ffn_norm_w"].T, a["L1_ffn_f_norm"][:, None],
           a["L1_ffn_Wg"].transpose(1, 0, 2).reshape(P, -1), padded(a["L1_ffn_fWg"]),
           a["L1_ffn_Wu"].transpose(1, 0, 2).reshape(P, -1), padded(a["L1_ffn_fWu"]),
           chunks(a["L1_ffn_Wd"].reshape(-1, D)), cols(a["L1_ffn_fWd"])]
    fw2 = [a["L2_ffn_gate_w"].T, everywhere(np.tile(a["L2_ffn_lb_bias"], T)),
           a["L2_ffn_expert_gate_w"].transpose(2, 0, 1).reshape(P, -1), a["L2_ffn_shared_gate_w"].T,
           a["L2_ffn_expert_up_w"].transpose(2, 0, 1).reshape(P, -1), a["L2_ffn_shared_up_w"].T,
           chunks(a["L2_ffn_expert_down_w"].transpose(0, 2, 1).reshape(-1, D)), a["L2_ffn_shared_down_w"].T]
    w12 = a["L3_ffn_w12"].transpose(2, 0, 1)
    fw3 = [a["L3_ffn_router_w"].T, a["L3_ffn_ln_gamma"][:, None], a["L3_ffn_ln_beta"][:, None],
           w12[:, :, :512].reshape(P, -1), w12[:, :, 512:].reshape(P, -1),
           chunks(a["L3_ffn_w3"].transpose(0, 2, 1).reshape(-1, D))]
    fw = [np.concatenate(f, 1) for f in (fw0, fw1, fw2, fw3)]

    i = np.arange(P)
    f = np.float32
    null = a["L2_xattn_null_kv"]
    consts = np.concatenate([
        np.eye(P, dtype=f), np.ones((P, P), f), (i[:, None] < i[None, :]).astype(f),
        np.broadcast_to(np.tile(np.arange(E, dtype=f), T), (P, P)),
        (i[:, None] // 8 == np.arange(16)[None, :]).astype(f), everywhere(a["L2_xattn_g_out"]),
        a["L2_xattn_g_norm"][:, None], np.concatenate([null[0], null[0]])[:, None], np.concatenate([null[1], null[1]])[:, None],
        a["L3_xattn_bq"][:, None], a["L3_xattn_bk"][:, None], a["L3_xattn_bv"][:, None]], 1)
    rows = np.concatenate([a["L0_xattn_bo"], a["L1_xattn_bo"], a["L3_xattn_bo"]])[None]
    m = a["mask_BxS2_bf1"]
    mask = np.concatenate([np.ones((B, 1), m.dtype), m], 1).reshape(1, -1).view(np.uint8)

    data = {"x": a["x"].reshape(NTOK, D), "ctxT": a["ctx_768"].reshape(B * NK, CD).T, "mask": mask,
            "consts": consts, "rows": rows}
    data.update({f"aw{l}": w for l, w in enumerate(aw)})
    data.update({f"fw{l}": w for l, w in enumerate(fw)})

    nc = bacc.Bacc("TRN2", target_bir_lowering=False, num_devices=1)
    arrays, aps = {}, {}
    for name, v in data.items():
        v = np.ascontiguousarray(v)
        arrays[f"in_{name}"] = v
        aps[name] = nc.dram_tensor(f"in_{name}", v.shape, mybir.dt.from_np(v.dtype), kind="ExternalInput").ap()
    out = nc.dram_tensor("out", (NTOK, D), F32, kind="ExternalOutput").ap()
    fused_decoder_kernel(nc, aps["x"], aps["ctxT"], aps["mask"], aps["consts"], aps["rows"],
                         [aps[f"aw{l}"] for l in range(4)], [aps[f"fw{l}"] for l in range(4)], out)
    r = run_bass_kernel_spmd(nc, [arrays], core_ids=[0])
    return r.results[0]["out"].reshape(B, S, D)
```

```python
from contextlib import ExitStack

import numpy as np

import concourse.bass as bass
from concourse import mybir

F32 = mybir.dt.float32
BF16 = mybir.dt.bfloat16
U8 = mybir.dt.uint8
I32 = mybir.dt.int32
ALU = mybir.AluOpType
ACT = mybir.ActivationFunctionType
AX = mybir.AxisListType

P = 128
B, S, D, CD, NK = 4, 512, 128, 96, 77
T = B * S // P
TPB = S // P
E = 8
NTOK = B * S

LN_EPS = 1e-5
RMS_EPS = 1e-6
NEG = -3.3e38
CAP = {1: 512, 3: 640}
CLAMP = 10000.0

HEADS = [16, 8, 16, 16]
KEYS = [NK, NK, NK + 1, NK]
PER = [2, 1, 2, 16]
CHUNKS = [8, 8, 8, 1]
HALVES = [2, 1, 2, 2]
LAG = [2, 3, 2, 2]
GROUP = [2, 4, 2, 2]
PEEL = [2, 1, 2, 2]
SCALE = [64 ** -0.5, 128 ** -0.5, 64 ** -0.5, 8 ** -0.5]
KMAX = NK + 1
UNIT0 = [T * sum(HALVES[:l]) for l in range(4)]
BLOCKS0 = [B * sum(HALVES[:l]) for l in range(4)]
PADV = 128

EB = E + 1
F0 = dict(gate=0, bias=8, up=136, down=136 + EB * 256)
F0["end"] = F0["down"] + EB * 128
F1 = dict(gate=0, norm=8, g=17, u=17 + 128, down=17 + 2 * 128)
F1["end"] = F1["down"] + 128
F2 = dict(gate=0, bias=8, g=136, u=136 + 5 * 128, down=136 + 10 * 128)
F2["end"] = F2["down"] + 5 * 128
F3 = dict(gate=0, gamma=8, beta=9, end=10)
FA_COLS = max(F0["end"], F2["end"])
C_ID, C_ONE, C_TRI, C_IOTA, C_BM, C_GO = 0, 128, 256, 384, 512, 528
C_COL = 528 + 128
C_SPARE = C_COL + 6
C_END = C_SPARE + 2 * T


PLAN2 = [(c, [(2 * c, 0, 64), (2 * c + 1, 64, P)]) for c in range(4)] + [(4, [(E, 0, P)])]
HID = {1: 2, 3: 4}
GROUPS = {1: [4], 3: [3, 2]}
SLOT_TILES = {l: CAP[l] // P for l in (1, 3)}
STEPS = {l: HID[l] * len(GROUPS[l]) for l in (1, 3)}
WCOLS = {l: 3 * HID[l] * P for l in (1, 3)}
ROW = D + 1
ROUND = {1: 0, 3: 1}
UP2, DOWN2 = B + E * STEPS[1], B
SLOT0 = {1: B, 3: UP2 + B * len(PLAN2)}
GROUP0 = {1: 0, 3: E * len(GROUPS[1])}
TWICE = (3, 4, 7)


def fused_decoder_kernel(nc, x, ctxT, mask, consts, rows, aw, fw, ew, slots, made, out):
    with ExitStack() as ctx:
        def sb(name, shape, dt=F32):
            return ctx.enter_context(nc.sbuf_tensor(name, shape, dt))

        def sem(name):
            return ctx.enter_context(nc.semaphore(name))

        X = sb("X", [P, T, D])
        XTA = sb("XTA", [P, NTOK])
        AW = sb("AW", [P, 4096])
        G = sb("G", [P, B * 16 * KMAX])
        VW = sb("VW", [P, B, 10, D])
        KV = sb("KV", [P, 8, B * NK + 1])
        VB = sb("VB", [P, 8, 2 * PADV + 2 * KMAX])
        FA = sb("FA", [P, FA_COLS])
        FB = sb("FB", [P, F1["end"]])
        FC = sb("FC", [P, F3["end"]])
        WS = sb("WS", [P, 2, WCOLS[3]])
        XS = sb("XS", [P, 2, SLOT_TILES[3], ROW])
        XTS = sb("XTS", [P, 2, CAP[3]])
        YS = sb("YS", [P, 4 * 3, D])
        RW = sb("RW", [P, 2, T, ROW])
        RK = sb("RK", [P, 4, 2, T])
        IX = sb("IX", [P, 2 * T], I32)
        ID = sb("ID", [P, 2, SLOT_TILES[3]], I32)
        CT = sb("CT", [CD, B * NK])
        CN = sb("CN", [P, C_END])
        BO = sb("BO", [1, 3 * 128])
        MK = sb("MK", [1, B * KMAX], U8)
        MB = sb("MB", [1, B, 8, KMAX], BF16)
        MKF = sb("MKF", [1, B * KMAX])
        gcol = sb("gcol", [P, 1])
        ONEB = sb("ONEB", [1, P], BF16)
        BMS = sb("BMS", [P, 16])
        NH = sb("NH", [P, T])
        ST = sb("ST", [P, T, 6])
        SM = sb("SM", [P, 16, T])
        XN = sb("XN", [P, 2, D])
        XTB = sb("XTB", [P, 2, P])
        QTB = sb("QTB", [P, 2, P])
        PR = sb("PR", [P, 4, 8 * KMAX])
        PT = sb("PT", [P, 5, P])
        MX = sb("MX", [P, 2, 8])
        RS = sb("RS", [P, 2, 8])
        RI = sb("RI", [P, 2, 8])
        OT = sb("OT", [P, 2, D])
        O6 = sb("O6", [P, 2, 6])
        O2 = sb("O2", [P, 2, 2])
        OR = sb("OR", [P, 2, 1])
        OE = sb("OE", [P, 2, 1])
        GS = sb("GS", [P, 2, 512])
        HS = sb("HS", [P, 2, 512])
        RT = sb("RT", [P, 12, T, E])
        RC = sb("RC", [P, 2, 24, E])
        W9 = sb("W9", [P, T, EB])
        S9 = sb("S9", [P, T, EB])
        W2 = sb("W2", [P, 4, E])
        PS = ctx.enter_context(nc.psum_tensor("PS", [P, 8, 512], F32))

        ident = CN[:, C_ID:C_ID + P]
        ones = CN[:, C_ONE:C_ONE + P]
        before = CN[:, C_TRI:C_TRI + P]
        iota = CN[:, C_IOTA:C_IOTA + T * E].rearrange("p (t e) -> p t e", e=E)
        headmask = CN[:, C_BM:C_BM + 16]
        g_out = CN[:, C_GO:C_GO + P]
        g_norm, null_k, null_v, bq, bk, bv = (CN[:, C_COL + i:C_COL + i + 1] for i in range(6))
        spare = CN[:, C_SPARE:C_SPARE + 2 * T].rearrange("p (k t) -> p k t", k=2)
        gamma, beta = (FC[:, F3[n]:F3[n] + 1] for n in ("gamma", "beta"))

        x_in, const_in, stored = sem("x_in"), sem("const_in"), sem("stored")
        aw_in = [sem(f"aw_in{l}") for l in range(4)]
        fw_in = [sem(f"fw_in{l}") for l in range(4)]
        zeroed, mask_made, nh_made = sem("zeroed"), sem("mask_made"), sem("nh_made")
        stats_done, var_ready, pow_ready = sem("stats_done"), sem("var_ready"), sem("pow_ready")
        p_mm, p_ev, vb_ready = sem("p_mm"), sem("p_ev"), sem("vb_ready")
        vb_zero, null_in, gk_done = sem("vb_zero"), sem("null_in"), sem("gk_done")
        xn_ready, xt_ready, xtb_ready = sem("xn_ready"), sem("xt_ready"), sem("xtb_ready")
        q_ready, qtb_ready = sem("q_ready"), sem("qtb_ready")
        score_ready, max_ready, sub_ready, exp_ready = sem("score_ready"), sem("max_ready"), sem("sub_ready"), sem("exp_ready")
        sum_ready, inv_ready, prob_ready = sem("sum_ready"), sem("inv_ready"), sem("prob_ready")
        pt_ready, pte_ready, out_ready, upd_done = sem("pt_ready"), sem("pte_ready"), sem("out_ready"), sem("upd_done")
        o_chain, o_eps, o_rstd = sem("o_chain"), sem("o_eps"), sem("o_rstd")
        zero_made, slots_clear, r_idx, scattered = sem("zero_made"), sem("slots_clear"), sem("r_idx"), sem("scattered")
        ws_in, xs_in, y_out = ([sem(f"{n}{k}") for k in range(2)] for n in ("ws_in", "xs_in", "y_out"))
        xs_blank, ids_set, ids_ready, rows_copied = sem("xs_blank"), sem("ids_set"), sem("ids_ready"), sem("rows_copied")
        xs_turned, xts_ready, y_made, ys_ready = sem("xs_turned"), sem("xts_ready"), sem("y_made"), sem("ys_ready")
        y_back = [sem(f"y_back{b}") for b in range(B)]
        x_acc = sem("x_acc")
        f_xn, f_xt, f_xta, f_gate = sem("f_xn"), sem("f_xt"), sem("f_xta"), sem("f_gate")
        r_chain, r_logit, r_exp, r_count, r_sums, r_done, wn_done = (
            sem("r_chain"), sem("r_logit"), sem("r_exp"), sem("r_count"), sem("r_sums"), sem("r_done"), sem("wn_done"))
        e_up, e_act, e_mul, e_down, e_acc = sem("e_up"), sem("e_act"), sem("e_mul"), sem("e_down"), sem("e_acc")
        t_in, t_up, t_act, t_mul, t_tr, t_ev, t_out, t_upd = (sem(n) for n in (
            "t_in", "t_up", "t_act", "t_mul", "t_tr", "t_ev", "t_out", "t_upd"))
        xres_done, bms_made = sem("xres_done"), sem("bms_made")

        block = ctx.enter_context(nc.Block())

        VB3 = VB[:, :, :].rearrange("p j n -> p (j n)")

        def gview(l):
            return G[:, 0:B * HEADS[l] * KEYS[l]].rearrange("p (b h k) -> p b h k", b=B, k=KEYS[l])

        def prview(l, i):
            return PR[:, i, 0:8 * KEYS[l]].rearrange("p (h k) -> p h k", k=KEYS[l])

        def wait(eng, s, v):
            if isinstance(v, int) and v <= 0:
                return
            eng.wait_ge(s, v)

        def wait_from(eng, s, base, v):
            if not isinstance(v, int) or v > 0:
                eng.wait_ge(s, base + v)

        def in_pairs(eng, body):
            body(0, 0)
            body(1, 1)
            with eng.Fori(1, T // 2 - 1) as i:
                body(2 * i, 0)
                body(2 * i + 1, 1)
            body(T - 2, 0)
            body(T - 1, 1)

        def in_groups(eng, l, body):
            n, peel = GROUP[l], PEEL[l]
            for t in range(peel * n):
                body(t, t % n)
            with eng.Fori(peel, T // n - 1) as i:
                for k in range(n):
                    body(n * i + k, k)
            for t in range(T - n, T):
                body(t, t % n)

        def in_expert_pairs(eng, body):
            body(0)
            with eng.Fori(1, E // 2 - 1) as i:
                body(2 * i)
            body(E - 2)

        def output_buffer(l, k, g):
            return 4 * k if l == 1 else 3 * (2 * k + g)

        def outputs_written(l, k, e):
            n = 16 * SLOT_TILES[l]
            done = n * ((e - k) // 2 + 1) if isinstance(e, int) else n // 2 * (e - k + 2)
            return ROUND[l] * 16 * SLOT_TILES[1] * E // 2 + done

        def turn_at(l):
            return max(1, STEPS[l] - 2)

        def steps_of(l):
            return [(g, n, sum(GROUPS[l][:g]), c) for g, n in enumerate(GROUPS[l]) for c in range(HID[l])]

        def at(start, n):
            return slice(start, start + n) if isinstance(start, int) else bass.ds(start, n)

        def before_by(l, ph, n):
            return (ph - n) % GROUP[l]

        def last(t):
            return isinstance(t, int) and t == T - 1

        def batch_of(t):
            return t // TPB

        def windows(l, r, m):
            wide = PER[l] * KEYS[l]
            return [(j, PADV + r - j * wide) for j in range(CHUNKS[l]) if r < (j + 1) * wide and j * wide < r + m]

        def rows_of(l, c):
            return min(P, 8 * KEYS[l] - P * c)

        def prep_counts(l):
            k = CHUNKS[l]
            g = HEADS[l] if l < 3 else 0
            return k, g, k, B * HALVES[l] * 2

        def values_made(l):
            return PREP0[l] + sum(prep_counts(l)[:3])
        PREP0 = [sum(sum(prep_counts(m)) for m in range(l)) for l in range(5)]

        @block.sync
        def _(sp):
            sp.dma_start(CT[:, :], ctxT).then_inc(const_in, 16)
            sp.dma_start(CN[:, :], consts).then_inc(const_in, 16)
            sp.dma_start(BO[:, :], rows).then_inc(const_in, 16)
            sp.dma_start(MK[:, :], mask).then_inc(const_in, 16)
            sp.dma_start(AW[:, 0:2048], aw[0][:, 0:2048]).then_inc(const_in, 16)
            sp.dma_start(AW[:, 2048:4096], aw[0][:, 2048:4096]).then_inc(aw_in[0], 16)
            sp.dma_start(X[:, :, :], x.rearrange("(t p) d -> p t d", p=P)).then_inc(x_in, 16)
            sp.dma_start(FA[:, 0:F0["end"]], fw[0]).then_inc(fw_in[0], 16)
            sp.dma_start(FB[:, :], fw[1]).then_inc(fw_in[1], 16)
            sp.dma_start(FC[:, :], fw[3]).then_inc(fw_in[3], 16)
            sp.wait_ge(zero_made, 1)
            for l in (1, 3):
                n = SLOT_TILES[l]
                sp.dma_start(slots[l].rearrange("(e p j) d -> p e (j d)", p=P, j=n),
                             XS[:, 0, 0:n, :].rearrange("p j d -> p (j d)").unsqueeze(1).to_broadcast([P, E, n * ROW])).then_inc(slots_clear, 16)
                sp.dma_start(made[l].rearrange("(p n) d -> p n d", p=P),
                             XS[:, 0, 0, 0:D].unsqueeze(1).to_broadcast([P, 2 * T, D])).then_inc(slots_clear, 16)

            def expert_weights(l, e, k):
                n = WCOLS[l]
                sp.dma_start(WS[:, k, 0:n], ew[l].rearrange("(e p) n -> p e n", p=P)[:, e, :]).then_inc(ws_in[k], 16)

            def expert_slots(l, e, k):
                n = SLOT_TILES[l]
                sp.dma_start(XS[:, k, 0:n, :].rearrange("p j d -> p (j d)"),
                             slots[l].rearrange("(e p j) d -> p e (j d)", p=P, j=n)[:, e, :]).then_inc(xs_in[k], 16)

            def sparse_experts(l):
                G = len(GROUPS[l])
                g0 = GROUP0[l]
                for k in range(2):
                    expert_weights(l, k, k)
                sp.wait_ge(scattered, 16 * 2 * T * (ROUND[l] + 1))
                for k in range(2):
                    expert_slots(l, k, k)

                def pair(e0):
                    more = not (isinstance(e0, int) and e0 == E - 2)
                    for k in range(2):
                        e = e0 + k
                        if more:
                            sp.wait_ge(xs_turned, E * ROUND[l] + e + 1)
                            sp.wait_ge(ids_ready, E * ROUND[l] + e + 1)
                            expert_slots(l, e + 2, k)
                        if more:
                            sp.wait_ge(y_made, g0 + (e + 1) * G)
                            expert_weights(l, e + 2, k)
                in_expert_pairs(sp, pair)

            def outputs_back(l):
                for q in range(2):
                    sp.wait_ge(y_out[q], 16 * SLOT_TILES[1] * E // 2 + 16 * SLOT_TILES[3] * E // 2 * ROUND[l])
                for b in range(B):
                    for k in range(2):
                        sp.dma_start(RW[:, k, b * TPB:(b + 1) * TPB, 0:D],
                                     made[l].rearrange("(k t p) d -> p k t d", p=P, k=2)[:, k, b * TPB:(b + 1) * TPB, :]).then_inc(y_back[b], 16)

            for l in (1, 2):
                sp.wait_ge(p_mm, PREP0[l])
                sp.dma_start(AW[:, :], aw[l]).then_inc(aw_in[l], 16)
            sp.wait_ge(t_upd, T)
            sp.dma_start(FA[:, 0:F2["end"]], fw[2]).then_inc(fw_in[2], 16)
            sparse_experts(1)
            outputs_back(1)
            sp.wait_ge(p_mm, PREP0[3])
            sp.dma_start(AW[:, 0:512], aw[3]).then_inc(aw_in[3], 16)
            sparse_experts(3)
            outputs_back(3)
            for b in range(B):
                sp.wait_ge(x_acc, 2 * T + 2 * TPB * (b + 1))
                sp.dma_start(out.rearrange("(b t p) d -> p b t d", p=P, t=TPB)[:, b, :, :],
                             X[:, :, :].rearrange("p (b t) d -> p b t d", t=TPB)[:, b, :, :]).then_inc(stored, 16)
            sp.wait_ge(stored, 16 * B)

        @block.tensor
        def _(pe):
            mm = nc.tensor.matmul

            def prep(l, between):
                k, g, v, vw = prep_counts(l)
                n0 = PREP0[l]
                if l == 0:
                    pe.wait_ge(const_in, 80)
                else:
                    pe.wait_ge(aw_in[l], 16)
                slot = [n0]

                def bank():
                    wait(pe, p_ev, slot[0] - 1)
                    slot[0] += 1
                    return 6 + (slot[0] - 1) % 2
                wide = 1024 if l < 3 else P
                for j in range(k):
                    bk_ = bank()
                    mm(PS[:, bk_, 0:B * NK], AW[0:CD, j * P:(j + 1) * P], CT[:, :], start=True, stop=True).then_inc(p_mm, 1)
                between()
                if l == 0:
                    pe.wait_ge(aw_in[0], 16)
                if l < 3:
                    dh = P // PER[l]
                    for h in range(g):
                        j, r = h // PER[l], dh * (h % PER[l])
                        if h == 0:
                            pe.wait_ge(p_ev, n0 + k)
                            if l == 2:
                                pe.wait_ge(null_in, 1)
                        bk_ = bank()
                        n = B * NK + (l == 2)
                        mm(PS[:, bk_, 0:n], AW[r:r + dh, 2048 + j * P:2048 + (j + 1) * P], KV[r:r + dh, j, 0:n],
                           start=True, stop=True).then_inc(p_mm, 1)
                for j in range(v):
                    bk_ = bank()
                    mm(PS[:, bk_, 0:B * NK], AW[0:CD, wide + j * P:wide + (j + 1) * P], CT[:, :], start=True, stop=True).then_inc(p_mm, 1)

            def project_values(l):
                k, g, v, vw = prep_counts(l)
                slot = [PREP0[l] + k + g + v]
                if l == 1:
                    pe.wait_ge(t_upd, T)
                if l == 2:
                    pe.wait_ge(xts_ready, E)

                def bank():
                    pe.wait_ge(p_ev, slot[0] - 1)
                    slot[0] += 1
                    return 6 + (slot[0] - 1) % 2
                w0 = 3072 if l < 3 else 384
                for b in range(B):
                    for hf in range(HALVES[l]):
                        pe.wait_ge(vb_ready, BLOCKS0[l] + b * HALVES[l] + hf + 1)
                        for part in ([0, 1, 2, 3], [4]):
                            bk_ = bank()
                            for c in part:
                                m = rows_of(l, c)
                                r = 8 * KEYS[l] * hf + P * c
                                ws = windows(l, r, m) if l < 3 else [(0, r)]
                                for n, (j, col) in enumerate(ws):
                                    lhs = VB[:, j, col:col + m] if l < 3 else VB3[:, col:col + m]
                                    op = mm(PS[0:m, bk_, (c % 4) * P:(c % 4 + 1) * P], lhs,
                                            AW[:, w0 + j * P:w0 + (j + 1) * P], start=(n == 0), stop=(n == len(ws) - 1))
                            op.then_inc(p_mm, 1)

            def attention(l):
                H, K8 = HALVES[l], 8 * KEYS[l]
                t0, u0 = T * l, UNIT0[l]
                lag = LAG[l]
                pe.wait_ge(p_ev, PREP0[l + 1])
                if l == 2:
                    pe.wait_ge(mask_made, 1)
                if l == 3:
                    pe.wait_ge(gk_done, B)

                def transpose_x(t, ph):
                    par = ph % 2
                    pe.wait_ge(xn_ready, t0 + t + 1)
                    wait(pe, xtb_ready, t0 + t)
                    if l == 3:
                        wait(pe, qtb_ready, t)
                    mm(PS[:, 5, P:2 * P], XN[:, par, :], ident, is_transpose=True, start=True, stop=True).then_inc(xt_ready, 1)

                def query(t, ph):
                    par = ph % 2
                    pe.wait_ge(xtb_ready, t0 + t + 1)
                    mm(PS[:, 5, 2 * P:3 * P], AW[:, 256:384], XTB[:, par, :], start=True, stop=True).then_inc(q_ready, 1)

                def scores(t, ph, hf):
                    u, par = t * H + hf, ph % 2
                    lhs = XTB if l < 3 else QTB
                    if hf == 0:
                        if l < 3:
                            pe.wait_ge(xtb_ready, t0 + t + 1)
                        else:
                            pe.wait_ge(qtb_ready, t + 1)
                    wait(pe, sub_ready, u0 + u - 1)
                    bk_ = 2 * ((ph * H + hf) % 2)
                    flat = PS[:, bk_:bk_ + 2, :].rearrange("p a n -> p (a n)")
                    g = gview(l).rearrange("p b h k -> p b (h k)")[:, batch_of(t), (hf * K8):(hf * K8) + K8]
                    for a, z in ((0, 512), (512, K8)):
                        op = mm(flat[:, a:z], lhs[:, par, :], g[:, a:z], start=True, stop=(l != 2))
                        if l == 2:
                            mb = MB[:, :, :, :].rearrange("p b h k -> p b (h k)")[:, batch_of(t), a:z]
                            op = mm(flat[:, a:z], ONEB[:, :], mb, start=False, stop=True)
                    op.then_inc(score_ready, 1)

                def transpose_p(t, ph, hf, x_next):
                    u = t * H + hf
                    pe.wait_ge(prob_ready, u0 + u + 1)
                    wait(pe, pte_ready, u0 + u)
                    src = PR[:, ph * H + hf, :]
                    for c in range(4):
                        mm(PS[:, 4, c * P:(c + 1) * P], src[:, c * P:(c + 1) * P], ident, is_transpose=True,
                           start=True, stop=True)
                    x_next()
                    m = rows_of(l, 4)
                    mm(PS[0:m, 5, 0:P], src[:, 4 * P:4 * P + m], ident, is_transpose=True,
                       start=True, stop=True).then_inc(pt_ready, 1)

                def project(t, ph, hf):
                    u, par = t * H + hf, ph % 2
                    acc = PS[:, 6 + par, 0:D]
                    if hf == 0:
                        wait_from(pe, stats_done, T * (2 * l + 1), t - 1)
                        if l != 2:
                            mm(acc, CN[0:1, C_ONE:C_ONE + P], BO[0:1, min(l, 2) * P:(min(l, 2) + 1) * P], start=True, stop=False)
                    pe.wait_ge(pte_ready, u0 + u + 1)
                    for c in range(5):
                        m = rows_of(l, c)
                        end = hf == H - 1 and c == 4
                        op = mm(acc, PT[0:m, c, :], VW[0:m, batch_of(t), hf * 5 + c, :],
                                start=(l == 2 and hf == 0 and c == 0), stop=end)
                    if hf == H - 1:
                        op.then_inc(out_ready, 1)

                transpose_x(0, 0)
                if l == 3:
                    query(0, 0)

                def body(t, ph):
                    nxt, old = (ph + 1) % 2, before_by(l, ph, lag)
                    more = not last(t)
                    if isinstance(t, int) and t < lag:
                        if more:
                            transpose_x(t + 1, nxt)
                            if l == 3:
                                query(t + 1, nxt)
                        for hf in range(H):
                            scores(t, ph, hf)
                        return
                    for hf in range(H):
                        def x_next():
                            if not more:
                                pe.wait_ge(xtb_ready, t0 + T)
                                if l == 3:
                                    pe.wait_ge(qtb_ready, T)
                            if more and hf == 0:
                                transpose_x(t + 1, nxt)
                            if more and hf == 1:
                                pe.wait_ge(xtb_ready, t0 + t + 2)
                            if more and l == 3 and hf == 1:
                                query(t + 1, nxt)
                        transpose_p(t - lag, old, hf, x_next)
                        scores(t, ph, hf)
                        project(t - lag, old, hf)

                in_groups(pe, l, body)
                for t in range(T - lag, T):
                    for hf in range(H):
                        transpose_p(t, t % GROUP[l], hf, lambda: pe.wait_ge(xtb_ready, t0 + T))
                        project(t, t % GROUP[l], hf)

            def front(l):
                pe.wait_ge(fw_in[l], 16)
                fbuf = {1: FB, 3: FC}.get(l, FA)

                def gates(b):
                    pe.wait_ge(f_xta, B * l + b + 1)
                    for t in range(b * TPB, (b + 1) * TPB):
                        op = mm(PS[:, 3, t * E:(t + 1) * E], XTA[:, t * P:(t + 1) * P], fbuf[:, 0:E], start=True, stop=True)
                    op.then_inc(f_gate, 1)

                for b in range(B):
                    pe.wait_ge(f_xn, T * l + (b + 1) * TPB)
                    if b >= 2:
                        pe.wait_ge(f_xta, B * l + b - 1)
                    for j in range(TPB):
                        t = b * TPB + j
                        op = mm(PS[:, 4 + b % 2, j * P:(j + 1) * P], RW[:, 0, t, 0:D], ident, is_transpose=True, start=True, stop=True)
                    op.then_inc(f_xt, 1)
                    if b:
                        gates(b - 1)
                gates(B - 1)

            def router(l):
                if l in (1, 3):
                    m = RT[:, 5, :, :].rearrange("p t e -> p (t e)")
                    pe.wait_ge(r_count, l)
                    mm(PS[:, 0, 0:T * E], before, m, start=True, stop=True)
                    mm(PS[:, 1, 0:T * E], ones, m, start=True, stop=True).then_inc(r_sums, 1)
                if l == 2:
                    pe.wait_ge(r_count, 2)
                    m = RT[:, 5:7, :, :].rearrange("p a t e -> p (a t e)")
                    mm(PS[:, 0, 0:2 * T * E], ones, m, start=True, stop=True).then_inc(r_sums, 1)

            def experts0():
                pe.wait_ge(p_ev, values_made(1))
                pe.wait_ge(r_done, 1)

                def up(t, par, g):
                    n = t * 3 + g
                    if g == 0:
                        pe.wait_ge(t_in, t + 1)
                    wait(pe, t_mul, n - 1)
                    q = (par * 3 + g) % 2
                    mm(PS[:, 2 * q, 0:384], XTB[:, par, :], FA[:, F0["up"] + g * 768:F0["up"] + g * 768 + 384], start=True, stop=True)
                    mm(PS[:, 2 * q + 1, 0:384], XTB[:, par, :], FA[:, F0["up"] + g * 768 + 384:F0["up"] + g * 768 + 768],
                       start=True, stop=True).then_inc(t_up, 1)

                def turn(t, par, g):
                    n = t * 3 + g
                    q = (par * 3 + g) % 2
                    pe.wait_ge(t_mul, n + 1)
                    wait(pe, t_ev, n)
                    for k in range(3):
                        op = mm(PS[:, 4, k * P:(k + 1) * P], HS[:, q, k * P:(k + 1) * P], ident, is_transpose=True, start=True, stop=True)
                    op.then_inc(t_tr, 1)

                def down(t, par, g):
                    n = t * 3 + g
                    if g == 0:
                            wait_from(pe, stats_done, 2 * T, t - 1)
                    pe.wait_ge(t_ev, n + 1)
                    for k in range(3):
                        e = g * 3 + k
                        op = mm(PS[:, 6 + par, 0:D], PT[:, k, :], FA[:, F0["down"] + e * P:F0["down"] + (e + 1) * P],
                                start=(e == 0), stop=(e == EB - 1))
                    if g == 2:
                        op.then_inc(t_out, 1)

                def before_by_two(t, par, g):
                    return (t, par, 0) if g == 2 else (t - 1, 1 - par, g + 1)

                def body(t, par):
                    for g in range(3):
                        late = not (isinstance(t, int) and t == 0 and g < 2)
                        if late:
                            turn(*before_by_two(t, par, g))
                        up(t, par, g)
                        if late:
                            down(*before_by_two(t, par, g))
                in_pairs(pe, body)
                for g in (1, 2):
                    turn(T - 1, 1, g)
                    down(T - 1, 1, g)

            def fallback():
                pe.wait_ge(f_xta, B * 2)
                pe.wait_ge(r_done, 2)
                pe.wait_ge(wn_done, 2)

                def down(b):
                    pe.wait_ge(e_mul, b + 1)
                    wait(pe, e_acc, b - 1)
                    for j in range(TPB):
                        op = mm(PS[:, 4 + b % 2, j * P:(j + 1) * P], HS[:, b % 2, j * P:(j + 1) * P],
                                FB[:, F1["down"]:F1["down"] + P], start=(j == 0), stop=True, skip_group_check=True)
                    op.then_inc(e_down, 1)

                for b in range(B):
                    wait(pe, e_mul, b - 1)
                    rhs = XTA[:, b * S:(b + 1) * S]
                    mm(PS[:, b % 2, :], FB[:, F1["g"]:F1["g"] + P], rhs, start=True, stop=True)
                    mm(PS[:, 2 + b % 2, :], FB[:, F1["u"]:F1["u"] + P], rhs, start=True, stop=True).then_inc(e_up, 1)
                    if b:
                        down(b - 1)
                down(B - 1)

            def experts2():
                plan, n0, q0 = PLAN2, UP2, DOWN2
                N, Q = len(plan), EB
                pe.wait_ge(f_xta, B * 3)
                pe.wait_ge(r_done, 3)

                def up(b, n):
                    c = plan[n][0]
                    k = n0 + b * N + n
                    pe.wait_ge(e_mul, k - 1 if n else k)
                    rhs = XTA[:, bass.ds(b * S, S)]
                    bkp = n % 2
                    mm(PS[:, bkp, :], FA[:, F2["g"] + c * P:F2["g"] + (c + 1) * P], rhs, start=True, stop=True)
                    mm(PS[:, 2 + bkp, :], FA[:, F2["u"] + c * P:F2["u"] + (c + 1) * P], rhs, start=True, stop=True).then_inc(e_up, 1)

                def down(b, n):
                    c, downs = plan[n]
                    k = n0 + b * N + n
                    pe.wait_ge(e_mul, k + 1)
                    for e, lo, hi in downs:
                        pe.wait_ge(e_acc, q0 + b * Q + (e - 1 if e else e))
                        for j in range(TPB):
                            op = mm(PS[:, 4 + e % 2, j * P:(j + 1) * P], HS[lo:hi, n % 2, j * P:(j + 1) * P],
                                    FA[lo:hi, F2["down"] + c * P:F2["down"] + (c + 1) * P],
                                    start=(j == 0), stop=True, skip_group_check=True)
                        op.then_inc(e_down, 1)

                with pe.Fori(0, B) as b:
                    for n in range(N):
                        up(b, n)
                        if n:
                            down(b, n - 1)
                    down(b, N - 1)

            def sparse_experts(l):
                G, N, H = len(GROUPS[l]), STEPS[l], HID[l]
                steps, r = steps_of(l), ROUND[l]
                n0, g0 = SLOT0[l], GROUP0[l]
                pe.wait_ge(r_done, l + 1)
                if l == 1:
                    pe.wait_ge(p_ev, values_made(2))

                def turn(e, k):
                    pe.wait_ge(xs_in[k], 16 * (E // 2 * r + (e - k) // 2 + 1) if isinstance(e, int) else 8 * (e - k) + 16 * (E // 2 * r + 1))
                    wait(pe, xts_ready, E * r + e)
                    for g, n in enumerate(GROUPS[l]):
                        for j in range(n):
                            op = mm(PS[:, 6 + (g if G == 2 else k), j * P:(j + 1) * P], XS[:, k, sum(GROUPS[l][:g]) + j, 0:D], ident,
                                    is_transpose=True, start=True, stop=True)
                    op.then_inc(xs_turned, 1)

                def up(e, k, n):
                    g, tiles, before, c = steps[n]
                    q = (k * N + n) % 2
                    if n == 0:
                        pe.wait_ge(xts_ready, E * r + e + 1)
                        pe.wait_ge(ws_in[k], 16 * (E // 2 * r + (e - k) // 2 + 1) if isinstance(e, int) else 8 * (e - k) + 16 * (E // 2 * r + 1))
                    wait(pe, e_mul, n0 + e * N + n - 1)
                    rhs = XTS[:, k, before * P:(before + tiles) * P]
                    mm(PS[:, q, 0:tiles * P], WS[:, k, c * P:(c + 1) * P], rhs, start=True, stop=True)
                    mm(PS[:, 2 + q, 0:tiles * P], WS[:, k, (H + c) * P:(H + c + 1) * P], rhs, start=True, stop=True).then_inc(e_up, 1)

                def down(e, k, n):
                    g, tiles, before, c = steps[n]
                    q = (k * N + n) % 2
                    pe.wait_ge(e_mul, n0 + e * N + n + 1)
                    if c == 0:
                        wait(pe, ys_ready, g0 + e * G + g - 1)
                    for j in range(tiles):
                        op = mm(PS[:, 4 + (k * G + g) % 2, j * P:(j + 1) * P], HS[:, q, j * P:(j + 1) * P],
                                WS[:, k, (2 * H + c) * P:(2 * H + c + 1) * P],
                                start=(c == 0 and j == 0), stop=(c == H - 1), skip_group_check=True)
                    if c == H - 1:
                        op.then_inc(y_made, 1)

                def pair(e0):
                    more = not (isinstance(e0, int) and e0 == E - 2)
                    for k in range(2):
                        for n in range(N):
                            up(e0 + k, k, n)
                            if n == turn_at(l) and (k == 0 or more):
                                turn(e0 + k + 1, 1 - k)
                            if n:
                                down(e0 + k, k, n - 1)
                            elif k:
                                down(e0, 0, N - 1)
                    down(e0 + 1, 1, N - 1)
                turn(0, 0)
                in_expert_pairs(pe, pair)

            prep(0, lambda: None)
            project_values(0)
            for l in range(4):
                attention(l)
                front(l)
                if l < 3:
                    prep(l + 1, lambda: router(l))
                else:
                    router(l)
                if l == 0:
                    experts0()
                if l == 1:
                    fallback()
                if l == 2:
                    experts2()
                if l in (1, 3):
                    sparse_experts(l)
                if l < 3:
                    project_values(l + 1)

        @block.scalar
        def _(act):
            A = nc.scalar.activation

            def prep(l):
                k, g, v, vw = prep_counts(l)
                slot = [PREP0[l]]

                def bank():
                    slot[0] += 1
                    act.wait_ge(p_mm, slot[0])
                    return 6 + (slot[0] - 1) % 2
                bkv = [bk, bv] if l == 3 else [0.0, 0.0]

                def take(dst, src, bias):
                    if l == 3:
                        return A(dst, src, ACT.Identity, bias=bias)
                    return A(dst, src, ACT.Copy)
                if l > 0:
                    act.wait_ge(vb_ready, BLOCKS0[l])
                for j in range(k):
                    b_ = bank()
                    take(KV[:, j, 0:B * NK], PS[:, b_, 0:B * NK], bkv[0]).then_inc(p_ev, 1)
                for h in range(g):
                    b_ = bank()
                    o = 1 if l == 2 else 0
                    dst = gview(l)[:, :, h, o:o + NK]
                    src = PS[:, b_, 0:B * NK].rearrange("p (b k) -> p b k", k=NK)
                    if l == 2:
                        A(dst, src, ACT.Copy, scale=gcol[:, 0:1])
                        A(gview(l)[:, :, h, 0:1], PS[:, b_, B * NK:B * NK + 1].unsqueeze(1).to_broadcast([P, B, 1]),
                          ACT.Copy, scale=gcol[:, 0:1]).then_inc(p_ev, 1)
                    else:
                        A(dst, src, ACT.Copy, scale=float(SCALE[l])).then_inc(p_ev, 1)
                for j in range(v):
                    b_ = bank()
                    take(KV[:, 1 if l == 3 else j, 0:B * NK], PS[:, b_, 0:B * NK], bkv[1]).then_inc(p_ev, 1)

            def project_values(l):
                slot = [values_made(l)]

                def bank():
                    slot[0] += 1
                    act.wait_ge(p_mm, slot[0])
                    return 6 + (slot[0] - 1) % 2
                H = HALVES[l]

                def blocks(b, hf):
                    if l == 3:
                        for h in range(8 * hf, 8 * hf + 8):
                            op = A(VB3[:, h * NK:(h + 1) * NK], KV[:, 1, b * NK:(b + 1) * NK], ACT.Copy, scale=headmask[:, h:h + 1])
                    else:
                        J, dh = CHUNKS[l] // H, P // PER[l]
                        for hh in range(PER[l]):
                            r, c = dh * hh, PADV + hh * KEYS[l] + (l == 2)
                            op = A(VB[r:r + dh, hf * J:(hf + 1) * J, c:c + NK], KV[r:r + dh, hf * J:(hf + 1) * J, b * NK:(b + 1) * NK], ACT.Copy)
                    op.then_inc(vb_ready, 1)

                if l < 3:
                    act.wait_ge(vb_zero, l + 1)
                if l == 2:
                    act.wait_ge(null_in, 3)
                act.wait_ge(p_ev, values_made(l))
                for hf in range(H):
                    blocks(0, hf)
                for b in range(B):
                    for hf in range(H):
                        b_ = bank()
                        A(VW[:, b, hf * 5:hf * 5 + 4, :], PS[:, b_, :].rearrange("p (c d) -> p c d", d=D), ACT.Copy).then_inc(p_ev, 1)
                        b_ = bank()
                        m = rows_of(l, 4)
                        if b < B - 1 and (l < 3 or hf == H - 1):
                            for half in ([hf] if l < 3 else range(H)):
                                blocks(b + 1, half)
                        A(VW[0:m, b, hf * 5 + 4, :], PS[0:m, b_, 0:D], ACT.Copy).then_inc(p_ev, 1)

            def attention(l):
                H = HALVES[l]
                t0, u0 = T * l, UNIT0[l]

                def x_out(t, par):
                    act.wait_ge(xt_ready, t0 + t + 1)
                    if l < 3:
                        wait(act, score_ready, u0 + (t - 1) * H)
                    else:
                        wait(act, q_ready, t - 1)
                    A(XTB[:, par, :], PS[:, 5, P:2 * P], ACT.Copy).then_inc(xtb_ready, 1)

                def q_out(t, par):
                    act.wait_ge(q_ready, t + 1)
                    wait(act, score_ready, u0 + (t - 1) * H)
                    A(QTB[:, par, :], PS[:, 5, 2 * P:3 * P], ACT.Identity, bias=bq).then_inc(qtb_ready, 1)

                def p_out(t, hf):
                    act.wait_ge(pt_ready, u0 + t * H + hf + 1)
                    A(PT[:, 0:4, :], PS[:, 4, :].rearrange("p (c n) -> p c n", n=P), ACT.Copy)
                    m = rows_of(l, 4)
                    A(PT[0:m, 4, :], PS[0:m, 5, 0:P], ACT.Copy).then_inc(pte_ready, 1)

                def expo(t, ph, hf):
                    u = t * H + hf
                    act.wait_ge(sub_ready, u0 + u + 1)
                    p = prview(l, ph * H + hf)
                    A(p, p, ACT.Exp).then_inc(exp_ready, 1)

                x_out(0, 0)
                if l == 3:
                    q_out(0, 0)

                lag = LAG[l]

                def body(t, ph):
                    nxt = (ph + 1) % 2
                    first = isinstance(t, int) and t == 0
                    for hf in range(H):
                        if not (isinstance(t, int) and t < lag):
                            p_out(t - lag, hf)
                        if hf == 0 and not last(t):
                            x_out(t + 1, nxt)
                        if l == 3 and (hf == 1 or first) and not last(t) and not (first and hf == 1):
                            q_out(t + 1, nxt)
                        if hf:
                            expo(t, ph, hf - 1)
                        elif not first:
                            expo(t - 1, before_by(l, ph, 1), H - 1)
                in_groups(act, l, body)
                expo(T - 1, GROUP[l] - 1, H - 1)
                for t in range(T - lag, T):
                    for hf in range(H):
                        p_out(t, hf)

            def front(l):
                if l == 3:
                    act.wait_ge(fw_in[3], 16)
                for b in range(B):
                    act.wait_ge(f_xt, B * l + b + 1)
                    dst = XTA[:, b * S:(b + 1) * S]
                    if l == 3:
                        A(dst, PS[:, 4 + b % 2, :], ACT.Identity, bias=beta, scale=gamma).then_inc(f_xta, 1)
                    else:
                        A(dst, PS[:, 4 + b % 2, :], ACT.Copy).then_inc(f_xta, 1)

            def router(l):
                if l == 0:
                    act.wait_ge(f_gate, B)
                    A(RT[:, 0, :, :], PS[:, 3, 0:T * E].rearrange("p (t e) -> p t e", e=E), ACT.Exp, scale=-1.0).then_inc(r_exp, 1)
                else:
                    act.wait_ge(r_logit, l)
                    if l == 3:
                        A(SM[:, 12, :], SM[:, 12, :], ACT.Exp).then_inc(r_exp, 1)
                    else:
                        A(RT[:, 0, :, :], RT[:, 0, :, :], ACT.Exp, scale=(1.0 if l == 1 else -1.0)).then_inc(r_exp, 1)

            def experts0():
                def gate(t, par, g):
                    n = t * 3 + g
                    q = (par * 3 + g) % 2
                    act.wait_ge(t_up, n + 1)
                    wait(act, t_mul, n - 1)
                    for k in range(3):
                        op = A(GS[:, q, k * P:(k + 1) * P], PS[:, 2 * q, k * P:(k + 1) * P], ACT.Silu,
                               scale=S9[:, t, g * 3 + k:g * 3 + k + 1])
                    op.then_inc(t_act, 1)

                def ev(t, par, g):
                    n = t * 3 + g
                    act.wait_ge(t_tr, n + 1)
                    A(PT[:, 0:3, :], PS[:, 4, 0:384].rearrange("p (c n) -> p c n", n=P), ACT.Copy).then_inc(t_ev, 1)

                act.wait_ge(r_done, 1)

                def body(t, par):
                    for g in range(3):
                        if not (isinstance(t, int) and t == 0 and g < 2):
                            ev(*((t, par, 0) if g == 2 else (t - 1, 1 - par, g + 1)))
                        gate(t, par, g)
                in_pairs(act, body)
                ev(T - 1, 1, 1)
                ev(T - 1, 1, 2)

            def fallback():
                for b in range(B):
                    act.wait_ge(e_up, b + 1)
                    wait(act, e_mul, b - 1)
                    A(GS[:, b % 2, :], PS[:, b % 2, :], ACT.Gelu).then_inc(e_act, 1)

            def experts2():
                n0, N = UP2, len(PLAN2)
                with act.Fori(0, B) as b:
                    for n in range(N):
                        act.wait_ge(e_up, n0 + b * N + n + 1)
                        act.wait_ge(e_mul, n0 + b * N + (n - 1 if n else n))
                        A(GS[:, n % 2, :], PS[:, n % 2, :], ACT.Silu).then_inc(e_act, 1)

            def sparse_experts(l):
                G, N = len(GROUPS[l]), STEPS[l]
                steps, r = steps_of(l), ROUND[l]
                n0, g0 = SLOT0[l], GROUP0[l]

                def turned(e, k):
                    act.wait_ge(xs_turned, E * r + e + 1)
                    wait(act, e_up, n0 + (e - 1) * N)
                    for g, tiles in enumerate(GROUPS[l]):
                        before = sum(GROUPS[l][:g])
                        dst = XTS[:, k, before * P:(before + tiles) * P]
                        src = PS[:, 6 + (g if G == 2 else k), 0:tiles * P]
                        if l == 1:
                            op = A(dst, src, ACT.Copy, scale=FB[:, at(F1["norm"] + e, 1)])
                        else:
                            op = A(dst, src, ACT.Identity, bias=beta, scale=gamma)
                    op.then_inc(xts_ready, 1)

                def gate(e, k, n):
                    tiles, q = steps[n][1], (k * N + n) % 2
                    act.wait_ge(e_up, n0 + e * N + n + 1)
                    wait(act, e_mul, n0 + e * N + n - 1)
                    A(GS[:, q, 0:tiles * P], PS[:, q, 0:tiles * P], ACT.Gelu if l == 1 else ACT.Silu).then_inc(e_act, 1)

                def output(e, k, n):
                    g, tiles, before, c = steps[n]
                    if c < HID[l] - 1:
                        return
                    act.wait_ge(y_made, g0 + e * G + g + 1)
                    wait(act, y_out[k], outputs_written(l, k, e - 2))
                    y0 = output_buffer(l, k, g)
                    A(YS[:, y0:y0 + tiles, :], PS[:, 4 + (k * G + g) % 2, 0:tiles * P].rearrange("p (j d) -> p j d", d=D), ACT.Copy).then_inc(ys_ready, 1)

                def pair(e0):
                    more = not (isinstance(e0, int) and e0 == E - 2)
                    for k in range(2):
                        for n in range(N):
                            gate(e0 + k, k, n)
                            if n == turn_at(l) and (k == 0 or more):
                                turned(e0 + k + 1, 1 - k)
                            if n:
                                output(e0 + k, k, n - 1)
                            elif k:
                                output(e0, 0, N - 1)
                    output(e0 + 1, 1, N - 1)
                turned(0, 0)
                in_expert_pairs(act, pair)

            act.wait_ge(const_in, 80)
            A(gcol[:, 0:1], g_norm, ACT.Copy, scale=float(SCALE[2])).then_inc(zeroed, 1)
            act.wait_ge(zeroed, 1)
            prep(0)
            project_values(0)
            for l in range(4):
                attention(l)
                front(l)
                router(l)
                if l < 3:
                    prep(l + 1)
                if l == 0:
                    experts0()
                if l == 1:
                    fallback()
                if l == 2:
                    experts2()
                if l in (1, 3):
                    sparse_experts(l)
                if l < 3:
                    project_values(l + 1)

        @block.gpsimd
        def _(pool):
            g = nc.gpsimd
            def powers(stage):
                pool.wait_ge(var_ready, stage + 1)
                g.tensor_tensor(SM[:, 10, :], SM[:, 6, :], NH[:, :], ALU.pow).then_inc(pow_ready, 1)
                if stage == 3:
                    g.tensor_tensor(SM[:, 8, :], SM[:, 7, :], NH[:, :], ALU.pow).then_inc(pow_ready, 1)

            def prep(l):
                if l < 3:
                    wait(pool, p_ev, PREP0[l])
                    g.memset(VB[:, :, :], 0.0).then_inc(vb_zero, 1)
                    pool.wait_ge(vb_zero, l + 1)
                if l == 2:
                    pool.wait_ge(vb_ready, BLOCKS0[2])
                    g.tensor_copy(KV[:, :, B * NK:B * NK + 1], null_k.unsqueeze(1).to_broadcast([P, 8, 1])).then_inc(null_in, 1)
                    pool.wait_ge(null_in, 1)
                    for hh in range(2):
                        r = 64 * hh
                        c = PADV + hh * KEYS[2]
                        g.tensor_copy(VB[r:r + 64, :, c:c + 1], CN[r:r + 64, C_COL + 2:C_COL + 3].unsqueeze(1).to_broadcast([64, 8, 1])).then_inc(null_in, 1)
                        pool.wait_ge(null_in, 2 + hh)
                if l == 1:
                    pool.wait_ge(fw_in[1], 16)
                    for o in (F1["g"], F1["u"]):
                        w = FB[:, o:o + P]
                        g.tensor_scalar(w, w, FB[:, F1["norm"] + E:F1["norm"] + EB], None, ALU.mult).then_inc(wn_done, 1)
                if l == 3:
                    g.tensor_scalar(BMS[:, :], headmask, float(SCALE[3]), None, ALU.mult).then_inc(bms_made, 1)
                    pool.wait_ge(bms_made, 1)
                    pool.wait_ge(p_ev, PREP0[3] + 1)
                    for b in range(B):
                        g.tensor_tensor(gview(3)[:, b, :, :], KV[:, 0, b * NK:(b + 1) * NK].unsqueeze(1).to_broadcast([P, 16, NK]),
                                        BMS[:, :].unsqueeze(2).to_broadcast([P, 16, NK]), ALU.mult).then_inc(gk_done, 1)

            def attention(l):
                H, lag = HALVES[l], LAG[l]
                u0 = UNIT0[l]

                def normalise(t, ph, hf):
                    u = t * H + hf
                    q = (ph * H + hf) % 2
                    pool.wait_ge(inv_ready, u0 + u + 1)
                    p = prview(l, ph * H + hf)
                    g.tensor_tensor(p, p, RI[:, q, :].unsqueeze(2).to_broadcast([P, 8, KEYS[l]]), ALU.mult).then_inc(prob_ready, 1)

                def o_pow(t, par):
                    pool.wait_ge(o_eps, t + 1)
                    g.tensor_tensor(OR[:, par, :], OE[:, par, :], NH[:, 0:1], ALU.pow).then_inc(o_rstd, 1)

                def body(t, ph):
                    if l == 2 and not (isinstance(t, int) and t <= lag):
                        o_pow(t - lag - 1, (ph + 1) % 2)
                    for hf in range(H):
                        normalise(t, ph, hf)
                in_groups(pool, l, body)
                if l == 2:
                    for t in range(T - lag - 1, T):
                        o_pow(t, t % 2)

            def experts0():
                def body(t, par):
                    wait(pool, t_up, 3 * (t - 1))
                    src = XTA[:, at(t * P, P)]
                    g.tensor_copy(XTB[:, par, :], src).then_inc(t_in, 1)
                pool.wait_ge(f_xta, B)
                in_pairs(pool, body)

            def scatter(l):
                for b in range(B):
                    pool.wait_ge(f_xn, T * l + (b + 1) * TPB)
                    g.tensor_copy(RW[:, 1, b * TPB:(b + 1) * TPB, 0:D], RW[:, 0, b * TPB:(b + 1) * TPB, 0:D]).then_inc(rows_copied, 1)
                pool.wait_ge(slots_clear, 64)
                pool.wait_ge(r_idx, ROUND[l] + 1)
                pool.wait_ge(rows_copied, B * (ROUND[l] + 1))
                for t in range(T):
                    for k in range(2):
                        i = k * T + t
                        g.indirect_dma_start(slots[l], bass.IndirectOffsetOnAxis(ap=IX[:, i:i + 1], axis=0), RW[:, k, t, :], None,
                                             bounds_check=E * CAP[l] - 1, oob_is_err=False).then_inc(scattered, 16)

            def write_outputs(l):
                G, r = len(GROUPS[l]), ROUND[l]

                for e in range(E):
                    k = e % 2
                    pool.wait_ge(ids_ready, E * r + e + 1)
                    for n, tiles in enumerate(GROUPS[l]):
                        pool.wait_ge(ys_ready, GROUP0[l] + e * G + n + 1)
                        for j in range(tiles):
                            i = sum(GROUPS[l][:n]) + j
                            g.indirect_dma_start(made[l], bass.IndirectOffsetOnAxis(ap=ID[:, k, i:i + 1], axis=0),
                                                 YS[:, output_buffer(l, k, n) + j, :], None,
                                                 bounds_check=2 * NTOK - 1, oob_is_err=False).then_inc(y_out[k], 16)

            g.memset(XS[:, 0, :, :], 0.0).then_inc(xs_blank, 1)
            g.memset(NH[:, :], -0.5).then_inc(nh_made, 1)
            pool.wait_ge(nh_made, 1)
            pool.wait_ge(const_in, 80)
            pool.wait_ge(xs_blank, 1)
            g.tensor_scalar(XS[:, 0, :, D], CN[:, C_SPARE:C_SPARE + SLOT_TILES[3]], float(2 * NTOK), None, ALU.add).then_inc(zero_made, 1)
            g.tensor_copy(RW[:, :, :, D], spare).then_inc(ids_set, 1)
            pool.wait_ge(ids_set, 1)
            prep(0)
            for l in range(4):
                powers(2 * l)
                attention(l)
                powers(2 * l + 1)
                if l < 3:
                    prep(l + 1)
                if l == 0:
                    experts0()
                if l in (1, 3):
                    scatter(l)
                    write_outputs(l)

        @block.vector
        def _(dve):
            v = nc.vector
            links = [0]

            def link(op):
                links[0] += 1
                op.then_inc(r_chain, 1)
                dve.wait_ge(r_chain, links[0])

            def tt(o, a, b_, op):
                return v.tensor_tensor(o, a, b_, op)

            def ts(o, a, s1, s2, op0, op1=None):
                return v.tensor_scalar(o, a, s1, s2, op0, op1) if op1 is not None else v.tensor_scalar(o, a, s1, s2, op0)

            def deviations(stage):
                l = stage // 2
                dve.wait_ge(stats_done, T * (stage + 1))
                m0, m1, q0, q1 = (ST[:, :, i] for i in (1, 4, 2, 5))
                link(tt(SM[:, 1, :], m0, m1, ALU.add))
                link(tt(SM[:, 2, :], q0, q1, ALU.add))
                link(tt(SM[:, 3, :], m0, m1, ALU.subtract))
                link(tt(SM[:, 3, :], SM[:, 3, :], SM[:, 3, :], ALU.mult))
                link(ts(SM[:, 0, :], SM[:, 1, :], 0.5, None, ALU.mult))
                link(ts(SM[:, 2, :], SM[:, 2, :], 1.0 / D, None, ALU.mult))
                link(v.scalar_tensor_tensor(out=SM[:, 5, :], in0=SM[:, 3, :], scalar=0.25, in1=SM[:, 2, :], op0=ALU.mult, op1=ALU.add))
                if stage not in TWICE:
                    v.tensor_scalar(SM[:, 6, :], SM[:, 5, :], LN_EPS, None, ALU.add).then_inc(var_ready, 1)
                else:
                    link(ts(SM[:, 7, :], SM[:, 5, :], LN_EPS, None, ALU.add))
                    v.scalar_tensor_tensor(out=SM[:, 6, :], in0=SM[:, 7, :], scalar=RMS_EPS if stage == 3 else LN_EPS, in1=SM[:, 5, :],
                                           op0=ALU.mult, op1=ALU.add).then_inc(var_ready, 1)
                dve.wait_ge(pow_ready, stage + 1 + (stage > 3))

            def stats(t):
                v.bn_stats(ST[:, t, :], X[:, t, :]).then_inc(stats_done, 1)

            def attention(l):
                H = HALVES[l]
                t0, u0 = T * l, UNIT0[l]
                K8 = 8 * KEYS[l]

                def x_norm(t, par):
                    wait_from(dve, xt_ready, t0, t - 1)
                    v.tensor_scalar(XN[:, par, :], X[:, t, :], SM[:, 0, at(t, 1)], SM[:, 10, at(t, 1)],
                                    ALU.subtract, ALU.mult).then_inc(xn_ready, 1)

                def scored(q):
                    return PS[:, 2 * q:2 * q + 2, :].rearrange("p a n -> p (a n)")[:, 0:K8].rearrange("p (h k) -> p h k", k=KEYS[l])

                def largest(t, ph, hf):
                    u, q = t * H + hf, (ph * H + hf) % 2
                    dve.wait_ge(score_ready, u0 + u + 1)
                    v.tensor_reduce(MX[:, q, :], scored(q), AX.X, ALU.max).then_inc(max_ready, 1)

                def shift(t, ph, hf):
                    u, q = t * H + hf, (ph * H + hf) % 2
                    dve.wait_ge(max_ready, u0 + u + 1)
                    wait(dve, pt_ready, u0 + u - 3)
                    v.tensor_tensor(prview(l, ph * H + hf), scored(q), MX[:, q, :].unsqueeze(2).to_broadcast([P, 8, KEYS[l]]),
                                    ALU.subtract).then_inc(sub_ready, 1)

                def total(t, ph, hf):
                    u, q = t * H + hf, (ph * H + hf) % 2
                    dve.wait_ge(exp_ready, u0 + u + 1)
                    v.tensor_reduce(RS[:, q, :], prview(l, ph * H + hf), AX.X, ALU.add).then_inc(sum_ready, 1)

                def invert(t, ph, hf):
                    u, q = t * H + hf, (ph * H + hf) % 2
                    dve.wait_ge(sum_ready, u0 + u + 1)
                    wait(dve, prob_ready, u0 + u - 1)
                    v.reciprocal(RI[:, q, :], RS[:, q, :]).then_inc(inv_ready, 1)

                def begin_update(t, par):
                    dve.wait_ge(out_ready, t0 + t + 1)
                    o = PS[:, 6 + par, 0:D]
                    if l != 2:
                        v.tensor_tensor(X[:, t, :], X[:, t, :], o, ALU.add).then_inc(upd_done, 1)
                    else:
                        v.bn_stats(O6[:, par, :], o)
                        dve.drain()
                        v.bn_aggr(O2[:, par, :], O6[:, par, :]).then_inc(o_chain, 1)
                        dve.wait_ge(o_chain, 2 * t + 1)
                        v.tensor_scalar(OE[:, par, :], O2[:, par, 1:2], LN_EPS, None, ALU.add).then_inc(o_eps, 1)
                        v.scalar_tensor_tensor(out=OT[:, par, :], in0=o, scalar=O2[:, par, 0:1], in1=g_out,
                                               op0=ALU.subtract, op1=ALU.mult).then_inc(o_chain, 1)

                def end_update(t, par):
                    if l == 2:
                        dve.wait_ge(o_rstd, t + 1)
                        dve.wait_ge(o_chain, 2 * t + 2)
                        v.scalar_tensor_tensor(out=X[:, t, :], in0=OT[:, par, :], scalar=OR[:, par, 0:1], in1=X[:, t, :],
                                               op0=ALU.mult, op1=ALU.add).then_inc(upd_done, 1)
                    dve.wait_ge(upd_done, t0 + t + 1)
                    stats(t)

                x_norm(0, 0)
                x_norm(1, 1)
                lag = LAG[l]

                def body(t, ph):
                    first = isinstance(t, int) and t == 0
                    done = t - lag - 1
                    updating = not (isinstance(t, int) and done < 0)
                    if not (isinstance(t, int) and t >= T - 2):
                        x_norm(t + 2, ph % 2)
                    for hf in range(H):
                        before_ = (t, ph, hf - 1) if hf else (t - 1, before_by(l, ph, 1), H - 1)
                        largest(t, ph, hf)
                        if hf or not first:
                            total(*before_)
                        shift(t, ph, hf)
                        if hf or not first:
                            invert(*before_)
                        if hf == 0 and updating:
                            begin_update(done, before_by(l, ph, lag + 1) % 2)
                        if hf == H - 1 and updating:
                            end_update(done, before_by(l, ph, lag + 1) % 2)
                in_groups(dve, l, body)
                total(T - 1, GROUP[l] - 1, H - 1)
                invert(T - 1, GROUP[l] - 1, H - 1)
                for t in range(T - lag - 1, T):
                    begin_update(t, t % 2)
                    end_update(t, t % 2)

            def front(l):
                if l == 2:
                    dve.wait_ge(x_acc, 2 * T)
                for t in range(T):
                    v.tensor_scalar(RW[:, 0, t, 0:D], X[:, t, :], SM[:, 0, t:t + 1], SM[:, 10, t:t + 1],
                                    ALU.subtract, ALU.mult).then_inc(f_xn, 1)

            def wide(a):
                return a.unsqueeze(2).to_broadcast([P, T, E])

            def top2(src):
                for k, (val, oh) in enumerate(((13, 1), (14, 2))):
                    link(v.tensor_reduce(SM[:, val, :], src, AX.X, ALU.max))
                    link(tt(RT[:, 3, :, :], src, wide(SM[:, val, :]), ALU.is_equal))
                    link(v.scalar_tensor_tensor(out=RT[:, 3, :, :], in0=RT[:, 3, :, :], scalar=-16.0, in1=iota, op0=ALU.mult, op1=ALU.add))
                    link(v.tensor_reduce(SM[:, 15, :], RT[:, 3, :, :], AX.X, ALU.min))
                    link(tt(RT[:, oh, :, :], RT[:, 3, :, :], wide(SM[:, 15, :]), ALU.is_equal))
                    if k == 0:
                        link(v.scalar_tensor_tensor(out=RT[:, 4, :, :], in0=RT[:, 1, :, :], scalar=-3e38, in1=src, op0=ALU.mult, op1=ALU.add))
                        src = RT[:, 4, :, :]

            def places():
                v.tensor_tensor(RT[:, 5, :, :], RT[:, 1, :, :], RT[:, 2, :, :], ALU.add).then_inc(r_count, 1)
                link(v.memset(RC[:, :, 0:8, :], 0.0))
                dve.wait_ge(r_sums, counts[0] + 1)
                counts[0] += 1
                flat = PS[:, 1, 0:T * E].rearrange("p (t e) -> p t e", e=E)
                link(v.tensor_copy(RC[:, 0, 8:24, :], flat))
                a = 0
                for step in (1, 2, 4, 8):
                    link(tt(RC[:, 1 - a, 8:24, :], RC[:, a, 8:24, :], RC[:, a, 8 - step:24 - step, :], ALU.add))
                    a = 1 - a
                link(tt(RT[:, 7, :, :], PS[:, 0, 0:T * E].rearrange("p (t e) -> p t e", e=E), RC[:, a, 7:23, :], ALU.add))

            def slot_rows(l):
                cap = float(CAP[l])
                link(ts(RT[:, 8, :, :], RT[:, 7, :, :], cap, None, ALU.is_lt))
                link(v.scalar_tensor_tensor(out=RT[:, 9, :, :], in0=iota, scalar=cap, in1=RT[:, 7, :, :], op0=ALU.mult, op1=ALU.add))
                for k in range(2):
                    link(tt(RT[:, 3, :, :], RT[:, 1 + k, :, :], RT[:, 8, :, :], ALU.mult))
                    link(v.tensor_reduce(RK[:, 0, k, :], RT[:, 3, :, :], AX.X, ALU.add))
                    link(tt(RT[:, 3, :, :], RT[:, 3, :, :], RT[:, 9, :, :], ALU.mult))
                    link(v.tensor_reduce(RK[:, 1, k, :], RT[:, 3, :, :], AX.X, ALU.add))
                link(ts(RK[:, 2, :, :], RK[:, 0, :, :], -1.0, 1.0, ALU.mult, ALU.add))
                link(v.scalar_tensor_tensor(out=RK[:, 2, :, :], in0=spare, scalar=float(E * CAP[l]), in1=RK[:, 2, :, :],
                                            op0=ALU.add, op1=ALU.mult))
                link(tt(RK[:, 2, :, :], RK[:, 2, :, :], RK[:, 1, :, :], ALU.add))
                v.tensor_copy(IX[:, :], RK[:, 2, :, :].rearrange("p k t -> p (k t)")).then_inc(r_idx, 1)

            counts = [0]

            def router(l):
                z = PS[:, 3, 0:T * E].rearrange("p (t e) -> p t e", e=E)
                dve.wait_ge(f_gate, B * (l + 1))
                dve.wait_ge(fw_in[l], 16)
                if l == 0:
                    dve.wait_ge(r_exp, 1)
                    link(ts(RT[:, 0, :, :], RT[:, 0, :, :], 1.0, None, ALU.add))
                    link(v.memset(S9[:, :, E:EB], 1.0))
                    link(v.memset(W9[:, :, E:EB], 1.0))
                    link(v.reciprocal(S9[:, :, 0:E], RT[:, 0, :, :]))
                    link(tt(RT[:, 6, :, :], S9[:, :, 0:E], FA[:, F0["bias"]:F0["bias"] + T * E].rearrange("p (t e) -> p t e", e=E), ALU.add))
                    top2(RT[:, 6, :, :])
                    link(tt(RT[:, 1, :, :], RT[:, 1, :, :], RT[:, 2, :, :], ALU.add))
                    link(tt(RT[:, 1, :, :], RT[:, 1, :, :], S9[:, :, 0:E], ALU.mult))
                    v.tensor_tensor(W9[:, :, 0:E], RT[:, 1, :, :], S9[:, :, 0:E], ALU.mult).then_inc(r_done, 1)
                if l == 1:
                    dve.wait_ge(pow_ready, 5)
                    link(tt(SM[:, 11, :], SM[:, 8, :], SM[:, 10, :], ALU.mult))
                    link(tt(SM[:, 11, :], SM[:, 11, :], SM[:, 6, :], ALU.mult))
                    link(tt(RT[:, 0, :, :], z, wide(SM[:, 11, :]), ALU.mult))
                    link(v.tensor_reduce(SM[:, 1, :], RT[:, 0, :, :], AX.X, ALU.max))
                    v.tensor_tensor(RT[:, 0, :, :], RT[:, 0, :, :], wide(SM[:, 1, :]), ALU.subtract).then_inc(r_logit, 1)
                    dve.wait_ge(r_exp, 2)
                    link(v.tensor_reduce(SM[:, 1, :], RT[:, 0, :, :], AX.X, ALU.add))
                    link(v.reciprocal(SM[:, 2, :], SM[:, 1, :]))
                    link(tt(RT[:, 6, :, :], RT[:, 0, :, :], wide(SM[:, 2, :]), ALU.mult))
                    top2(RT[:, 6, :, :])
                    places()
                    slot_rows(1)
                    link(tt(SM[:, 4, :], RK[:, 0, 0, :], RK[:, 0, 1, :], ALU.mult))
                    link(tt(RK[:, 3, 0, :], SM[:, 13, :], SM[:, 4, :], ALU.mult))
                    link(tt(RK[:, 3, 1, :], SM[:, 14, :], SM[:, 4, :], ALU.mult))
                    link(ts(W9[:, :, E], SM[:, 4, :], -1.0, 1.0, ALU.mult, ALU.add))
                    link(tt(SM[:, 5, :], RK[:, 3, 0, :], RK[:, 3, 1, :], ALU.add))
                    link(ts(SM[:, 5, :], SM[:, 5, :], 1.0, None, ALU.add))
                    link(tt(SM[:, 5, :], SM[:, 5, :], SM[:, 8, :], ALU.mult))
                    link(tt(SM[:, 1, :], SM[:, 0, :], SM[:, 5, :], ALU.mult))
                    link(ts(SM[:, 2, :], SM[:, 5, :], 1.0, None, ALU.add))
                    v.tensor_copy(SM[:, 3, :], SM[:, 1, :]).then_inc(r_done, 1)
                if l == 2:
                    v.tensor_tensor(RT[:, 0, :, :], z, FA[:, F2["bias"]:F2["bias"] + T * E].rearrange("p (t e) -> p t e", e=E), ALU.add).then_inc(r_logit, 1)
                    dve.wait_ge(r_exp, 3)
                    link(ts(RT[:, 0, :, :], RT[:, 0, :, :], 1.0, None, ALU.add))
                    link(v.reciprocal(RT[:, 7, :, :], RT[:, 0, :, :]))
                    top2(RT[:, 7, :, :])
                    link(tt(SM[:, 1, :], SM[:, 13, :], SM[:, 14, :], ALU.add))
                    link(ts(SM[:, 1, :], SM[:, 1, :], 1e-8, None, ALU.add))
                    link(v.reciprocal(SM[:, 2, :], SM[:, 1, :]))
                    link(tt(RT[:, 6, :, :], RT[:, 1, :, :], RT[:, 2, :, :], ALU.add))
                    link(tt(RT[:, 5, :, :], RT[:, 7, :, :], wide(SM[:, 2, :]), ALU.mult))
                    v.tensor_tensor(RT[:, 5, :, :], RT[:, 5, :, :], RT[:, 6, :, :], ALU.mult).then_inc(r_count, 1)
                    dve.wait_ge(r_sums, counts[0] + 1)
                    counts[0] += 1
                    sums = PS[:, 0, 0:2 * T * E].rearrange("p (a t e) -> p a e t", a=2, e=E)
                    for a in range(2):
                        link(v.tensor_reduce(W2[:, a, :], sums[:, a, :, :], AX.X, ALU.add))
                    link(ts(W2[:, 1, :], W2[:, 1, :], 1.0, None, ALU.max))
                    link(v.reciprocal(W2[:, 2, :], W2[:, 1, :]))
                    link(tt(W2[:, 3, :], W2[:, 0, :], W2[:, 2, :], ALU.mult))
                    link(v.memset(W9[:, :, E:EB], 1.0))
                    v.tensor_tensor(W9[:, :, 0:E], RT[:, 6, :, :], W2[:, 3, :].unsqueeze(1).to_broadcast([P, T, E]), ALU.mult).then_inc(r_done, 1)
                if l == 3:
                    link(ts(RT[:, 0, :, :], z, CLAMP, -CLAMP, ALU.min, ALU.max))
                    top2(RT[:, 0, :, :])
                    v.tensor_tensor(SM[:, 12, :], SM[:, 14, :], SM[:, 13, :], ALU.subtract).then_inc(r_logit, 1)
                    dve.wait_ge(r_exp, 4)
                    link(ts(SM[:, 1, :], SM[:, 12, :], 1.0, 1e-12, ALU.add, ALU.add))
                    link(v.reciprocal(SM[:, 2, :], SM[:, 1, :]))
                    link(tt(SM[:, 3, :], SM[:, 12, :], SM[:, 2, :], ALU.mult))
                    places()
                    slot_rows(3)
                    link(tt(RK[:, 3, 0, :], SM[:, 2, :], RK[:, 0, 0, :], ALU.mult))
                    v.tensor_tensor(RK[:, 3, 1, :], SM[:, 3, :], RK[:, 0, 1, :], ALU.mult).then_inc(r_done, 1)

            def residual():
                dve.wait_ge(r_done, 2)
                for t in range(T):
                    v.tensor_scalar(X[:, t, :], X[:, t, :], SM[:, 2, t:t + 1], SM[:, 1, t:t + 1],
                                    ALU.mult, ALU.subtract).then_inc(xres_done, 1)
                dve.wait_ge(xres_done, T)

            def experts0():
                dve.wait_ge(r_done, 1)

                def gated(t, par, g):
                    n = t * 3 + g
                    q = (par * 3 + g) % 2
                    dve.wait_ge(t_act, n + 1)
                    wait(dve, t_tr, n - 1)
                    for k in range(3):
                        e = g * 3 + k
                        op = v.scalar_tensor_tensor(out=HS[:, q, k * P:(k + 1) * P], in0=PS[:, 2 * q + 1, k * P:(k + 1) * P],
                                                    scalar=W9[:, t, e:e + 1], in1=GS[:, q, k * P:(k + 1) * P], op0=ALU.mult, op1=ALU.mult)
                    op.then_inc(t_mul, 1)

                def update(t, par):
                    dve.wait_ge(t_out, t + 1)
                    v.tensor_tensor(X[:, t, :], X[:, t, :], PS[:, 6 + par, 0:D], ALU.add).then_inc(t_upd, 1)
                    dve.wait_ge(t_upd, t + 1)
                    stats(t)

                def body(t, par):
                    for g in range(3):
                        if g == 2 and not (isinstance(t, int) and t == 0):
                            update(t - 1, 1 - par)
                        gated(t, par, g)
                in_pairs(dve, body)
                update(T - 1, 1)

            def weigh(b, e, bank_, count):
                dve.wait_ge(e_down, count)
                for j in range(TPB):
                    t = b * TPB + j
                    op = v.scalar_tensor_tensor(out=X[:, t, :], in0=PS[:, bank_, j * P:(j + 1) * P],
                                                scalar=W9[:, t, e:e + 1], in1=X[:, t, :], op0=ALU.mult, op1=ALU.add)
                op.then_inc(e_acc, 1)
                dve.wait_ge(e_acc, count)

            def fallback():
                for b in range(B):
                    dve.wait_ge(e_act, b + 1)
                    v.tensor_tensor(HS[:, b % 2, :], PS[:, 2 + b % 2, :], GS[:, b % 2, :], ALU.mult).then_inc(e_mul, 1)
                    if b:
                        weigh(b - 1, E, 4 + (b - 1) % 2, b)
                weigh(B - 1, E, 4 + (B - 1) % 2, B)

            def experts2():
                plan, n0, q0 = PLAN2, UP2, DOWN2
                N = len(plan)
                dve.wait_ge(r_done, 3)

                def gated(b, n):
                    dve.wait_ge(e_act, n0 + b * N + n + 1)
                    v.tensor_tensor(HS[:, n % 2, :], PS[:, 2 + n % 2, :], GS[:, n % 2, :], ALU.mult).then_inc(e_mul, 1)

                with dve.Fori(0, B) as b:
                    for n in range(N):
                        gated(b, n)
                        if n:
                            for e, lo, hi in plan[n - 1][1]:
                                weigh(b, e, 4 + e % 2, q0 + b * EB + e + 1)
                    for e, lo, hi in plan[N - 1][1]:
                        weigh(b, e, 4 + e % 2, q0 + b * EB + e + 1)
                    for j in range(TPB):
                        stats(b * TPB + j)

            def sparse_experts(l):
                N, steps, n0 = STEPS[l], steps_of(l), SLOT0[l]

                r = ROUND[l]

                def numbers(e, k):
                    dve.wait_ge(xs_in[k], 16 * (E // 2 * r + (e - k) // 2 + 1) if isinstance(e, int) else 8 * (e - k) + 16 * (E // 2 * r + 1))
                    wait(dve, y_out[k], outputs_written(l, k, e - 2))
                    n = SLOT_TILES[l]
                    v.tensor_copy(ID[:, k, 0:n], XS[:, k, 0:n, D]).then_inc(ids_ready, 1)

                def pair(e0):
                    for k in range(2):
                        for n in range(N):
                            cols, q = steps[n][1] * P, (k * N + n) % 2
                            dve.wait_ge(e_act, n0 + (e0 + k) * N + n + 1)
                            v.tensor_tensor(HS[:, q, 0:cols], PS[:, 2 + q, 0:cols], GS[:, q, 0:cols], ALU.mult).then_inc(e_mul, 1)
                            if n == 0:
                                numbers(e0 + k, k)
                in_expert_pairs(dve, pair)
                a0 = 2 * T * r
                for b in range(B):
                    dve.wait_ge(y_back[b], 16 * 2 * (r + 1))
                    for k in range(2):
                        for t in range(b * TPB, (b + 1) * TPB):
                            v.scalar_tensor_tensor(out=X[:, t, :], in0=RW[:, k, t, 0:D], scalar=RK[:, 3, k, t:t + 1],
                                                   in1=X[:, t, :], op0=ALU.mult, op1=ALU.add).then_inc(x_acc, 1)
                        dve.wait_ge(x_acc, a0 + (2 * b + k + 1) * TPB)
                    if l == 1:
                        for t in range(b * TPB, (b + 1) * TPB):
                            stats(t)

            dve.wait_ge(const_in, 80)
            v.memset(ONEB[:, :], 1.0)
            link(ts(MKF[:, :], MK[:, :], -NEG, NEG, ALU.mult, ALU.add))
            for h in range(8):
                op = v.tensor_copy(MB[:, :, h, :], MKF[:, :].rearrange("p (b k) -> p b k", k=KMAX))
            op.then_inc(mask_made, 1)
            dve.wait_ge(x_in, 16)
            with dve.Fori(0, T) as t:
                stats(t)
            for l in range(4):
                deviations(2 * l)
                attention(l)
                deviations(2 * l + 1)
                front(l)
                router(l)
                if l == 1:
                    residual()
                if l == 0:
                    experts0()
                if l == 1:
                    fallback()
                if l == 2:
                    experts2()
                if l in (1, 3):
                    sparse_experts(l)


def kernel(**inputs):
    import concourse.bacc as bacc
    from concourse.bass_utils import run_bass_kernel_spmd

    a = {k: np.asarray(v) for k, v in inputs.items()}

    def cols(w):
        o = np.zeros((P, w.shape[1]), w.dtype)
        o[:w.shape[0]] = w
        return o

    def chunks(w):
        return w.reshape(-1, P, w.shape[1]).transpose(1, 0, 2).reshape(P, -1)

    def everywhere(r):
        return np.broadcast_to(r.reshape(1, -1), (P, r.size))

    def attention_weights(wq, wk, wv, wo):
        return np.concatenate([cols(wk), cols(wv), chunks(wq.T), chunks(wo)], 1)

    l2k, l2v = np.split(a["L2_xattn_Wkv"], 2, axis=1)
    aw = [
        attention_weights(a["L0_xattn_Wq"], a["L0_xattn_Wk"], a["L0_xattn_Wv"], a["L0_xattn_Wo"]),
        attention_weights(a["L1_xattn_Wq"], a["L1_xattn_Wk"], a["L1_xattn_Wv"], a["L1_xattn_Wo"]),
        attention_weights(a["L2_xattn_Wq"], l2k, l2v, a["L2_xattn_Wout"]),
        np.concatenate([cols(a["L3_xattn_wk"].T), cols(a["L3_xattn_wv"].T), a["L3_xattn_wq"].T, a["L3_xattn_wo"].T], 1),
    ]

    w1 = np.concatenate([a["L0_ffn_w1"], a["L0_ffn_sw1"][None]]).transpose(2, 0, 1)
    w3 = np.concatenate([a["L0_ffn_w3"], a["L0_ffn_sw3"][None]]).transpose(2, 0, 1)
    w2 = np.concatenate([a["L0_ffn_w2"], a["L0_ffn_sw2"][None]]).transpose(2, 0, 1)
    up = np.stack([w1.reshape(P, 3, 384), w3.reshape(P, 3, 384)], 2).reshape(P, -1)
    fw0 = [a["L0_ffn_gate_w"].T, everywhere(np.tile(a["L0_ffn_expert_bias"], T)), up, w2.reshape(P, -1)]

    def padded(w):
        return np.concatenate([w, np.zeros((P, P - w.shape[1]), w.dtype)], 1)

    fw1 = [a["L1_ffn_Wr"], a["L1_ffn_norm_w"].T, a["L1_ffn_f_norm"][:, None],
           padded(a["L1_ffn_fWg"]), padded(a["L1_ffn_fWu"]), cols(a["L1_ffn_fWd"])]
    fw2 = [a["L2_ffn_gate_w"].T, everywhere(np.tile(a["L2_ffn_lb_bias"], T)),
           a["L2_ffn_expert_gate_w"].transpose(2, 0, 1).reshape(P, -1), a["L2_ffn_shared_gate_w"].T,
           a["L2_ffn_expert_up_w"].transpose(2, 0, 1).reshape(P, -1), a["L2_ffn_shared_up_w"].T,
           chunks(a["L2_ffn_expert_down_w"].transpose(0, 2, 1).reshape(-1, D)), a["L2_ffn_shared_down_w"].T]
    fw3 = [a["L3_ffn_router_w"].T, a["L3_ffn_ln_gamma"][:, None], a["L3_ffn_ln_beta"][:, None]]
    fw = [np.concatenate(f, 1) for f in (fw0, fw1, fw2, fw3)]

    def expert_weights(gate_up, down):
        d = down.reshape(E, -1, P, D).transpose(0, 2, 1, 3).reshape(E, P, -1)
        return np.concatenate([gate_up, d], 2).reshape(E * P, -1)

    ew = {1: expert_weights(np.concatenate([a["L1_ffn_Wg"], a["L1_ffn_Wu"]], 2), a["L1_ffn_Wd"]),
          3: expert_weights(a["L3_ffn_w12"].transpose(0, 2, 1), a["L3_ffn_w3"].transpose(0, 2, 1))}

    i = np.arange(P)
    f = np.float32
    null = a["L2_xattn_null_kv"]
    consts = np.concatenate([
        np.eye(P, dtype=f), np.ones((P, P), f), (i[:, None] < i[None, :]).astype(f),
        np.broadcast_to(np.tile(np.arange(E, dtype=f), T), (P, P)),
        (i[:, None] // 8 == np.arange(16)[None, :]).astype(f), everywhere(a["L2_xattn_g_out"]),
        a["L2_xattn_g_norm"][:, None], np.concatenate([null[0], null[0]])[:, None], np.concatenate([null[1], null[1]])[:, None],
        a["L3_xattn_bq"][:, None], a["L3_xattn_bk"][:, None], a["L3_xattn_bv"][:, None],
        (i[:, None] + P * np.arange(2 * T)[None, :]).astype(f)], 1)
    rows = np.concatenate([a["L0_xattn_bo"], a["L1_xattn_bo"], a["L3_xattn_bo"]])[None]
    m = a["mask_BxS2_bf1"]
    mask = np.concatenate([np.ones((B, 1), m.dtype), m], 1).reshape(1, -1).view(np.uint8)

    data = {"x": a["x"].reshape(NTOK, D), "ctxT": a["ctx_768"].reshape(B * NK, CD).T, "mask": mask,
            "consts": consts, "rows": rows}
    data.update({f"aw{l}": w for l, w in enumerate(aw)})
    data.update({f"fw{l}": w for l, w in enumerate(fw)})
    data.update({f"ew{l}": w for l, w in ew.items()})

    nc = bacc.Bacc("TRN2", target_bir_lowering=False, num_devices=1)
    arrays, aps = {}, {}
    for name, v in data.items():
        v = np.ascontiguousarray(v)
        arrays[f"in_{name}"] = v
        aps[name] = nc.dram_tensor(f"in_{name}", v.shape, mybir.dt.from_np(v.dtype), kind="ExternalInput").ap()
    out = nc.dram_tensor("out", (NTOK, D), F32, kind="ExternalOutput").ap()
    slots = {l: nc.dram_tensor(f"slots{l}", (E * CAP[l], ROW), F32).ap() for l in (1, 3)}
    made = {l: nc.dram_tensor(f"made{l}", (2 * NTOK, D), F32).ap() for l in (1, 3)}
    fused_decoder_kernel(nc, aps["x"], aps["ctxT"], aps["mask"], aps["consts"], aps["rows"],
                         [aps[f"aw{l}"] for l in range(4)], [aps[f"fw{l}"] for l in range(4)], {l: aps[f"ew{l}"] for l in ew}, slots, made, out)
    r = run_bass_kernel_spmd(nc, [arrays], core_ids=[0])
    return r.results[0]["out"].reshape(B, S, D)
```

```python
from contextlib import ExitStack

import numpy as np

import concourse.bass as bass
from concourse import mybir

F32 = mybir.dt.float32
BF16 = mybir.dt.bfloat16
F32R = mybir.dt.float32r
U8 = mybir.dt.uint8
I32 = mybir.dt.int32
ALU = mybir.AluOpType
ACT = mybir.ActivationFunctionType
AX = mybir.AxisListType

P = 128
B, S, D, CD, NK = 4, 512, 128, 96, 77
T = B * S // P
TPB = S // P
E = 8
NTOK = B * S

LN_EPS = 1e-5
RMS_EPS = 1e-6
NEG = -3.3e38
CAP = {1: 512, 3: 640}
CLAMP = 10000.0

HEADS = [16, 8, 16, 16]
KEYS = [NK, NK, NK + 1, NK]
PER = [2, 1, 2, 16]
CHUNKS = [8, 8, 8, 1]
HALVES = [2, 1, 2, 2]
LAG = [2, 3, 2, 2]
GROUP = [2, 4, 2, 2]
PEEL = [2, 1, 2, 2]
SCALE = [64 ** -0.5, 128 ** -0.5, 64 ** -0.5, 8 ** -0.5]
KMAX = NK + 1
UNIT0 = [T * sum(HALVES[:l]) for l in range(4)]
BLOCKS0 = [B * sum(HALVES[:l]) for l in range(4)]
PADV = 128

EB = E + 1
F0 = dict(gate=0, bias=8, up=136, down=136 + EB * 256)
F0["end"] = F0["down"] + EB * 128
F1 = dict(gate=0, norm=8, g=17, u=17 + 128, down=17 + 2 * 128)
F1["end"] = F1["down"] + 128
F2 = dict(gate=0, bias=8, g=136, u=136 + 5 * 128, down=136 + 10 * 128)
F2["end"] = F2["down"] + 5 * 128
F3 = dict(gate=0, gamma=8, beta=9, end=10)
FA_COLS = max(F0["end"], F2["end"])
C_ID, C_ONE, C_TRI, C_IOTA, C_BM, C_GO = 0, 128, 256, 384, 512, 528
C_COL = 528 + 128
C_SPARE = C_COL + 6
C_END = C_SPARE + 2 * T


PLAN2 = [(c, [(2 * c, 0, 64), (2 * c + 1, 64, P)]) for c in range(4)] + [(4, [(E, 0, P)])]
HID = {1: 2, 3: 4}
GROUPS = {1: [4], 3: [3, 2]}
SLOT_TILES = {l: CAP[l] // P for l in (1, 3)}
STEPS = {l: HID[l] * len(GROUPS[l]) for l in (1, 3)}
WCOLS = {l: 3 * HID[l] * P for l in (1, 3)}
ROW = D + 1
ROUND = {1: 0, 3: 1}
UP2, DOWN2 = B + E * STEPS[1], B
SLOT0 = {1: B, 3: UP2 + B * len(PLAN2)}
GROUP0 = {1: 0, 3: E * len(GROUPS[1])}
TWICE = (3, 4, 7)
PARTS = [[(0, T)] if stage % 2 == 0 else [(0, T - TPB), (T - TPB, T)] for stage in range(8)]
PART0 = [sum(len(p) for p in PARTS[:stage]) for stage in range(8)]


def fused_decoder_kernel(nc, x, ctxT, mask, consts, rows, aw, fw, ew, slots, made, out):
    with ExitStack() as ctx:
        def sb(name, shape, dt=F32):
            return ctx.enter_context(nc.sbuf_tensor(name, shape, dt))

        def sem(name):
            return ctx.enter_context(nc.semaphore(name))

        def under(name, before, cols):
            with nc.sbuf_tensor(name + "_before", [P, max(before, 1)], F32) if before else ExitStack():
                with nc.sbuf_tensor(name, [P, cols], F32R) as upper:
                    return upper

        X = sb("X", [P, T, D])
        XAL = under("XAL", 0, NTOK)
        XTA = sb("XTA", [P, NTOK])
        AW = sb("AW", [P, 4096])
        G = sb("G", [P, B * 16 * KMAX])
        VW = sb("VW", [P, B, 10, D])
        KV = sb("KV", [P, 8, B * NK + 1])
        VB = sb("VB", [P, 8, 2 * PADV + 2 * KMAX])
        UL = under("UL", F0["up"], F0["down"] - F0["up"])
        SPLIT3 = 2 * HID[3] * P
        H3 = under("H3", 0, 2 * SPLIT3 + 2 * CAP[3])
        W2L = under("W2L", F2["g"], F2["down"] - F2["g"])
        FA = sb("FA", [P, FA_COLS])
        FB = sb("FB", [P, F1["end"]])
        FC = sb("FC", [P, F3["end"]])
        UH = under("UH", 0, F0["down"] - F0["up"])
        WL = under("WL", 0, 2 * WCOLS[3])
        WS = sb("WS", [P, 2, WCOLS[3]])
        HI2 = under("HI2", 0, NTOK + F2["down"] - F2["g"])
        assert NTOK + F2["down"] - F2["g"] <= 2 * SLOT_TILES[3] * ROW + 2 * CAP[3] + 12 * D
        XS = sb("XS", [P, 2, SLOT_TILES[3], ROW])
        XSL = under("XSL", 0, 2 * CAP[3])
        XTS = sb("XTS", [P, 2, CAP[3]])
        YS = sb("YS", [P, 4 * 3, D])
        RW = sb("RW", [P, 2, T, ROW])
        RK = sb("RK", [P, 4, 2, T])
        IX = sb("IX", [P, 2 * T], I32)
        ID = sb("ID", [P, 2, SLOT_TILES[3]], I32)
        CT = sb("CT", [CD, B * NK])
        CN = sb("CN", [P, C_END])
        BO = sb("BO", [1, 4 * 128])
        MK = sb("MK", [1, B * KMAX], U8)
        MB = sb("MB", [1, B, 8, KMAX], BF16)
        MKF = sb("MKF", [1, B * KMAX])
        gcol = sb("gcol", [P, 1])
        ONEB = sb("ONEB", [1, P], BF16)
        BMS = sb("BMS", [P, 16])
        NH = sb("NH", [P, T])
        ST = sb("ST", [P, T, 6])
        SM = sb("SM", [P, 16, T])
        XN = sb("XN", [P, 2, D])
        XTB = sb("XTB", [P, 2, P])
        QTB = sb("QTB", [P, 2, P])
        PR = sb("PR", [P, 4, 8 * KMAX])
        PT = sb("PT", [P, 5, P])
        XH = sb("XH", [P, 2, P], F32R)
        XL = sb("XL", [P, 2, P], F32R)
        MX = sb("MX", [P, 2, 8])
        RS = sb("RS", [P, 2, 8])
        RI = sb("RI", [P, 2, 8])
        OT = sb("OT", [P, 2, D])
        O6 = sb("O6", [P, 2, 6])
        O2 = sb("O2", [P, 2, 2])
        OR = sb("OR", [P, 2, 1])
        OE = sb("OE", [P, 2, 1])
        GS = sb("GS", [P, 2, 512])
        HS = sb("HS", [P, 2, 512])
        RT = sb("RT", [P, 12, T, E])
        RC = sb("RC", [P, 2, 24, E])
        W9 = sb("W9", [P, T, EB])
        S9 = sb("S9", [P, T, EB])
        W2 = sb("W2", [P, 4, E])
        PS = ctx.enter_context(nc.psum_tensor("PS", [P, 8, 512], F32))

        up0 = FA[:, F0["up"]:F0["down"]]
        WH3 = H3[:, 0:2 * SPLIT3].rearrange("p (k n) -> p k n", k=2)
        XH3 = H3[:, 2 * SPLIT3:2 * SPLIT3 + 2 * CAP[3]].rearrange("p (k n) -> p k n", k=2)
        WL3 = WL[:, :].rearrange("p (k n) -> p k n", k=2)
        XL3 = XSL[:, :].rearrange("p (k n) -> p k n", k=2)
        ident = CN[:, C_ID:C_ID + P]
        ones = CN[:, C_ONE:C_ONE + P]
        before = CN[:, C_TRI:C_TRI + P]
        iota = CN[:, C_IOTA:C_IOTA + T * E].rearrange("p (t e) -> p t e", e=E)
        headmask = CN[:, C_BM:C_BM + 16]
        g_out = CN[:, C_GO:C_GO + P]
        g_norm, null_k, null_v, bq, bk, bv = (CN[:, C_COL + i:C_COL + i + 1] for i in range(6))
        spare = CN[:, C_SPARE:C_SPARE + 2 * T].rearrange("p (k t) -> p k t", k=2)
        gamma, beta = (FC[:, F3[n]:F3[n] + 1] for n in ("gamma", "beta"))

        x_in, const_in, stored = sem("x_in"), sem("const_in"), sem("stored")
        aw_in = [sem(f"aw_in{l}") for l in range(4)]
        fw_in = [sem(f"fw_in{l}") for l in range(4)]
        zeroed, mask_made, nh_made = sem("zeroed"), sem("mask_made"), sem("nh_made")
        shift_ready, first_ready = sem("shift_ready"), sem("first_ready")
        stats_done, var_ready, pow_ready = sem("stats_done"), sem("var_ready"), sem("pow_ready")
        p_mm, p_ev, vb_ready = sem("p_mm"), sem("p_ev"), sem("vb_ready")
        vb_zero, null_in, gk_done = sem("vb_zero"), sem("null_in"), sem("gk_done")
        xn_ready, xt_ready, xtb_ready = sem("xn_ready"), sem("xt_ready"), sem("xtb_ready")
        q_ready, qtb_ready = sem("q_ready"), sem("qtb_ready")
        score_ready, max_ready, sub_ready, exp_ready = sem("score_ready"), sem("max_ready"), sem("sub_ready"), sem("exp_ready")
        sum_ready, inv_ready, prob_ready = sem("sum_ready"), sem("inv_ready"), sem("prob_ready")
        pt_ready, pte_ready, out_ready, upd_done = sem("pt_ready"), sem("pte_ready"), sem("out_ready"), sem("upd_done")
        o_chain, o_eps, o_rstd = sem("o_chain"), sem("o_eps"), sem("o_rstd")
        zero_made, slots_clear, r_idx, scattered = sem("zero_made"), sem("slots_clear"), sem("r_idx"), sem("scattered")
        ws_in, xs_in, y_out = ([sem(f"{n}{k}") for k in range(2)] for n in ("ws_in", "xs_in", "y_out"))
        xs_blank, ids_set, ids_ready, rows_copied = sem("xs_blank"), sem("ids_set"), sem("ids_ready"), sem("rows_copied")
        xs_turned, xts_ready, y_made, ys_ready = sem("xs_turned"), sem("xts_ready"), sem("y_made"), sem("ys_ready")
        y_back = [sem(f"y_back{b}") for b in range(B)]
        x_acc = sem("x_acc")
        f_xn, f_xt, f_xta, f_gate = sem("f_xn"), sem("f_xt"), sem("f_xta"), sem("f_gate")
        r_chain, r_logit, r_exp, r_count, r_sums, r_done, wn_done = (
            sem("r_chain"), sem("r_logit"), sem("r_exp"), sem("r_count"), sem("r_sums"), sem("r_done"), sem("wn_done"))
        e_up, e_act, e_mul, e_down, e_acc = sem("e_up"), sem("e_act"), sem("e_mul"), sem("e_down"), sem("e_acc")
        w3_hi, w3_split, x3_hi, x3_split = sem("w3_hi"), sem("w3_split"), sem("x3_hi"), sem("x3_split")
        w2_halves, x2_halves = sem("w2_halves"), sem("x2_halves")
        up_halves, t_split = sem("up_halves"), sem("t_split")
        t_in, t_up, t_act, t_mul, t_tr, t_ev, t_out, t_upd = (sem(n) for n in (
            "t_in", "t_up", "t_act", "t_mul", "t_tr", "t_ev", "t_out", "t_upd"))
        xres_done, bms_made = sem("xres_done"), sem("bms_made")

        block = ctx.enter_context(nc.Block())

        VB3 = VB[:, :, :].rearrange("p j n -> p (j n)")

        def gview(l):
            return G[:, 0:B * HEADS[l] * KEYS[l]].rearrange("p (b h k) -> p b h k", b=B, k=KEYS[l])

        def prview(l, i):
            return PR[:, i, 0:8 * KEYS[l]].rearrange("p (h k) -> p h k", k=KEYS[l])

        def wait(eng, s, v):
            if isinstance(v, int) and v <= 0:
                return
            eng.wait_ge(s, v)

        def wait_from(eng, s, base, v):
            if not isinstance(v, int) or v > 0:
                eng.wait_ge(s, base + v)

        def in_pairs(eng, body):
            body(0, 0)
            body(1, 1)
            with eng.Fori(1, T // 2 - 1) as i:
                body(2 * i, 0)
                body(2 * i + 1, 1)
            body(T - 2, 0)
            body(T - 1, 1)

        def in_groups(eng, l, body):
            n, peel = GROUP[l], PEEL[l]
            for t in range(peel * n):
                body(t, t % n)
            with eng.Fori(peel, T // n - 1) as i:
                for k in range(n):
                    body(n * i + k, k)
            for t in range(T - n, T):
                body(t, t % n)

        def in_expert_pairs(eng, body):
            body(0)
            with eng.Fori(1, E // 2 - 1) as i:
                body(2 * i)
            body(E - 2)

        def output_buffer(l, k, g):
            return 4 * k if l == 1 else 3 * (2 * k + g)

        def outputs_written(l, k, e):
            n = 16 * SLOT_TILES[l]
            done = n * ((e - k) // 2 + 1) if isinstance(e, int) else n // 2 * (e - k + 2)
            return ROUND[l] * 16 * SLOT_TILES[1] * E // 2 + done

        def turn_at(l):
            return max(1, STEPS[l] - 3)

        def steps_of(l):
            return [(g, n, sum(GROUPS[l][:g]), c) for g, n in enumerate(GROUPS[l]) for c in range(HID[l])]

        def at(start, n):
            return slice(start, start + n) if isinstance(start, int) else bass.ds(start, n)

        def keys_between(l, t, hf):
            if l == 3:
                return []
            n, i = LAG[l] * HALVES[l], (t - (T - LAG[l])) * HALVES[l] + hf
            return range(i * CHUNKS[l + 1] // n, (i + 1) * CHUNKS[l + 1] // n)

        def before_by(l, ph, n):
            return (ph - n) % GROUP[l]

        def last(t):
            return isinstance(t, int) and t == T - 1

        def batch_of(t):
            return t // TPB

        def windows(l, r, m):
            wide = PER[l] * KEYS[l]
            return [(j, PADV + r - j * wide) for j in range(CHUNKS[l]) if r < (j + 1) * wide and j * wide < r + m]

        def rows_of(l, c):
            return min(P, 8 * KEYS[l] - P * c)

        def prep_counts(l):
            k = CHUNKS[l]
            g = HEADS[l] if l < 3 else 0
            return k, g, k, B * HALVES[l] * 2

        def value_bank(u):
            return 6 if u % 2 == 0 else 0

        def values_made(l):
            return PREP0[l] + sum(prep_counts(l)[:3])
        PREP0 = [sum(sum(prep_counts(m)) for m in range(l)) for l in range(5)]

        @block.sync
        def _(sp):
            sp.dma_start(CT[:, :], ctxT).then_inc(const_in, 16)
            sp.dma_start(CN[:, :], consts).then_inc(const_in, 16)
            sp.dma_start(BO[:, :], rows).then_inc(const_in, 16)
            sp.dma_start(MK[:, :], mask).then_inc(const_in, 16)
            sp.dma_start(AW[:, 0:2048], aw[0][:, 0:2048]).then_inc(const_in, 16)
            sp.dma_start(AW[:, 2048:4096], aw[0][:, 2048:4096]).then_inc(aw_in[0], 16)
            sp.dma_start(X[:, :, :], x.rearrange("(t p) d -> p t d", p=P)).then_inc(x_in, 16)
            sp.dma_start(FA[:, 0:F0["end"]], fw[0]).then_inc(fw_in[0], 16)
            sp.dma_start(FB[:, :], fw[1]).then_inc(fw_in[1], 16)
            sp.dma_start(FC[:, :], fw[3]).then_inc(fw_in[3], 16)
            sp.wait_ge(zero_made, 1)
            for l in (1, 3):
                n = SLOT_TILES[l]
                sp.dma_start(slots[l].rearrange("(e p j) d -> p e (j d)", p=P, j=n),
                             XS[:, 0, 0:n, :].rearrange("p j d -> p (j d)").unsqueeze(1).to_broadcast([P, E, n * ROW])).then_inc(slots_clear, 16)
                sp.dma_start(made[l].rearrange("(p n) d -> p n d", p=P),
                             XS[:, 0, 0, 0:D].unsqueeze(1).to_broadcast([P, 2 * T, D])).then_inc(slots_clear, 16)

            def expert_weights(l, e, k):
                n = WCOLS[l]
                sp.dma_start(WS[:, k, 0:n], ew[l].rearrange("(e p) n -> p e n", p=P)[:, e, :]).then_inc(ws_in[k], 16)

            def expert_slots(l, e, k):
                n = SLOT_TILES[l]
                sp.dma_start(XS[:, k, 0:n, :].rearrange("p j d -> p (j d)"),
                             slots[l].rearrange("(e p j) d -> p e (j d)", p=P, j=n)[:, e, :]).then_inc(xs_in[k], 16)

            def sparse_experts(l):
                G = len(GROUPS[l])
                g0 = GROUP0[l]
                for k in range(2):
                    expert_weights(l, k, k)
                sp.wait_ge(scattered, 16 * 2 * T * (ROUND[l] + 1))
                for k in range(2):
                    expert_slots(l, k, k)

                def pair(e0):
                    more = not (isinstance(e0, int) and e0 == E - 2)
                    for k in range(2):
                        e = e0 + k
                        if more:
                            sp.wait_ge(xs_turned, E * ROUND[l] + e + 1)
                            sp.wait_ge(ids_ready, E * ROUND[l] + e + 1)
                            expert_slots(l, e + 2, k)
                        if more:
                            sp.wait_ge(y_made, g0 + (e + 1) * G)
                            expert_weights(l, e + 2, k)
                in_expert_pairs(sp, pair)

            def outputs_back(l):
                for q in range(2):
                    sp.wait_ge(y_out[q], 16 * SLOT_TILES[1] * E // 2 + 16 * SLOT_TILES[3] * E // 2 * ROUND[l])
                for b in range(B):
                    for k in range(2):
                        sp.dma_start(RW[:, k, b * TPB:(b + 1) * TPB, 0:D],
                                     made[l].rearrange("(k t p) d -> p k t d", p=P, k=2)[:, k, b * TPB:(b + 1) * TPB, :]).then_inc(y_back[b], 16)

            for l in (1, 2):
                sp.wait_ge(p_mm, PREP0[l])
                sp.dma_start(AW[:, :], aw[l]).then_inc(aw_in[l], 16)
            sp.wait_ge(t_upd, T)
            sp.dma_start(FA[:, 0:F2["end"]], fw[2]).then_inc(fw_in[2], 16)
            sparse_experts(1)
            outputs_back(1)
            sp.wait_ge(p_mm, PREP0[3])
            sp.dma_start(AW[:, 0:512], aw[3]).then_inc(aw_in[3], 16)
            sparse_experts(3)
            outputs_back(3)
            for b in range(B):
                sp.wait_ge(x_acc, 2 * T + 2 * TPB * (b + 1))
                sp.dma_start(out.rearrange("(b t p) d -> p b t d", p=P, t=TPB)[:, b, :, :],
                             X[:, :, :].rearrange("p (b t) d -> p b t d", t=TPB)[:, b, :, :]).then_inc(stored, 16)
            sp.wait_ge(stored, 16 * B)

        @block.tensor
        def _(pe):
            mm = nc.tensor.matmul

            def keys(l, j):
                if j == 0:
                    if l == 0:
                        pe.wait_ge(const_in, 80)
                    else:
                        pe.wait_ge(aw_in[l], 16)
                        pe.wait_ge(sub_ready, UNIT0[l] - 1)
                wait(pe, p_ev, PREP0[l] + j - 1)
                mm(PS[:, j % 2, 0:B * NK], AW[0:CD, j * P:(j + 1) * P], CT[:, :], start=True, stop=True).then_inc(p_mm, 1)

            def prep(l, between):
                k, g, v, vw = prep_counts(l)
                n0 = PREP0[l]
                slot = [n0 + k]

                def bank():
                    pe.wait_ge(p_ev, slot[0] - 1)
                    slot[0] += 1
                    return 6 + (slot[0] - 1) % 2
                wide = 1024 if l < 3 else P
                if l == 0:
                    pe.wait_ge(aw_in[0], 16)
                if l < 3:
                    dh = P // PER[l]
                    for h in range(g):
                        j, r = h // PER[l], dh * (h % PER[l])
                        if h == 0:
                            pe.wait_ge(p_ev, n0 + k)
                            if l == 2:
                                pe.wait_ge(null_in, 1)
                        if h == g // 4:
                            between()
                        bk_ = bank()
                        n = B * NK + (l == 2)
                        mm(PS[:, bk_, 0:n], AW[r:r + dh, 2048 + j * P:2048 + (j + 1) * P], KV[r:r + dh, j, 0:n],
                           start=True, stop=True).then_inc(p_mm, 1)
                for j in range(v):
                    bk_ = bank()
                    mm(PS[:, bk_, 0:B * NK], AW[0:CD, wide + j * P:wide + (j + 1) * P], CT[:, :], start=True, stop=True).then_inc(p_mm, 1)
                if l == 3:
                    between()

            def project_values(l):
                n0 = values_made(l)
                if l == 1:
                    pe.wait_ge(t_upd, T)
                if l == 2:
                    pe.wait_ge(xts_ready, E)
                    pe.wait_ge(e_mul, UP2)
                if l == 3:
                    pe.wait_ge(e_mul, SLOT0[3])
                w0 = 3072 if l < 3 else 384
                bo_row = {0: 0, 1: 1, 3: 2}.get(l)
                for u in range(B * HALVES[l]):
                    hf = u % HALVES[l]
                    pe.wait_ge(vb_ready, BLOCKS0[l] + u + 1)
                    for i, part in enumerate(([0, 1, 2, 3], [4])):
                        pe.wait_ge(p_ev, n0 + max(0, 2 * (u - 2) + i + 1))
                        for c in part:
                            m = rows_of(l, c)
                            r = 8 * KEYS[l] * hf + P * c
                            ws = windows(l, r, m) if l < 3 else [(0, r)]
                            acc = PS[0:m, value_bank(u) + i, (c % 4) * P:(c % 4 + 1) * P]
                            bias = bo_row is not None and r == 0
                            for n, (j, col) in enumerate(ws):
                                lhs = VB[:, j, col:col + m] if l < 3 else VB3[:, col:col + m]
                                op = mm(acc, lhs, AW[:, w0 + j * P:w0 + (j + 1) * P], start=(n == 0), stop=(n == len(ws) - 1 and not bias))
                            if bias:
                                op = mm(acc, BO[0:1, 3 * P:4 * P], BO[0:1, bo_row * P:(bo_row + 1) * P], start=False, stop=True)
                        op.then_inc(p_mm, 1)

            def attention(l):
                H, K8 = HALVES[l], 8 * KEYS[l]
                t0, u0 = T * l, UNIT0[l]
                lag = LAG[l]
                pe.wait_ge(p_ev, PREP0[l + 1])
                if l == 2:
                    pe.wait_ge(mask_made, 1)
                if l == 3:
                    pe.wait_ge(gk_done, B)

                def transpose_x(t, ph):
                    par = ph % 2
                    pe.wait_ge(xn_ready, t0 + t + 1)
                    wait(pe, xtb_ready, t0 + t)
                    if l == 3:
                        wait(pe, qtb_ready, t)
                    mm(PS[:, 5, P:2 * P], XN[:, par, :], ident, is_transpose=True, start=True, stop=True).then_inc(xt_ready, 1)

                def query(t, ph):
                    par = ph % 2
                    pe.wait_ge(xtb_ready, t0 + t + 1)
                    mm(PS[:, 5, 2 * P:3 * P], AW[:, 256:384], XTB[:, par, :], start=True, stop=True).then_inc(q_ready, 1)

                def scores(t, ph, hf):
                    u, par = t * H + hf, ph % 2
                    lhs = XTB if l < 3 else QTB
                    if hf == 0:
                        if l < 3:
                            pe.wait_ge(xtb_ready, t0 + t + 1)
                        else:
                            pe.wait_ge(qtb_ready, t + 1)
                    wait(pe, sub_ready, u0 + u - 1)
                    bk_ = 2 * ((ph * H + hf) % 2)
                    flat = PS[:, bk_:bk_ + 2, :].rearrange("p a n -> p (a n)")
                    g = gview(l).rearrange("p b h k -> p b (h k)")[:, batch_of(t), (hf * K8):(hf * K8) + K8]
                    for a, z in ((0, 512), (512, K8)):
                        op = mm(flat[:, a:z], lhs[:, par, :], g[:, a:z], start=True, stop=(l != 2))
                        if l == 2:
                            mb = MB[:, :, :, :].rearrange("p b h k -> p b (h k)")[:, batch_of(t), a:z]
                            op = mm(flat[:, a:z], ONEB[:, :], mb, start=False, stop=True)
                    op.then_inc(score_ready, 1)

                def transpose_p(t, ph, hf, x_next):
                    u = t * H + hf
                    pe.wait_ge(prob_ready, u0 + u + 1)
                    wait(pe, pte_ready, u0 + u)
                    src = PR[:, ph * H + hf, :]
                    for c in range(4):
                        mm(PS[:, 4, c * P:(c + 1) * P], src[:, c * P:(c + 1) * P], ident, is_transpose=True,
                           start=True, stop=True)
                    x_next()
                    m = rows_of(l, 4)
                    mm(PS[0:m, 5, 0:P], src[:, 4 * P:4 * P + m], ident, is_transpose=True,
                       start=True, stop=True).then_inc(pt_ready, 1)

                def project(t, ph, hf):
                    u, par = t * H + hf, ph % 2
                    acc = PS[:, 6 + par, 0:D]
                    if hf == 0:
                        wait_from(pe, stats_done, T * (2 * l + 1), t - 1)
                    pe.wait_ge(pte_ready, u0 + u + 1)
                    for c in range(5):
                        m = rows_of(l, c)
                        end = hf == H - 1 and c == 4
                        op = mm(acc, PT[0:m, c, :], VW[0:m, batch_of(t), hf * 5 + c, :],
                                start=(hf == 0 and c == 0), stop=end)
                    if hf == H - 1:
                        op.then_inc(out_ready, 1)

                transpose_x(0, 0)
                if l == 3:
                    query(0, 0)

                def body(t, ph):
                    nxt, old = (ph + 1) % 2, before_by(l, ph, lag)
                    more = not last(t)
                    if isinstance(t, int) and t < lag:
                        if more:
                            transpose_x(t + 1, nxt)
                            if l == 3:
                                query(t + 1, nxt)
                        for hf in range(H):
                            scores(t, ph, hf)
                        return
                    for hf in range(H):
                        def x_next():
                            if not more:
                                pe.wait_ge(xtb_ready, t0 + T)
                                if l == 3:
                                    pe.wait_ge(qtb_ready, T)
                            if more and hf == 0:
                                transpose_x(t + 1, nxt)
                            if more and hf == 1:
                                pe.wait_ge(xtb_ready, t0 + t + 2)
                            if more and l == 3 and hf == 1:
                                query(t + 1, nxt)
                        transpose_p(t - lag, old, hf, x_next)
                        scores(t, ph, hf)
                        project(t - lag, old, hf)

                in_groups(pe, l, body)
                for t in range(T - lag, T):
                    for hf in range(H):
                        transpose_p(t, t % GROUP[l], hf, lambda: pe.wait_ge(xtb_ready, t0 + T))
                        for j in keys_between(l, t, hf):
                            keys(l + 1, j)
                        project(t, t % GROUP[l], hf)

            def front(l):
                pe.wait_ge(fw_in[l], 16)
                fbuf = {1: FB, 3: FC}.get(l, FA)

                def gates(b):
                    pe.wait_ge(f_xta, B * l + b + 1)
                    for t in range(b * TPB, (b + 1) * TPB):
                        op = mm(PS[:, 3, t * E:(t + 1) * E], XTA[:, t * P:(t + 1) * P], fbuf[:, 0:E], start=True, stop=True)
                    op.then_inc(f_gate, 1)

                for b in range(B):
                    pe.wait_ge(f_xn, T * l + (b + 1) * TPB)
                    if b >= 2:
                        pe.wait_ge(f_xta, B * l + b - 1)
                    for j in range(TPB):
                        t = b * TPB + j
                        op = mm(PS[:, 4 + b % 2, j * P:(j + 1) * P], RW[:, 0, t, 0:D], ident, is_transpose=True, start=True, stop=True)
                    op.then_inc(f_xt, 1)
                    if b:
                        gates(b - 1)
                gates(B - 1)

            def router(l):
                if l < 3:
                    pe.wait_ge(p_ev, PREP0[l + 1] + CHUNKS[l + 1])
                if l in (1, 3):
                    m = RT[:, 5, :, :].rearrange("p t e -> p (t e)")
                    pe.wait_ge(r_count, l)
                    mm(PS[:, 0, 0:T * E], before, m, start=True, stop=True)
                    mm(PS[:, 1, 0:T * E], ones, m, start=True, stop=True).then_inc(r_sums, 1)
                if l == 2:
                    pe.wait_ge(r_count, 2)
                    m = RT[:, 5:7, :, :].rearrange("p a t e -> p (a t e)")
                    mm(PS[:, 0, 0:2 * T * E], ones, m, start=True, stop=True).then_inc(r_sums, 1)

            def experts0():
                pe.wait_ge(p_ev, values_made(1))
                pe.wait_ge(r_done, 1)
                pe.wait_ge(up_halves, 2)

                def up(t, par, g):
                    n = t * 3 + g
                    if g == 0:
                        pe.wait_ge(t_split, t + 1)
                    wait(pe, t_mul, n - 1)
                    q = (par * 3 + g) % 2
                    for i in range(2):
                        w = g * 768 + i * 384
                        acc = PS[:, 2 * q + i, 0:384]
                        mm(acc, XH[:, par, :], UH[:, w:w + 384], start=True, stop=False)
                        mm(acc, XH[:, par, :], UL[:, w:w + 384], start=False, stop=False)
                        op = mm(acc, XL[:, par, :], UH[:, w:w + 384], start=False, stop=True)
                    op.then_inc(t_up, 1)

                def turn(t, par, g):
                    n = t * 3 + g
                    q = (par * 3 + g) % 2
                    pe.wait_ge(t_mul, n + 1)
                    wait(pe, t_ev, n)
                    for k in range(3):
                        op = mm(PS[:, 4, k * P:(k + 1) * P], HS[:, q, k * P:(k + 1) * P], ident, is_transpose=True, start=True, stop=True)
                    op.then_inc(t_tr, 1)

                def down(t, par, g):
                    n = t * 3 + g
                    if g == 0:
                            wait_from(pe, stats_done, 2 * T, t - 1)
                    pe.wait_ge(t_ev, n + 1)
                    for k in range(3):
                        e = g * 3 + k
                        op = mm(PS[:, 6 + par, 0:D], PT[:, k, :], FA[:, F0["down"] + e * P:F0["down"] + (e + 1) * P],
                                start=(e == 0), stop=(e == EB - 1))
                    if g == 2:
                        op.then_inc(t_out, 1)

                def before_by_two(t, par, g):
                    return (t, par, 0) if g == 2 else (t - 1, 1 - par, g + 1)

                def body(t, par):
                    for g in range(3):
                        late = not (isinstance(t, int) and t == 0 and g < 2)
                        if late:
                            turn(*before_by_two(t, par, g))
                        up(t, par, g)
                        if late:
                            down(*before_by_two(t, par, g))
                in_pairs(pe, body)
                for g in (1, 2):
                    turn(T - 1, 1, g)
                    down(T - 1, 1, g)

            def fallback():
                pe.wait_ge(f_xta, B * 2)
                pe.wait_ge(r_done, 2)
                pe.wait_ge(wn_done, 2)

                def down(b):
                    pe.wait_ge(e_mul, b + 1)
                    wait(pe, e_acc, b - 1)
                    for j in range(TPB):
                        op = mm(PS[:, 4 + b % 2, j * P:(j + 1) * P], HS[:, b % 2, j * P:(j + 1) * P],
                                FB[:, F1["down"]:F1["down"] + P], start=(j == 0), stop=True, skip_group_check=True)
                    op.then_inc(e_down, 1)

                for b in range(B):
                    wait(pe, e_mul, b - 1)
                    rhs = XTA[:, b * S:(b + 1) * S]
                    mm(PS[:, b % 2, :], FB[:, F1["g"]:F1["g"] + P], rhs, start=True, stop=True)
                    mm(PS[:, 2 + b % 2, :], FB[:, F1["u"]:F1["u"] + P], rhs, start=True, stop=True).then_inc(e_up, 1)
                    if b:
                        down(b - 1)
                down(B - 1)

            def experts2():
                plan, n0, q0 = PLAN2, UP2, DOWN2
                N, Q = len(plan), EB
                pe.wait_ge(f_xta, B * 3)
                pe.wait_ge(r_done, 3)

                pe.wait_ge(w2_halves, 2)
                pe.wait_ge(x2_halves, 2 * B)

                def up(b0, m):
                    b, c = b0 + m // N, plan[m % N][0]
                    pe.wait_ge(e_mul, n0 + b0 * N + m - 1)
                    x_hi, x_lo = HI2[:, bass.ds(b * S, S)], XAL[:, bass.ds(b * S, S)]
                    for bank, w in ((m % 2, c * P), (2 + m % 2, F2["u"] - F2["g"] + c * P)):
                        w_hi = HI2[:, NTOK + w:NTOK + w + P]
                        mm(PS[:, bank, :], w_hi, x_hi, start=True, stop=False)
                        mm(PS[:, bank, :], w_hi, x_lo, start=False, stop=False)
                        op = mm(PS[:, bank, :], W2L[:, w:w + P], x_hi, start=False, stop=True)
                    op.then_inc(e_up, 1)

                def down(b0, m):
                    c, downs = plan[m % N]
                    pe.wait_ge(e_mul, n0 + b0 * N + m + 1)
                    for e, lo, hi in downs:
                        i = m // N * Q + e
                        pe.wait_ge(e_acc, q0 + b0 * Q + i - 1)
                        for j in range(TPB):
                            op = mm(PS[:, 4 + i % 2, j * P:(j + 1) * P], HS[lo:hi, m % 2, j * P:(j + 1) * P],
                                    FA[lo:hi, F2["down"] + c * P:F2["down"] + (c + 1) * P],
                                    start=(j == 0), stop=True, skip_group_check=True)
                        op.then_inc(e_down, 1)

                with pe.Fori(0, B // 2) as i:
                    for m in range(2 * N):
                        up(2 * i, m)
                        if m:
                            down(2 * i, m - 1)
                    down(2 * i, 2 * N - 1)

            def sparse_experts(l):
                G, N, H = len(GROUPS[l]), STEPS[l], HID[l]
                steps, r = steps_of(l), ROUND[l]
                n0, g0 = SLOT0[l], GROUP0[l]
                pe.wait_ge(r_done, l + 1)
                if l == 1:
                    pe.wait_ge(p_ev, values_made(2))

                def turn(e, k):
                    pe.wait_ge(xs_in[k], 16 * (E // 2 * r + (e - k) // 2 + 1) if isinstance(e, int) else 8 * (e - k) + 16 * (E // 2 * r + 1))
                    wait(pe, xts_ready, E * r + e)
                    for g, n in enumerate(GROUPS[l]):
                        for j in range(n):
                            op = mm(PS[:, 6 + (g if G == 2 else k), j * P:(j + 1) * P], XS[:, k, sum(GROUPS[l][:g]) + j, 0:D], ident,
                                    is_transpose=True, start=True, stop=True)
                    op.then_inc(xs_turned, 1)

                def up(e, k, n):
                    g, tiles, before, c = steps[n]
                    q = (k * N + n) % 2
                    if n == 0 and l == 3:
                        pe.wait_ge(x3_split, e + 1)
                        pe.wait_ge(w3_split, e + 1)
                    elif n == 0:
                        pe.wait_ge(xts_ready, E * r + e + 1)
                        pe.wait_ge(ws_in[k], 16 * (E // 2 * r + (e - k) // 2 + 1) if isinstance(e, int) else 8 * (e - k) + 16 * (E // 2 * r + 1))
                    wait(pe, e_mul, n0 + e * N + n - 1)
                    cols = slice(before * P, (before + tiles) * P)
                    if l == 3:
                        for bank, w in ((q, c * P), (2 + q, (H + c) * P)):
                            acc = PS[:, bank, 0:tiles * P]
                            mm(acc, WH3[:, k, w:w + P], XH3[:, k, cols], start=True, stop=False)
                            mm(acc, WH3[:, k, w:w + P], XL3[:, k, cols], start=False, stop=False)
                            op = mm(acc, WL3[:, k, w:w + P], XH3[:, k, cols], start=False, stop=True)
                        op.then_inc(e_up, 1)
                        return
                    rhs = XTS[:, k, cols]
                    mm(PS[:, q, 0:tiles * P], WS[:, k, c * P:(c + 1) * P], rhs, start=True, stop=True)
                    mm(PS[:, 2 + q, 0:tiles * P], WS[:, k, (H + c) * P:(H + c + 1) * P], rhs, start=True, stop=True).then_inc(e_up, 1)

                def down(e, k, n):
                    g, tiles, before, c = steps[n]
                    q = (k * N + n) % 2
                    pe.wait_ge(e_mul, n0 + e * N + n + 1)
                    if c == 0:
                        wait(pe, ys_ready, g0 + e * G + g - 1)
                    for j in range(tiles):
                        op = mm(PS[:, 4 + (k * G + g) % 2, j * P:(j + 1) * P], HS[:, q, j * P:(j + 1) * P],
                                WS[:, k, (2 * H + c) * P:(2 * H + c + 1) * P],
                                start=(c == 0 and j == 0), stop=(c == H - 1), skip_group_check=True)
                    if c == H - 1:
                        op.then_inc(y_made, 1)

                def pair(e0):
                    more = not (isinstance(e0, int) and e0 == E - 2)
                    for k in range(2):
                        for n in range(N):
                            up(e0 + k, k, n)
                            if n == turn_at(l) and (k == 0 or more):
                                turn(e0 + k + 1, 1 - k)
                            if n:
                                down(e0 + k, k, n - 1)
                            elif k:
                                down(e0, 0, N - 1)
                    down(e0 + 1, 1, N - 1)
                turn(0, 0)
                in_expert_pairs(pe, pair)

            for j in range(CHUNKS[0]):
                keys(0, j)
            prep(0, lambda: None)
            project_values(0)
            for l in range(4):
                attention(l)
                front(l)
                if l < 3:
                    prep(l + 1, lambda: router(l))
                else:
                    router(l)
                if l == 0:
                    experts0()
                if l == 1:
                    fallback()
                if l == 2:
                    experts2()
                if l in (1, 3):
                    sparse_experts(l)
                if l < 3:
                    project_values(l + 1)

        @block.scalar
        def _(act):
            A = nc.scalar.activation

            def take(l, dst, src, bias):
                if l == 3:
                    return A(dst, src, ACT.Identity, bias=bias)
                return A(dst, src, ACT.Copy)

            def keys(l, j):
                if j == 0 and l > 0:
                    act.wait_ge(vb_ready, BLOCKS0[l])
                act.wait_ge(p_mm, PREP0[l] + j + 1)
                take(l, KV[:, j, 0:B * NK], PS[:, j % 2, 0:B * NK], bk).then_inc(p_ev, 1)

            def prep(l):
                k, g, v, vw = prep_counts(l)
                slot = [PREP0[l] + k]

                def bank():
                    slot[0] += 1
                    act.wait_ge(p_mm, slot[0])
                    return 6 + (slot[0] - 1) % 2
                for h in range(g):
                    b_ = bank()
                    o = 1 if l == 2 else 0
                    dst = gview(l)[:, :, h, o:o + NK]
                    src = PS[:, b_, 0:B * NK].rearrange("p (b k) -> p b k", k=NK)
                    if l == 2:
                        A(dst, src, ACT.Copy, scale=gcol[:, 0:1])
                        A(gview(l)[:, :, h, 0:1], PS[:, b_, B * NK:B * NK + 1].unsqueeze(1).to_broadcast([P, B, 1]),
                          ACT.Copy, scale=gcol[:, 0:1]).then_inc(p_ev, 1)
                    else:
                        A(dst, src, ACT.Copy, scale=float(SCALE[l])).then_inc(p_ev, 1)
                for j in range(v):
                    b_ = bank()
                    take(l, KV[:, 1 if l == 3 else j, 0:B * NK], PS[:, b_, 0:B * NK], bv).then_inc(p_ev, 1)

            def blocks(l, b, hf):
                J, dh = CHUNKS[l] // HALVES[l], P // PER[l]
                for hh in range(PER[l]):
                    r, c = dh * hh, PADV + hh * KEYS[l] + (l == 2)
                    op = A(VB[r:r + dh, hf * J:(hf + 1) * J, c:c + NK], KV[r:r + dh, hf * J:(hf + 1) * J, b * NK:(b + 1) * NK], ACT.Copy)
                op.then_inc(vb_ready, 1)

            def first_blocks(l):
                act.wait_ge(vb_zero, l + 1)
                if l == 2:
                    act.wait_ge(null_in, 3)
                act.wait_ge(p_ev, values_made(l))
                for hf in range(HALVES[l]):
                    blocks(l, 0, hf)

            def project_values(l):
                n0, H = values_made(l), HALVES[l]
                for u in range(B * H):
                    b, hf, bank_ = u // H, u % H, value_bank(u)
                    act.wait_ge(p_mm, n0 + 2 * u + 1)
                    A(VW[:, b, hf * 5:hf * 5 + 4, :], PS[:, bank_, :].rearrange("p (c d) -> p c d", d=D), ACT.Copy).then_inc(p_ev, 1)
                    act.wait_ge(p_mm, n0 + 2 * u + 2)
                    if b < B - 1 and l < 3:
                        blocks(l, b + 1, hf)
                    m = rows_of(l, 4)
                    A(VW[0:m, b, hf * 5 + 4, :], PS[0:m, bank_ + 1, 0:D], ACT.Copy).then_inc(p_ev, 1)

            def attention(l):
                H = HALVES[l]
                t0, u0 = T * l, UNIT0[l]

                def x_norm(t, par):
                    A(XN[:, par, :], X[:, t, :], ACT.Identity, bias=SM[:, 4, at(t, 1)], scale=SM[:, 10, at(t, 1)]).then_inc(xn_ready, 1)

                def x_out(t, par):
                    act.wait_ge(xt_ready, t0 + t + 1)
                    if l < 3:
                        wait(act, score_ready, u0 + (t - 1) * H)
                    else:
                        wait(act, q_ready, t - 1)
                    A(XTB[:, par, :], PS[:, 5, P:2 * P], ACT.Copy).then_inc(xtb_ready, 1)

                def q_out(t, par):
                    act.wait_ge(q_ready, t + 1)
                    wait(act, score_ready, u0 + (t - 1) * H)
                    A(QTB[:, par, :], PS[:, 5, 2 * P:3 * P], ACT.Identity, bias=bq).then_inc(qtb_ready, 1)

                def p_out(t, hf):
                    act.wait_ge(pt_ready, u0 + t * H + hf + 1)
                    A(PT[:, 0:4, :], PS[:, 4, :].rearrange("p (c n) -> p c n", n=P), ACT.Copy)
                    m = rows_of(l, 4)
                    A(PT[0:m, 4, :], PS[0:m, 5, 0:P], ACT.Copy).then_inc(pte_ready, 1)

                def expo(t, ph, hf):
                    u = t * H + hf
                    act.wait_ge(sub_ready, u0 + u + 1)
                    p = prview(l, ph * H + hf)
                    A(p, p, ACT.Exp).then_inc(exp_ready, 1)

                act.wait_ge(shift_ready, l + 1)
                x_norm(0, 0)
                x_norm(1, 1)
                x_out(0, 0)
                if l == 3:
                    q_out(0, 0)

                lag = LAG[l]

                def body(t, ph):
                    nxt = (ph + 1) % 2
                    first = isinstance(t, int) and t == 0
                    for hf in range(H):
                        if not (isinstance(t, int) and t < lag):
                            p_out(t - lag, hf)
                        if hf == 0 and not last(t):
                            x_out(t + 1, nxt)
                        if hf == 0 and not (isinstance(t, int) and t >= T - 2):
                            x_norm(t + 2, ph % 2)
                        if l == 3 and (hf == 1 or first) and not last(t) and not (first and hf == 1):
                            q_out(t + 1, nxt)
                        if hf:
                            expo(t, ph, hf - 1)
                        elif not first:
                            expo(t - 1, before_by(l, ph, 1), H - 1)
                in_groups(act, l, body)
                expo(T - 1, GROUP[l] - 1, H - 1)
                for t in range(T - lag, T):
                    for hf in range(H):
                        p_out(t, hf)
                        for j in keys_between(l, t, hf):
                            keys(l + 1, j)

            def front(l):
                if l == 3:
                    act.wait_ge(fw_in[3], 16)
                for b in range(B):
                    act.wait_ge(f_xt, B * l + b + 1)
                    dst = XTA[:, b * S:(b + 1) * S]
                    if l == 3:
                        A(dst, PS[:, 4 + b % 2, :], ACT.Identity, bias=beta, scale=gamma).then_inc(f_xta, 1)
                    else:
                        A(dst, PS[:, 4 + b % 2, :], ACT.Copy).then_inc(f_xta, 1)

            def router(l):
                if l == 0:
                    act.wait_ge(f_gate, B)
                    A(RT[:, 0, :, :], PS[:, 3, 0:T * E].rearrange("p (t e) -> p t e", e=E), ACT.Exp, scale=-1.0).then_inc(r_exp, 1)
                else:
                    act.wait_ge(r_logit, l)
                    if l == 3:
                        A(SM[:, 12, :], SM[:, 12, :], ACT.Exp).then_inc(r_exp, 1)
                    else:
                        A(RT[:, 0, :, :], RT[:, 0, :, :], ACT.Exp, scale=(1.0 if l == 1 else -1.0)).then_inc(r_exp, 1)

            def experts0():
                def gate(t, par, g):
                    n = t * 3 + g
                    q = (par * 3 + g) % 2
                    act.wait_ge(t_up, n + 1)
                    wait(act, t_mul, n - 1)
                    for k in range(3):
                        op = A(GS[:, q, k * P:(k + 1) * P], PS[:, 2 * q, k * P:(k + 1) * P], ACT.Silu,
                               scale=S9[:, t, g * 3 + k:g * 3 + k + 1])
                    op.then_inc(t_act, 1)

                def ev(t, par, g):
                    n = t * 3 + g
                    act.wait_ge(t_tr, n + 1)
                    A(PT[:, 0:3, :], PS[:, 4, 0:384].rearrange("p (c n) -> p c n", n=P), ACT.Copy).then_inc(t_ev, 1)

                act.wait_ge(r_done, 1)

                def body(t, par):
                    for g in range(3):
                        if not (isinstance(t, int) and t == 0 and g < 2):
                            ev(*((t, par, 0) if g == 2 else (t - 1, 1 - par, g + 1)))
                        gate(t, par, g)
                in_pairs(act, body)
                ev(T - 1, 1, 1)
                ev(T - 1, 1, 2)

            def fallback():
                for b in range(B):
                    act.wait_ge(e_up, b + 1)
                    wait(act, e_mul, b - 1)
                    A(GS[:, b % 2, :], PS[:, b % 2, :], ACT.Gelu).then_inc(e_act, 1)

            def experts2():
                n0, N = UP2, len(PLAN2)
                with act.Fori(0, B // 2) as i:
                    for m in range(2 * N):
                        n = n0 + i * (2 * N) + m
                        act.wait_ge(e_up, n + 1)
                        act.wait_ge(e_mul, n - 1)
                        A(GS[:, m % 2, :], PS[:, m % 2, :], ACT.Silu).then_inc(e_act, 1)

            def sparse_experts(l):
                G, N = len(GROUPS[l]), STEPS[l]
                steps, r = steps_of(l), ROUND[l]
                n0, g0 = SLOT0[l], GROUP0[l]

                def turned(e, k):
                    act.wait_ge(xs_turned, E * r + e + 1)
                    wait(act, e_up, n0 + (e - 1) * N)
                    for g, tiles in enumerate(GROUPS[l]):
                        before = sum(GROUPS[l][:g])
                        dst = XTS[:, k, before * P:(before + tiles) * P]
                        src = PS[:, 6 + (g if G == 2 else k), 0:tiles * P]
                        if l == 1:
                            op = A(dst, src, ACT.Copy, scale=FB[:, at(F1["norm"] + e, 1)])
                        else:
                            op = A(dst, src, ACT.Identity, bias=beta, scale=gamma)
                    op.then_inc(xts_ready, 1)

                def gate(e, k, n):
                    tiles, q = steps[n][1], (k * N + n) % 2
                    act.wait_ge(e_up, n0 + e * N + n + 1)
                    wait(act, e_mul, n0 + e * N + n - 1)
                    A(GS[:, q, 0:tiles * P], PS[:, q, 0:tiles * P], ACT.Gelu if l == 1 else ACT.Silu).then_inc(e_act, 1)

                def output(e, k, n):
                    g, tiles, before, c = steps[n]
                    if c < HID[l] - 1:
                        return
                    act.wait_ge(y_made, g0 + e * G + g + 1)
                    wait(act, y_out[k], outputs_written(l, k, e - 2))
                    y0 = output_buffer(l, k, g)
                    A(YS[:, y0:y0 + tiles, :], PS[:, 4 + (k * G + g) % 2, 0:tiles * P].rearrange("p (j d) -> p j d", d=D), ACT.Copy).then_inc(ys_ready, 1)

                def pair(e0):
                    more = not (isinstance(e0, int) and e0 == E - 2)
                    for k in range(2):
                        for n in range(N):
                            gate(e0 + k, k, n)
                            if n == turn_at(l) and (k == 0 or more):
                                turned(e0 + k + 1, 1 - k)
                            if n:
                                output(e0 + k, k, n - 1)
                            elif k:
                                output(e0, 0, N - 1)
                    output(e0 + 1, 1, N - 1)
                turned(0, 0)
                in_expert_pairs(act, pair)

            act.wait_ge(const_in, 80)
            A(gcol[:, 0:1], g_norm, ACT.Copy, scale=float(SCALE[2])).then_inc(zeroed, 1)
            act.wait_ge(zeroed, 1)
            for j in range(CHUNKS[0]):
                keys(0, j)
            prep(0)
            first_blocks(0)
            project_values(0)
            for l in range(4):
                attention(l)
                front(l)
                router(l)
                if l < 3:
                    prep(l + 1)
                if l < 2:
                    first_blocks(l + 1)
                if l == 0:
                    experts0()
                if l == 1:
                    fallback()
                if l == 2:
                    experts2()
                if l in (1, 3):
                    sparse_experts(l)
                if l < 3:
                    project_values(l + 1)

        @block.gpsimd
        def _(pool):
            g = nc.gpsimd
            def powers(stage, part):
                a, z = PARTS[stage][part]
                pool.wait_ge(var_ready, PART0[stage] + part + 1)
                g.tensor_tensor(SM[:, 10, a:z], SM[:, 6, a:z], NH[:, a:z], ALU.pow).then_inc(pow_ready, 1)
                if stage == 3:
                    g.tensor_tensor(SM[:, 8, a:z], SM[:, 7, a:z], NH[:, a:z], ALU.pow).then_inc(first_ready, 1)

            def prep(l):
                if l < 3:
                    wait(pool, p_ev, PREP0[l])
                    g.memset(VB[:, :, :], 0.0).then_inc(vb_zero, 1)
                    pool.wait_ge(vb_zero, l + 1)
                if l == 2:
                    pool.wait_ge(vb_ready, BLOCKS0[2])
                    g.tensor_copy(KV[:, :, B * NK:B * NK + 1], null_k.unsqueeze(1).to_broadcast([P, 8, 1])).then_inc(null_in, 1)
                    pool.wait_ge(null_in, 1)
                    for hh in range(2):
                        r = 64 * hh
                        c = PADV + hh * KEYS[2]
                        g.tensor_copy(VB[r:r + 64, :, c:c + 1], CN[r:r + 64, C_COL + 2:C_COL + 3].unsqueeze(1).to_broadcast([64, 8, 1])).then_inc(null_in, 1)
                        pool.wait_ge(null_in, 2 + hh)
                if l == 1:
                    pool.wait_ge(fw_in[1], 16)
                    for o in (F1["g"], F1["u"]):
                        w = FB[:, o:o + P]
                        g.tensor_scalar(w, w, FB[:, F1["norm"] + E:F1["norm"] + EB], None, ALU.mult).then_inc(wn_done, 1)
                if l == 3:
                    g.tensor_scalar(BMS[:, :], headmask, float(SCALE[3]), None, ALU.mult).then_inc(bms_made, 1)
                    pool.wait_ge(bms_made, 1)
                    pool.wait_ge(p_ev, PREP0[3] + 1)
                    for b in range(B):
                        g.tensor_tensor(gview(3)[:, b, :, :], KV[:, 0, b * NK:(b + 1) * NK].unsqueeze(1).to_broadcast([P, 16, NK]),
                                        BMS[:, :].unsqueeze(2).to_broadcast([P, 16, NK]), ALU.mult).then_inc(gk_done, 1)

            def blocks3():
                pool.wait_ge(p_ev, values_made(3))
                w = 8 * NK
                for b in range(B):
                    for hf in range(2):
                        if b:
                            pool.wait_ge(p_mm, values_made(3) + ((b - 1) * 2 + hf + 1) * 2)
                        g.tensor_tensor(VB3[:, hf * w:(hf + 1) * w].rearrange("p (h k) -> p h k", k=NK),
                                        KV[:, 1, b * NK:(b + 1) * NK].unsqueeze(1).to_broadcast([P, 8, NK]),
                                        headmask[:, 8 * hf:8 * hf + 8].unsqueeze(2).to_broadcast([P, 8, NK]), ALU.mult).then_inc(vb_ready, 1)

            def attention(l):
                H, lag = HALVES[l], LAG[l]
                u0 = UNIT0[l]

                def normalise(t, ph, hf):
                    u = t * H + hf
                    q = (ph * H + hf) % 2
                    pool.wait_ge(inv_ready, u0 + u + 1)
                    p = prview(l, ph * H + hf)
                    g.tensor_tensor(p, p, RI[:, q, :].unsqueeze(2).to_broadcast([P, 8, KEYS[l]]), ALU.mult).then_inc(prob_ready, 1)

                def o_pow(t, par):
                    pool.wait_ge(o_eps, t + 1)
                    g.tensor_tensor(OR[:, par, :], OE[:, par, :], NH[:, 0:1], ALU.pow).then_inc(o_rstd, 1)

                def body(t, ph):
                    if l == 2 and not (isinstance(t, int) and t <= lag):
                        o_pow(t - lag - 1, (ph + 1) % 2)
                    for hf in range(H):
                        normalise(t, ph, hf)
                in_groups(pool, l, body)
                powers(2 * l + 1, 0)
                if l == 2:
                    for t in range(T - lag - 1, T):
                        o_pow(t, t % 2)

            def experts0():
                def body(t, par):
                    wait(pool, t_up, 3 * (t - 1))
                    src = XTA[:, at(t * P, P)]
                    g.tensor_copy(XTB[:, par, :], src).then_inc(t_in, 1)
                    g.tensor_copy(XH[:, par, :], src).then_inc(t_in, 1)
                    pool.wait_ge(t_in, 2 * t + 2)
                    g.tensor_tensor(XL[:, par, :], XTB[:, par, :], XH[:, par, :], ALU.subtract).then_inc(t_split, 1)
                pool.wait_ge(f_xta, B)
                in_pairs(pool, body)

            def split_weights():
                pool.wait_ge(fw_in[0], 16)
                g.tensor_copy(UH[:, :], up0).then_inc(up_halves, 1)
                pool.wait_ge(up_halves, 1)
                g.tensor_tensor(UL[:, :], up0, UH[:, :], ALU.subtract).then_inc(up_halves, 1)

            def split_weights2():
                pool.wait_ge(fw_in[2], 16)
                for q in range(2):
                    pool.wait_ge(y_out[q], 16 * SLOT_TILES[1] * E // 2)
                w, hi = FA[:, F2["g"]:F2["down"]], HI2[:, NTOK:NTOK + F2["down"] - F2["g"]]
                g.tensor_copy(hi, w).then_inc(w2_halves, 1)
                pool.wait_ge(w2_halves, 1)
                g.tensor_tensor(W2L[:, :], w, hi, ALU.subtract).then_inc(w2_halves, 1)

            def split_input2():
                for b in range(B):
                    pool.wait_ge(f_gate, B * 2 + b + 1)
                    x_b, hi = XTA[:, b * S:(b + 1) * S], HI2[:, b * S:(b + 1) * S]
                    g.tensor_copy(hi, x_b).then_inc(x2_halves, 1)
                    pool.wait_ge(x2_halves, 2 * b + 1)
                    g.tensor_tensor(XAL[:, b * S:(b + 1) * S], x_b, hi, ALU.subtract).then_inc(x2_halves, 1)

            def split_expert(e):
                k = e % 2
                pool.wait_ge(ws_in[k], 16 * (E // 2 * ROUND[3] + e // 2 + 1))
                w = WS[:, k, 0:SPLIT3]
                g.tensor_copy(WH3[:, k, :], w).then_inc(w3_hi, 1)
                pool.wait_ge(w3_hi, e + 1)
                g.tensor_tensor(WL3[:, k, 0:SPLIT3], w, WH3[:, k, :], ALU.subtract).then_inc(w3_split, 1)

            def scatter(l):
                for b in range(B):
                    pool.wait_ge(f_xn, T * l + (b + 1) * TPB)
                    g.tensor_copy(RW[:, 1, b * TPB:(b + 1) * TPB, 0:D], RW[:, 0, b * TPB:(b + 1) * TPB, 0:D]).then_inc(rows_copied, 1)
                if l == 3:
                    pool.wait_ge(e_down, DOWN2 + B * EB)
                    split_expert(0)
                pool.wait_ge(slots_clear, 64)
                pool.wait_ge(r_idx, ROUND[l] + 1)
                pool.wait_ge(rows_copied, B * (ROUND[l] + 1))
                for t in range(T):
                    for k in range(2):
                        i = k * T + t
                        g.indirect_dma_start(slots[l], bass.IndirectOffsetOnAxis(ap=IX[:, i:i + 1], axis=0), RW[:, k, t, :], None,
                                             bounds_check=E * CAP[l] - 1, oob_is_err=False).then_inc(scattered, 16)

            def write_outputs(l):
                G, r = len(GROUPS[l]), ROUND[l]

                for e in range(E):
                    k = e % 2
                    if l == 3 and e < E - 1:
                        split_expert(e + 1)
                    pool.wait_ge(ids_ready, E * r + e + 1)
                    for n, tiles in enumerate(GROUPS[l]):
                        pool.wait_ge(ys_ready, GROUP0[l] + e * G + n + 1)
                        for j in range(tiles):
                            i = sum(GROUPS[l][:n]) + j
                            g.indirect_dma_start(made[l], bass.IndirectOffsetOnAxis(ap=ID[:, k, i:i + 1], axis=0),
                                                 YS[:, output_buffer(l, k, n) + j, :], None,
                                                 bounds_check=2 * NTOK - 1, oob_is_err=False).then_inc(y_out[k], 16)

            g.memset(XS[:, 0, :, :], 0.0).then_inc(xs_blank, 1)
            g.memset(NH[:, :], -0.5).then_inc(nh_made, 1)
            pool.wait_ge(nh_made, 1)
            pool.wait_ge(const_in, 80)
            pool.wait_ge(xs_blank, 1)
            g.tensor_scalar(XS[:, 0, :, D], CN[:, C_SPARE:C_SPARE + SLOT_TILES[3]], float(2 * NTOK), None, ALU.add).then_inc(zero_made, 1)
            g.tensor_copy(RW[:, :, :, D], spare).then_inc(ids_set, 1)
            pool.wait_ge(ids_set, 1)
            prep(0)
            for l in range(4):
                if l == 2:
                    split_weights2()
                powers(2 * l, 0)
                if l == 0:
                    split_weights()
                attention(l)
                powers(2 * l + 1, 1)
                if l == 2:
                    split_input2()
                if l < 3:
                    prep(l + 1)
                if l == 0:
                    experts0()
                if l == 2:
                    blocks3()
                if l in (1, 3):
                    scatter(l)
                    write_outputs(l)

        @block.vector
        def _(dve):
            v = nc.vector
            links = [0]

            def link(op):
                links[0] += 1
                op.then_inc(r_chain, 1)
                dve.wait_ge(r_chain, links[0])

            def tt(o, a, b_, op):
                return v.tensor_tensor(o, a, b_, op)

            def ts(o, a, s1, s2, op0, op1=None):
                return v.tensor_scalar(o, a, s1, s2, op0, op1) if op1 is not None else v.tensor_scalar(o, a, s1, s2, op0)

            def variances(stage, part):
                a, z = PARTS[stage][part]
                dve.wait_ge(stats_done, T * stage + z)
                m0, m1, q0, q1 = (ST[:, a:z, i] for i in (1, 4, 2, 5))
                sm = [SM[:, i, a:z] for i in range(16)]
                link(tt(sm[1], m0, m1, ALU.add))
                link(tt(sm[2], q0, q1, ALU.add))
                link(tt(sm[3], m0, m1, ALU.subtract))
                link(tt(sm[3], sm[3], sm[3], ALU.mult))
                link(ts(sm[0], sm[1], 0.5, None, ALU.mult))
                link(ts(sm[2], sm[2], 1.0 / D, None, ALU.mult))
                link(v.scalar_tensor_tensor(out=sm[5], in0=sm[3], scalar=0.25, in1=sm[2], op0=ALU.mult, op1=ALU.add))
                if stage not in TWICE:
                    v.tensor_scalar(sm[6], sm[5], LN_EPS, None, ALU.add).then_inc(var_ready, 1)
                else:
                    link(ts(sm[7], sm[5], LN_EPS, None, ALU.add))
                    v.scalar_tensor_tensor(out=sm[6], in0=sm[7], scalar=RMS_EPS if stage == 3 else LN_EPS, in1=sm[5],
                                           op0=ALU.mult, op1=ALU.add).then_inc(var_ready, 1)

            def deviations(l):
                variances(2 * l, 0)
                dve.wait_ge(pow_ready, PART0[2 * l] + 1)
                v.scalar_tensor_tensor(out=SM[:, 4, :], in0=SM[:, 0, :], scalar=-1.0, in1=SM[:, 10, :],
                                       op0=ALU.mult, op1=ALU.mult).then_inc(shift_ready, 1)

            def front(l, part):
                stage = 2 * l + 1
                a, z = PARTS[stage][part]
                dve.wait_ge(pow_ready, PART0[stage] + part + 1)
                if l == 2 and part == 0:
                    dve.wait_ge(x_acc, 2 * T)
                for t in range(a, z):
                    v.tensor_scalar(RW[:, 0, t, 0:D], X[:, t, :], SM[:, 0, t:t + 1], SM[:, 10, t:t + 1],
                                    ALU.subtract, ALU.mult).then_inc(f_xn, 1)

            def stats(t):
                v.bn_stats(ST[:, t, :], X[:, t, :]).then_inc(stats_done, 1)

            def attention(l):
                H = HALVES[l]
                t0, u0 = T * l, UNIT0[l]
                K8 = 8 * KEYS[l]

                def scored(q):
                    return PS[:, 2 * q:2 * q + 2, :].rearrange("p a n -> p (a n)")[:, 0:K8].rearrange("p (h k) -> p h k", k=KEYS[l])

                def largest(t, ph, hf):
                    u, q = t * H + hf, (ph * H + hf) % 2
                    dve.wait_ge(score_ready, u0 + u + 1)
                    v.tensor_reduce(MX[:, q, :], scored(q), AX.X, ALU.max).then_inc(max_ready, 1)

                def shift(t, ph, hf):
                    u, q = t * H + hf, (ph * H + hf) % 2
                    dve.wait_ge(max_ready, u0 + u + 1)
                    wait(dve, pt_ready, u0 + u - 3)
                    v.tensor_tensor(prview(l, ph * H + hf), scored(q), MX[:, q, :].unsqueeze(2).to_broadcast([P, 8, KEYS[l]]),
                                    ALU.subtract).then_inc(sub_ready, 1)

                def total(t, ph, hf):
                    u, q = t * H + hf, (ph * H + hf) % 2
                    dve.wait_ge(exp_ready, u0 + u + 1)
                    v.tensor_reduce(RS[:, q, :], prview(l, ph * H + hf), AX.X, ALU.add).then_inc(sum_ready, 1)

                def invert(t, ph, hf):
                    u, q = t * H + hf, (ph * H + hf) % 2
                    dve.wait_ge(sum_ready, u0 + u + 1)
                    wait(dve, prob_ready, u0 + u - 1)
                    v.reciprocal(RI[:, q, :], RS[:, q, :]).then_inc(inv_ready, 1)

                def begin_update(t, par):
                    dve.wait_ge(out_ready, t0 + t + 1)
                    o = PS[:, 6 + par, 0:D]
                    if l != 2:
                        v.tensor_tensor(X[:, t, :], X[:, t, :], o, ALU.add).then_inc(upd_done, 1)
                    else:
                        v.bn_stats(O6[:, par, :], o)
                        dve.drain()
                        v.bn_aggr(O2[:, par, :], O6[:, par, :]).then_inc(o_chain, 1)
                        dve.wait_ge(o_chain, 2 * t + 1)
                        v.tensor_scalar(OE[:, par, :], O2[:, par, 1:2], LN_EPS, None, ALU.add).then_inc(o_eps, 1)
                        v.scalar_tensor_tensor(out=OT[:, par, :], in0=o, scalar=O2[:, par, 0:1], in1=g_out,
                                               op0=ALU.subtract, op1=ALU.mult).then_inc(o_chain, 1)

                def end_update(t, par):
                    if l == 2:
                        dve.wait_ge(o_rstd, t + 1)
                        dve.wait_ge(o_chain, 2 * t + 2)
                        v.scalar_tensor_tensor(out=X[:, t, :], in0=OT[:, par, :], scalar=OR[:, par, 0:1], in1=X[:, t, :],
                                               op0=ALU.mult, op1=ALU.add).then_inc(upd_done, 1)
                    dve.wait_ge(upd_done, t0 + t + 1)
                    stats(t)

                lag = LAG[l]

                def body(t, ph):
                    first = isinstance(t, int) and t == 0
                    done = t - lag - 1
                    updating = not (isinstance(t, int) and done < 0)
                    for hf in range(H):
                        before_ = (t, ph, hf - 1) if hf else (t - 1, before_by(l, ph, 1), H - 1)
                        largest(t, ph, hf)
                        if hf or not first:
                            total(*before_)
                        shift(t, ph, hf)
                        if hf or not first:
                            invert(*before_)
                        if hf == 0 and updating:
                            begin_update(done, before_by(l, ph, lag + 1) % 2)
                        if hf == H - 1 and updating:
                            end_update(done, before_by(l, ph, lag + 1) % 2)
                in_groups(dve, l, body)
                total(T - 1, GROUP[l] - 1, H - 1)
                invert(T - 1, GROUP[l] - 1, H - 1)
                variances(2 * l + 1, 0)
                for t in range(T - lag - 1, T):
                    begin_update(t, t % 2)
                    end_update(t, t % 2)
                    if t == T - lag - 1:
                        front(l, 0)

            def wide(a):
                return a.unsqueeze(2).to_broadcast([P, T, E])

            def top2(src):
                for k, (val, oh) in enumerate(((13, 1), (14, 2))):
                    link(v.tensor_reduce(SM[:, val, :], src, AX.X, ALU.max))
                    link(tt(RT[:, 3, :, :], src, wide(SM[:, val, :]), ALU.is_equal))
                    link(v.scalar_tensor_tensor(out=RT[:, 3, :, :], in0=RT[:, 3, :, :], scalar=-16.0, in1=iota, op0=ALU.mult, op1=ALU.add))
                    link(v.tensor_reduce(SM[:, 15, :], RT[:, 3, :, :], AX.X, ALU.min))
                    link(tt(RT[:, oh, :, :], RT[:, 3, :, :], wide(SM[:, 15, :]), ALU.is_equal))
                    if k == 0:
                        link(v.scalar_tensor_tensor(out=RT[:, 4, :, :], in0=RT[:, 1, :, :], scalar=-3e38, in1=src, op0=ALU.mult, op1=ALU.add))
                        src = RT[:, 4, :, :]

            def places():
                v.tensor_tensor(RT[:, 5, :, :], RT[:, 1, :, :], RT[:, 2, :, :], ALU.add).then_inc(r_count, 1)
                link(v.memset(RC[:, :, 0:8, :], 0.0))
                dve.wait_ge(r_sums, counts[0] + 1)
                counts[0] += 1
                flat = PS[:, 1, 0:T * E].rearrange("p (t e) -> p t e", e=E)
                link(v.tensor_copy(RC[:, 0, 8:24, :], flat))
                a = 0
                for step in (1, 2, 4, 8):
                    link(tt(RC[:, 1 - a, 8:24, :], RC[:, a, 8:24, :], RC[:, a, 8 - step:24 - step, :], ALU.add))
                    a = 1 - a
                link(tt(RT[:, 7, :, :], PS[:, 0, 0:T * E].rearrange("p (t e) -> p t e", e=E), RC[:, a, 7:23, :], ALU.add))

            def slot_rows(l):
                cap = float(CAP[l])
                link(ts(RT[:, 8, :, :], RT[:, 7, :, :], cap, None, ALU.is_lt))
                link(v.scalar_tensor_tensor(out=RT[:, 9, :, :], in0=iota, scalar=cap, in1=RT[:, 7, :, :], op0=ALU.mult, op1=ALU.add))
                for k in range(2):
                    link(tt(RT[:, 3, :, :], RT[:, 1 + k, :, :], RT[:, 8, :, :], ALU.mult))
                    link(v.tensor_reduce(RK[:, 0, k, :], RT[:, 3, :, :], AX.X, ALU.add))
                    link(tt(RT[:, 3, :, :], RT[:, 3, :, :], RT[:, 9, :, :], ALU.mult))
                    link(v.tensor_reduce(RK[:, 1, k, :], RT[:, 3, :, :], AX.X, ALU.add))
                link(ts(RK[:, 2, :, :], RK[:, 0, :, :], -1.0, 1.0, ALU.mult, ALU.add))
                link(v.scalar_tensor_tensor(out=RK[:, 2, :, :], in0=spare, scalar=float(E * CAP[l]), in1=RK[:, 2, :, :],
                                            op0=ALU.add, op1=ALU.mult))
                link(tt(RK[:, 2, :, :], RK[:, 2, :, :], RK[:, 1, :, :], ALU.add))
                v.tensor_copy(IX[:, :], RK[:, 2, :, :].rearrange("p k t -> p (k t)")).then_inc(r_idx, 1)

            counts = [0]

            def router(l):
                z = PS[:, 3, 0:T * E].rearrange("p (t e) -> p t e", e=E)
                dve.wait_ge(f_gate, B * (l + 1))
                dve.wait_ge(fw_in[l], 16)
                if l == 0:
                    dve.wait_ge(r_exp, 1)
                    link(ts(RT[:, 0, :, :], RT[:, 0, :, :], 1.0, None, ALU.add))
                    link(v.memset(S9[:, :, E:EB], 1.0))
                    link(v.memset(W9[:, :, E:EB], 1.0))
                    link(v.reciprocal(S9[:, :, 0:E], RT[:, 0, :, :]))
                    link(tt(RT[:, 6, :, :], S9[:, :, 0:E], FA[:, F0["bias"]:F0["bias"] + T * E].rearrange("p (t e) -> p t e", e=E), ALU.add))
                    top2(RT[:, 6, :, :])
                    link(tt(RT[:, 1, :, :], RT[:, 1, :, :], RT[:, 2, :, :], ALU.add))
                    link(tt(RT[:, 1, :, :], RT[:, 1, :, :], S9[:, :, 0:E], ALU.mult))
                    v.tensor_tensor(W9[:, :, 0:E], RT[:, 1, :, :], S9[:, :, 0:E], ALU.mult).then_inc(r_done, 1)
                if l == 1:
                    dve.wait_ge(first_ready, 2)
                    link(tt(SM[:, 11, :], SM[:, 8, :], SM[:, 10, :], ALU.mult))
                    link(tt(SM[:, 11, :], SM[:, 11, :], SM[:, 6, :], ALU.mult))
                    link(tt(RT[:, 0, :, :], z, wide(SM[:, 11, :]), ALU.mult))
                    link(v.tensor_reduce(SM[:, 1, :], RT[:, 0, :, :], AX.X, ALU.max))
                    v.tensor_tensor(RT[:, 0, :, :], RT[:, 0, :, :], wide(SM[:, 1, :]), ALU.subtract).then_inc(r_logit, 1)
                    dve.wait_ge(r_exp, 2)
                    link(v.tensor_reduce(SM[:, 1, :], RT[:, 0, :, :], AX.X, ALU.add))
                    link(v.reciprocal(SM[:, 2, :], SM[:, 1, :]))
                    link(tt(RT[:, 6, :, :], RT[:, 0, :, :], wide(SM[:, 2, :]), ALU.mult))
                    top2(RT[:, 6, :, :])
                    places()
                    slot_rows(1)
                    link(tt(SM[:, 4, :], RK[:, 0, 0, :], RK[:, 0, 1, :], ALU.mult))
                    link(tt(RK[:, 3, 0, :], SM[:, 13, :], SM[:, 4, :], ALU.mult))
                    link(tt(RK[:, 3, 1, :], SM[:, 14, :], SM[:, 4, :], ALU.mult))
                    link(ts(W9[:, :, E], SM[:, 4, :], -1.0, 1.0, ALU.mult, ALU.add))
                    link(tt(SM[:, 5, :], RK[:, 3, 0, :], RK[:, 3, 1, :], ALU.add))
                    link(ts(SM[:, 5, :], SM[:, 5, :], 1.0, None, ALU.add))
                    link(tt(SM[:, 5, :], SM[:, 5, :], SM[:, 8, :], ALU.mult))
                    link(tt(SM[:, 1, :], SM[:, 0, :], SM[:, 5, :], ALU.mult))
                    link(ts(SM[:, 2, :], SM[:, 5, :], 1.0, None, ALU.add))
                    v.tensor_copy(SM[:, 3, :], SM[:, 1, :]).then_inc(r_done, 1)
                if l == 2:
                    v.tensor_tensor(RT[:, 0, :, :], z, FA[:, F2["bias"]:F2["bias"] + T * E].rearrange("p (t e) -> p t e", e=E), ALU.add).then_inc(r_logit, 1)
                    dve.wait_ge(r_exp, 3)
                    link(ts(RT[:, 0, :, :], RT[:, 0, :, :], 1.0, None, ALU.add))
                    link(v.reciprocal(RT[:, 7, :, :], RT[:, 0, :, :]))
                    top2(RT[:, 7, :, :])
                    link(tt(SM[:, 1, :], SM[:, 13, :], SM[:, 14, :], ALU.add))
                    link(ts(SM[:, 1, :], SM[:, 1, :], 1e-8, None, ALU.add))
                    link(v.reciprocal(SM[:, 2, :], SM[:, 1, :]))
                    link(tt(RT[:, 6, :, :], RT[:, 1, :, :], RT[:, 2, :, :], ALU.add))
                    link(tt(RT[:, 5, :, :], RT[:, 7, :, :], wide(SM[:, 2, :]), ALU.mult))
                    v.tensor_tensor(RT[:, 5, :, :], RT[:, 5, :, :], RT[:, 6, :, :], ALU.mult).then_inc(r_count, 1)
                    dve.wait_ge(r_sums, counts[0] + 1)
                    counts[0] += 1
                    sums = PS[:, 0, 0:2 * T * E].rearrange("p (a t e) -> p a e t", a=2, e=E)
                    for a in range(2):
                        link(v.tensor_reduce(W2[:, a, :], sums[:, a, :, :], AX.X, ALU.add))
                    link(ts(W2[:, 1, :], W2[:, 1, :], 1.0, None, ALU.max))
                    link(v.reciprocal(W2[:, 2, :], W2[:, 1, :]))
                    link(tt(W2[:, 3, :], W2[:, 0, :], W2[:, 2, :], ALU.mult))
                    link(v.memset(W9[:, :, E:EB], 1.0))
                    v.tensor_tensor(W9[:, :, 0:E], RT[:, 6, :, :], W2[:, 3, :].unsqueeze(1).to_broadcast([P, T, E]), ALU.mult).then_inc(r_done, 1)
                if l == 3:
                    link(ts(RT[:, 0, :, :], z, CLAMP, -CLAMP, ALU.min, ALU.max))
                    top2(RT[:, 0, :, :])
                    v.tensor_tensor(SM[:, 12, :], SM[:, 14, :], SM[:, 13, :], ALU.subtract).then_inc(r_logit, 1)
                    dve.wait_ge(r_exp, 4)
                    link(ts(SM[:, 1, :], SM[:, 12, :], 1.0, 1e-12, ALU.add, ALU.add))
                    link(v.reciprocal(SM[:, 2, :], SM[:, 1, :]))
                    link(tt(SM[:, 3, :], SM[:, 12, :], SM[:, 2, :], ALU.mult))
                    places()
                    slot_rows(3)
                    link(tt(RK[:, 3, 0, :], SM[:, 2, :], RK[:, 0, 0, :], ALU.mult))
                    v.tensor_tensor(RK[:, 3, 1, :], SM[:, 3, :], RK[:, 0, 1, :], ALU.mult).then_inc(r_done, 1)

            def residual():
                dve.wait_ge(r_done, 2)
                for t in range(T):
                    v.tensor_scalar(X[:, t, :], X[:, t, :], SM[:, 2, t:t + 1], SM[:, 1, t:t + 1],
                                    ALU.mult, ALU.subtract).then_inc(xres_done, 1)
                dve.wait_ge(xres_done, T)

            def experts0():
                dve.wait_ge(r_done, 1)

                def gated(t, par, g):
                    n = t * 3 + g
                    q = (par * 3 + g) % 2
                    dve.wait_ge(t_act, n + 1)
                    wait(dve, t_tr, n - 1)
                    for k in range(3):
                        e = g * 3 + k
                        op = v.scalar_tensor_tensor(out=HS[:, q, k * P:(k + 1) * P], in0=PS[:, 2 * q + 1, k * P:(k + 1) * P],
                                                    scalar=W9[:, t, e:e + 1], in1=GS[:, q, k * P:(k + 1) * P], op0=ALU.mult, op1=ALU.mult)
                    op.then_inc(t_mul, 1)

                def update(t, par):
                    dve.wait_ge(t_out, t + 1)
                    v.tensor_tensor(X[:, t, :], X[:, t, :], PS[:, 6 + par, 0:D], ALU.add).then_inc(t_upd, 1)
                    dve.wait_ge(t_upd, t + 1)
                    stats(t)

                def body(t, par):
                    for g in range(3):
                        if g == 2 and not (isinstance(t, int) and t == 0):
                            update(t - 1, 1 - par)
                        gated(t, par, g)
                in_pairs(dve, body)
                update(T - 1, 1)

            def weigh(b, e, bank_, count):
                dve.wait_ge(e_down, count)
                wait(dve, e_acc, count - 1)
                for j in range(TPB):
                    t = b * TPB + j
                    op = v.scalar_tensor_tensor(out=X[:, t, :], in0=PS[:, bank_, j * P:(j + 1) * P],
                                                scalar=W9[:, t, e:e + 1], in1=X[:, t, :], op0=ALU.mult, op1=ALU.add)
                op.then_inc(e_acc, 1)

            def fallback():
                for b in range(B):
                    dve.wait_ge(e_act, b + 1)
                    v.tensor_tensor(HS[:, b % 2, :], PS[:, 2 + b % 2, :], GS[:, b % 2, :], ALU.mult).then_inc(e_mul, 1)
                    if b:
                        weigh(b - 1, E, 4 + (b - 1) % 2, b)
                weigh(B - 1, E, 4 + (B - 1) % 2, B)
                dve.wait_ge(e_acc, B)

            def experts2():
                plan, n0, q0 = PLAN2, UP2, DOWN2
                N = len(plan)
                dve.wait_ge(r_done, 3)

                def gated(b0, m):
                    dve.wait_ge(e_act, n0 + b0 * N + m + 1)
                    v.tensor_tensor(HS[:, m % 2, :], PS[:, 2 + m % 2, :], GS[:, m % 2, :], ALU.mult).then_inc(e_mul, 1)

                def outputs(b0, m):
                    b = b0 + m // N
                    for e, lo, hi in plan[m % N][1]:
                        i = m // N * EB + e
                        weigh(b, e, 4 + i % 2, q0 + b0 * EB + i + 1)
                    if m % N == N - 1:
                        dve.wait_ge(e_acc, q0 + b0 * EB + i + 1)
                        for j in range(TPB):
                            stats(b * TPB + j)

                with dve.Fori(0, B // 2) as r:
                    for m in range(2 * N):
                        gated(2 * r, m)
                        if m:
                            outputs(2 * r, m - 1)
                    outputs(2 * r, 2 * N - 1)

            def sparse_experts(l):
                N, steps, n0 = STEPS[l], steps_of(l), SLOT0[l]

                r = ROUND[l]

                def numbers(e, k):
                    dve.wait_ge(xs_in[k], 16 * (E // 2 * r + (e - k) // 2 + 1) if isinstance(e, int) else 8 * (e - k) + 16 * (E // 2 * r + 1))
                    wait(dve, y_out[k], outputs_written(l, k, e - 2))
                    n = SLOT_TILES[l]
                    v.tensor_copy(ID[:, k, 0:n], XS[:, k, 0:n, D]).then_inc(ids_ready, 1)

                def split(e, k):
                    dve.wait_ge(xts_ready, E * r + e + 1)
                    v.tensor_copy(XH3[:, k, :], XTS[:, k, :]).then_inc(x3_hi, 1)
                    dve.wait_ge(x3_hi, e + 1)
                    v.tensor_tensor(XL3[:, k, :], XTS[:, k, :], XH3[:, k, :], ALU.subtract).then_inc(x3_split, 1)

                def pair(e0):
                    more = not (isinstance(e0, int) and e0 == E - 2)
                    for k in range(2):
                        for n in range(N):
                            cols, q = steps[n][1] * P, (k * N + n) % 2
                            dve.wait_ge(e_act, n0 + (e0 + k) * N + n + 1)
                            v.tensor_tensor(HS[:, q, 0:cols], PS[:, 2 + q, 0:cols], GS[:, q, 0:cols], ALU.mult).then_inc(e_mul, 1)
                            if n == 0:
                                numbers(e0 + k, k)
                            if l == 3 and n == turn_at(l) and (k == 0 or more):
                                split(e0 + k + 1, 1 - k)
                if l == 3:
                    split(0, 0)
                in_expert_pairs(dve, pair)
                a0 = 2 * T * r
                for b in range(B):
                    dve.wait_ge(y_back[b], 16 * 2 * (r + 1))
                    for k in range(2):
                        for t in range(b * TPB, (b + 1) * TPB):
                            v.scalar_tensor_tensor(out=X[:, t, :], in0=RW[:, k, t, 0:D], scalar=RK[:, 3, k, t:t + 1],
                                                   in1=X[:, t, :], op0=ALU.mult, op1=ALU.add).then_inc(x_acc, 1)
                        dve.wait_ge(x_acc, a0 + (2 * b + k + 1) * TPB)
                    if l == 1:
                        for t in range(b * TPB, (b + 1) * TPB):
                            stats(t)

            dve.wait_ge(const_in, 80)
            v.memset(ONEB[:, :], 1.0)
            link(ts(MKF[:, :], MK[:, :], -NEG, NEG, ALU.mult, ALU.add))
            for h in range(8):
                op = v.tensor_copy(MB[:, :, h, :], MKF[:, :].rearrange("p (b k) -> p b k", k=KMAX))
            op.then_inc(mask_made, 1)
            dve.wait_ge(x_in, 16)
            with dve.Fori(0, T) as t:
                stats(t)
            for l in range(4):
                deviations(l)
                attention(l)
                variances(2 * l + 1, 1)
                front(l, 1)
                router(l)
                if l == 1:
                    residual()
                if l == 0:
                    experts0()
                if l == 1:
                    fallback()
                if l == 2:
                    experts2()
                if l in (1, 3):
                    sparse_experts(l)


def kernel(**inputs):
    import concourse.bacc as bacc
    from concourse.bass_utils import run_bass_kernel_spmd

    a = {k: np.asarray(v) for k, v in inputs.items()}

    def cols(w):
        o = np.zeros((P, w.shape[1]), w.dtype)
        o[:w.shape[0]] = w
        return o

    def chunks(w):
        return w.reshape(-1, P, w.shape[1]).transpose(1, 0, 2).reshape(P, -1)

    def everywhere(r):
        return np.broadcast_to(r.reshape(1, -1), (P, r.size))

    def attention_weights(wq, wk, wv, wo):
        return np.concatenate([cols(wk), cols(wv), chunks(wq.T), chunks(wo)], 1)

    l2k, l2v = np.split(a["L2_xattn_Wkv"], 2, axis=1)
    aw = [
        attention_weights(a["L0_xattn_Wq"], a["L0_xattn_Wk"], a["L0_xattn_Wv"], a["L0_xattn_Wo"]),
        attention_weights(a["L1_xattn_Wq"], a["L1_xattn_Wk"], a["L1_xattn_Wv"], a["L1_xattn_Wo"]),
        attention_weights(a["L2_xattn_Wq"], l2k, l2v, a["L2_xattn_Wout"]),
        np.concatenate([cols(a["L3_xattn_wk"].T), cols(a["L3_xattn_wv"].T), a["L3_xattn_wq"].T, a["L3_xattn_wo"].T], 1),
    ]

    w1 = np.concatenate([a["L0_ffn_w1"], a["L0_ffn_sw1"][None]]).transpose(2, 0, 1)
    w3 = np.concatenate([a["L0_ffn_w3"], a["L0_ffn_sw3"][None]]).transpose(2, 0, 1)
    w2 = np.concatenate([a["L0_ffn_w2"], a["L0_ffn_sw2"][None]]).transpose(2, 0, 1)
    up = np.stack([w1.reshape(P, 3, 384), w3.reshape(P, 3, 384)], 2).reshape(P, -1)
    fw0 = [a["L0_ffn_gate_w"].T, everywhere(np.tile(a["L0_ffn_expert_bias"], T)), up, w2.reshape(P, -1)]

    def padded(w):
        return np.concatenate([w, np.zeros((P, P - w.shape[1]), w.dtype)], 1)

    fw1 = [a["L1_ffn_Wr"], a["L1_ffn_norm_w"].T, a["L1_ffn_f_norm"][:, None],
           padded(a["L1_ffn_fWg"]), padded(a["L1_ffn_fWu"]), cols(a["L1_ffn_fWd"])]
    fw2 = [a["L2_ffn_gate_w"].T, everywhere(np.tile(a["L2_ffn_lb_bias"], T)),
           a["L2_ffn_expert_gate_w"].transpose(2, 0, 1).reshape(P, -1), a["L2_ffn_shared_gate_w"].T,
           a["L2_ffn_expert_up_w"].transpose(2, 0, 1).reshape(P, -1), a["L2_ffn_shared_up_w"].T,
           chunks(a["L2_ffn_expert_down_w"].transpose(0, 2, 1).reshape(-1, D)), a["L2_ffn_shared_down_w"].T]
    fw3 = [a["L3_ffn_router_w"].T, a["L3_ffn_ln_gamma"][:, None], a["L3_ffn_ln_beta"][:, None]]
    fw = [np.concatenate(f, 1) for f in (fw0, fw1, fw2, fw3)]

    def expert_weights(gate_up, down):
        d = down.reshape(E, -1, P, D).transpose(0, 2, 1, 3).reshape(E, P, -1)
        return np.concatenate([gate_up, d], 2).reshape(E * P, -1)

    ew = {1: expert_weights(np.concatenate([a["L1_ffn_Wg"], a["L1_ffn_Wu"]], 2), a["L1_ffn_Wd"]),
          3: expert_weights(a["L3_ffn_w12"].transpose(0, 2, 1), a["L3_ffn_w3"].transpose(0, 2, 1))}

    i = np.arange(P)
    f = np.float32
    null = a["L2_xattn_null_kv"]
    consts = np.concatenate([
        np.eye(P, dtype=f), np.ones((P, P), f), (i[:, None] < i[None, :]).astype(f),
        np.broadcast_to(np.tile(np.arange(E, dtype=f), T), (P, P)),
        (i[:, None] // 8 == np.arange(16)[None, :]).astype(f), everywhere(a["L2_xattn_g_out"]),
        a["L2_xattn_g_norm"][:, None], np.concatenate([null[0], null[0]])[:, None], np.concatenate([null[1], null[1]])[:, None],
        a["L3_xattn_bq"][:, None], a["L3_xattn_bk"][:, None], a["L3_xattn_bv"][:, None],
        (i[:, None] + P * np.arange(2 * T)[None, :]).astype(f)], 1)
    rows = np.concatenate([a["L0_xattn_bo"], a["L1_xattn_bo"], a["L3_xattn_bo"], (i < NK).astype(f)])[None]
    m = a["mask_BxS2_bf1"]
    mask = np.concatenate([np.ones((B, 1), m.dtype), m], 1).reshape(1, -1).view(np.uint8)

    data = {"x": a["x"].reshape(NTOK, D), "ctxT": a["ctx_768"].reshape(B * NK, CD).T, "mask": mask,
            "consts": consts, "rows": rows}
    data.update({f"aw{l}": w for l, w in enumerate(aw)})
    data.update({f"fw{l}": w for l, w in enumerate(fw)})
    data.update({f"ew{l}": w for l, w in ew.items()})

    nc = bacc.Bacc("TRN2", target_bir_lowering=False, num_devices=1)
    arrays, aps = {}, {}
    for name, v in data.items():
        v = np.ascontiguousarray(v)
        arrays[f"in_{name}"] = v
        aps[name] = nc.dram_tensor(f"in_{name}", v.shape, mybir.dt.from_np(v.dtype), kind="ExternalInput").ap()
    out = nc.dram_tensor("out", (NTOK, D), F32, kind="ExternalOutput").ap()
    slots = {l: nc.dram_tensor(f"slots{l}", (E * CAP[l], ROW), F32).ap() for l in (1, 3)}
    made = {l: nc.dram_tensor(f"made{l}", (2 * NTOK, D), F32).ap() for l in (1, 3)}
    fused_decoder_kernel(nc, aps["x"], aps["ctxT"], aps["mask"], aps["consts"], aps["rows"],
                         [aps[f"aw{l}"] for l in range(4)], [aps[f"fw{l}"] for l in range(4)], {l: aps[f"ew{l}"] for l in ew}, slots, made, out)
    r = run_bass_kernel_spmd(nc, [arrays], core_ids=[0])
    return r.results[0]["out"].reshape(B, S, D)
```
